# Optimizing a Trainium2 kernel written in Bass

```python
import numpy as np
import jax
import jax.numpy as jnp

def _softmax(x, axis=-1):
    return jax.nn.softmax(x, axis=axis)

def _gelu(x):
    return jax.nn.gelu(x, approximate=True)

def _silu(x):
    return jax.nn.silu(x)

def _sigmoid(x):
    return jax.nn.sigmoid(x)

def _layernorm(x, axis=-1, eps=1e-05):
    m = jnp.mean(x, axis=axis, keepdims=True)
    v = jnp.var(x, axis=axis, keepdims=True)
    return (x - m) / jnp.sqrt(v + eps)

def _scatter_add(tgt, idx, src, axis=0):
    return tgt.at[idx].add(src)

def _segment_sum(src, seg, n):
    return jax.ops.segment_sum(src, seg, n)
kernel_name = 'mk_seq_postln_d2_jaxref_r8_0f54eb'

def setup_inputs(seed: int=0):
    np.random.seed(seed)
    _w = jnp.asarray

    def _L0_attn_setup():
        import jax, jax.numpy as jnp
        import numpy as np
        B, L = (2, 128)
        D_MODEL, D_CKV, D_CQ = (128, 32, 64)
        N_HEAD, D_HEAD, D_ROPE = (8, 64, 32)
        N_IDX_HEAD = 4
        K_TS, LW = (96, 64)
        ROPE_BASE = 10000.0

        def _pope(x, angles):
            cos, sin = (jnp.cos(angles), jnp.sin(angles))
            mu1, mu2 = jnp.split(jax.nn.softplus(x), 2, axis=-1)
            return jnp.concatenate([mu1 * cos - mu2 * sin, mu1 * sin + mu2 * cos], axis=-1)

        def _forward(x, W_dkv, W_uk, W_uv, W_dq, W_uq, W_qr, W_kr, W_out, idx_wq, idx_wk, idx_w, raw_delta):
            B_, L_, _ = x.shape
            c_kv = x @ W_dkv
            q_i = (x @ idx_wq).reshape(B_, L_, N_IDX_HEAD, D_HEAD)
            k_i = x @ idx_wk
            s_i = jax.nn.relu(jnp.einsum('bthd,bsd->bths', q_i, k_i))
            I = jnp.einsum('bths,h->bts', s_i, idx_w)
            qpos = jnp.arange(L_)[:, None]
            kpos = jnp.arange(L_)[None, :]
            local = (kpos >= qpos - LW + 1) & (kpos <= qpos)
            causal = kpos > qpos
            I = jnp.where(local[None], jnp.inf, I)
            I = jnp.where(causal[None], -jnp.inf, I)
            kk = min(K_TS, L_)
            _, idx = jax.lax.top_k(I, kk)
            bi = jnp.arange(B_)[:, None, None]
            key_c = (c_kv @ W_uk)[bi, idx].reshape(B_, L_, kk, N_HEAD, D_HEAD)
            value = (c_kv @ W_uv)[bi, idx].reshape(B_, L_, kk, N_HEAD, D_HEAD)
            c_q = x @ W_dq
            query_c = (c_q @ W_uq).reshape(B_, L_, N_HEAD, D_HEAD)
            half = D_ROPE // 2
            theta = 1.0 / ROPE_BASE ** (2.0 * jnp.arange(half, dtype=jnp.float32) / D_ROPE)
            delta = -2.0 * jnp.pi * jax.nn.sigmoid(raw_delta)
            angles_q = jnp.arange(L_, dtype=jnp.float32)[:, None] * theta[None, :] + delta
            query_r = _pope((c_q @ W_qr).reshape(B_, L_, N_HEAD, D_ROPE), angles_q[None, :, None, :])
            kr_sel = (x @ W_kr)[bi, idx]
            angles_k = jnp.arange(kk, dtype=jnp.float32)[:, None] * theta[None, :] + delta
            key_r = _pope(kr_sel, angles_k[None, None, :, :])
            scale = (D_HEAD + D_ROPE) ** (-0.5)
            q_c = query_c.transpose(0, 2, 1, 3)
            q_r = query_r.transpose(0, 2, 1, 3)
            k_c = key_c.transpose(0, 3, 1, 2, 4)
            v = value.transpose(0, 3, 1, 2, 4)
            scores = (jnp.einsum('bhld,bhlkd->bhlk', q_c, k_c) + jnp.einsum('bhld,blkd->bhlk', q_r, key_r)) * scale
            attn = jax.nn.softmax(scores.astype(jnp.float32), axis=-1).astype(v.dtype)
            out = jnp.einsum('bhlk,bhlkd->bhld', attn, v)
            out = out.transpose(0, 2, 1, 3).reshape(B_, L_, N_HEAD * D_HEAD)
            return out @ W_out
        key = jax.random.key(seed)
        ks = jax.random.split(key, 14)

        def w(k, shape, fan_in):
            return jax.random.normal(k, shape, dtype=jnp.float32) * fan_in ** (-0.5)
        return {'x': jax.random.normal(ks[0], (B, L, D_MODEL), dtype=jnp.float32), 'W_dkv': w(ks[1], (D_MODEL, D_CKV), D_MODEL), 'W_uk': w(ks[2], (D_CKV, N_HEAD * D_HEAD), D_CKV), 'W_uv': w(ks[3], (D_CKV, N_HEAD * D_HEAD), D_CKV), 'W_dq': w(ks[4], (D_MODEL, D_CQ), D_MODEL), 'W_uq': w(ks[5], (D_CQ, N_HEAD * D_HEAD), D_CQ), 'W_qr': w(ks[6], (D_CQ, N_HEAD * D_ROPE), D_CQ), 'W_kr': w(ks[7], (D_MODEL, D_ROPE), D_MODEL), 'W_out': w(ks[8], (N_HEAD * D_HEAD, D_MODEL), N_HEAD * D_HEAD), 'idx_wq': w(ks[9], (D_MODEL, N_IDX_HEAD * D_HEAD), D_MODEL), 'idx_wk': w(ks[10], (D_MODEL, D_HEAD), D_MODEL), 'idx_w': jnp.ones((N_IDX_HEAD,), dtype=jnp.float32), 'raw_delta': jax.random.normal(ks[11], (D_ROPE // 2,), dtype=jnp.float32) * 0.1}
    _L0_attn_in = _L0_attn_setup()

    def _L0_ffn_setup():
        import math
        import jax, jax.numpy as jnp
        import numpy as np
        CAPACITY_FACTOR = 1.25
        key = jax.random.key(seed)
        ks = jax.random.split(key, 5)
        B, S, H, F, E = (4, 512, 128, 128, 32)
        scale_in = 1.0 / math.sqrt(H)
        scale_mid = 1.0 / math.sqrt(F)
        return {'x': jax.random.normal(ks[0], (B, S, H), dtype=jnp.float32), 'w_router': jax.random.normal(ks[1], (H, E), dtype=jnp.float32) * scale_in, 'w_gate': jax.random.normal(ks[2], (E, H, F), dtype=jnp.float32) * scale_in, 'w_up': jax.random.normal(ks[3], (E, H, F), dtype=jnp.float32) * scale_in, 'w_down': jax.random.normal(ks[4], (E, F, H), dtype=jnp.float32) * scale_mid}
    _L0_ffn_in = _L0_ffn_setup()

    def _L1_attn_setup():
        import jax, jax.numpy as jnp
        import numpy as np
        SHIFTS = (-32, -16, -4, -1, 1, 4, 16, 32)
        LN_EPS = 1e-05
        key = jax.random.key(seed)
        k_x, k_g, k_v, k_gm, k_bt = jax.random.split(key, 5)
        B, L, D = (4, 512, 128)
        n = len(SHIFTS) + 1
        scale = 1.0 / np.sqrt(D)
        x = jax.random.normal(k_x, (B, L, D), dtype=jnp.float32)
        gate_W = jax.random.normal(k_g, (n * D, D), dtype=jnp.float32) * scale
        value_W = jax.random.normal(k_v, (D, D), dtype=jnp.float32) * scale
        gamma = jnp.ones((D,), dtype=jnp.float32)
        beta = jnp.zeros((D,), dtype=jnp.float32)
        return {'x': x, 'gate_W': gate_W, 'value_W': value_W, 'gamma': gamma, 'beta': beta}
    _L1_attn_in = _L1_attn_setup()

    def _L1_ffn_setup():
        import jax, jax.numpy as jnp
        import numpy as np
        B, T, D = (2, 256, 128)
        E, K, H = (8, 2, 88)
        SH = 88 * 2
        EPS = 1e-20
        STD = 0.02
        key = jax.random.key(seed)
        ks = jax.random.split(key, 8)
        return {'x': jax.random.normal(ks[0], (B, T, D), jnp.float32), 'Wg': jax.random.normal(ks[1], (E, D), jnp.float32) * STD, 'W1': jax.random.normal(ks[2], (E, D, H), jnp.float32) * STD, 'W3': jax.random.normal(ks[3], (E, D, H), jnp.float32) * STD, 'W2': jax.random.normal(ks[4], (E, H, D), jnp.float32) * STD, 'Ws1': jax.random.normal(ks[5], (D, SH), jnp.float32) * STD, 'Ws3': jax.random.normal(ks[6], (D, SH), jnp.float32) * STD, 'Ws2': jax.random.normal(ks[7], (SH, D), jnp.float32) * STD}
    _L1_ffn_in = _L1_ffn_setup()
    _d = {'L0_attn_x': _L0_attn_in['x'], 'L0_attn_W_dkv': _L0_attn_in['W_dkv'], 'L0_attn_W_uk': _L0_attn_in['W_uk'], 'L0_attn_W_uv': _L0_attn_in['W_uv'], 'L0_attn_W_dq': _L0_attn_in['W_dq'], 'L0_attn_W_uq': _L0_attn_in['W_uq'], 'L0_attn_W_qr': _L0_attn_in['W_qr'], 'L0_attn_W_kr': _L0_attn_in['W_kr'], 'L0_attn_W_out': _L0_attn_in['W_out'], 'L0_attn_idx_wq': _L0_attn_in['idx_wq'], 'L0_attn_idx_wk': _L0_attn_in['idx_wk'], 'L0_attn_idx_w': _L0_attn_in['idx_w'], 'L0_attn_raw_delta': _L0_attn_in['raw_delta'], 'L0_ffn_w_router': _L0_ffn_in['w_router'], 'L0_ffn_w_gate': _L0_ffn_in['w_gate'], 'L0_ffn_w_up': _L0_ffn_in['w_up'], 'L0_ffn_w_down': _L0_ffn_in['w_down'], 'L1_attn_gate_W': _L1_attn_in['gate_W'], 'L1_attn_value_W': _L1_attn_in['value_W'], 'L1_attn_gamma': _L1_attn_in['gamma'], 'L1_attn_beta': _L1_attn_in['beta'], 'L1_ffn_Wg': _L1_ffn_in['Wg'], 'L1_ffn_W1': _L1_ffn_in['W1'], 'L1_ffn_W3': _L1_ffn_in['W3'], 'L1_ffn_W2': _L1_ffn_in['W2'], 'L1_ffn_Ws1': _L1_ffn_in['Ws1'], 'L1_ffn_Ws3': _L1_ffn_in['Ws3'], 'L1_ffn_Ws2': _L1_ffn_in['Ws2']}
    _x0 = _d['L0_attn_x']
    _d['L0_attn_x'] = jax.random.normal(jax.random.fold_in(jax.random.key(seed), 1), (1, 2048, 128), dtype=_x0.dtype)
    del _x0
    return _d

def reference(L0_attn_x, L0_attn_W_dkv, L0_attn_W_uk, L0_attn_W_uv, L0_attn_W_dq, L0_attn_W_uq, L0_attn_W_qr, L0_attn_W_kr, L0_attn_W_out, L0_attn_idx_wq, L0_attn_idx_wk, L0_attn_idx_w, L0_attn_raw_delta, L0_ffn_w_router, L0_ffn_w_gate, L0_ffn_w_up, L0_ffn_w_down, L1_attn_gate_W, L1_attn_value_W, L1_attn_gamma, L1_attn_beta, L1_ffn_Wg, L1_ffn_W1, L1_ffn_W3, L1_ffn_W2, L1_ffn_Ws1, L1_ffn_Ws3, L1_ffn_Ws2):

    def _L0_attn_ref(x, W_dkv, W_uk, W_uv, W_dq, W_uq, W_qr, W_kr, W_out, idx_wq, idx_wk, idx_w, raw_delta):
        import jax, jax.numpy as jnp
        import numpy as np
        B, L = (2, 128)
        D_MODEL, D_CKV, D_CQ = (128, 32, 64)
        N_HEAD, D_HEAD, D_ROPE = (8, 64, 32)
        N_IDX_HEAD = 4
        K_TS, LW = (96, 64)
        ROPE_BASE = 10000.0

        def _pope(x, angles):
            cos, sin = (jnp.cos(angles), jnp.sin(angles))
            mu1, mu2 = jnp.split(jax.nn.softplus(x), 2, axis=-1)
            return jnp.concatenate([mu1 * cos - mu2 * sin, mu1 * sin + mu2 * cos], axis=-1)

        def _forward(x, W_dkv, W_uk, W_uv, W_dq, W_uq, W_qr, W_kr, W_out, idx_wq, idx_wk, idx_w, raw_delta):
            B_, L_, _ = x.shape
            c_kv = x @ W_dkv
            q_i = (x @ idx_wq).reshape(B_, L_, N_IDX_HEAD, D_HEAD)
            k_i = x @ idx_wk
            s_i = jax.nn.relu(jnp.einsum('bthd,bsd->bths', q_i, k_i))
            I = jnp.einsum('bths,h->bts', s_i, idx_w)
            qpos = jnp.arange(L_)[:, None]
            kpos = jnp.arange(L_)[None, :]
            local = (kpos >= qpos - LW + 1) & (kpos <= qpos)
            causal = kpos > qpos
            I = jnp.where(local[None], jnp.inf, I)
            I = jnp.where(causal[None], -jnp.inf, I)
            kk = min(K_TS, L_)
            _, idx = jax.lax.top_k(I, kk)
            bi = jnp.arange(B_)[:, None, None]
            key_c = (c_kv @ W_uk)[bi, idx].reshape(B_, L_, kk, N_HEAD, D_HEAD)
            value = (c_kv @ W_uv)[bi, idx].reshape(B_, L_, kk, N_HEAD, D_HEAD)
            c_q = x @ W_dq
            query_c = (c_q @ W_uq).reshape(B_, L_, N_HEAD, D_HEAD)
            half = D_ROPE // 2
            theta = 1.0 / ROPE_BASE ** (2.0 * jnp.arange(half, dtype=jnp.float32) / D_ROPE)
            delta = -2.0 * jnp.pi * jax.nn.sigmoid(raw_delta)
            angles_q = jnp.arange(L_, dtype=jnp.float32)[:, None] * theta[None, :] + delta
            query_r = _pope((c_q @ W_qr).reshape(B_, L_, N_HEAD, D_ROPE), angles_q[None, :, None, :])
            kr_sel = (x @ W_kr)[bi, idx]
            angles_k = jnp.arange(kk, dtype=jnp.float32)[:, None] * theta[None, :] + delta
            key_r = _pope(kr_sel, angles_k[None, None, :, :])
            scale = (D_HEAD + D_ROPE) ** (-0.5)
            q_c = query_c.transpose(0, 2, 1, 3)
            q_r = query_r.transpose(0, 2, 1, 3)
            k_c = key_c.transpose(0, 3, 1, 2, 4)
            v = value.transpose(0, 3, 1, 2, 4)
            scores = (jnp.einsum('bhld,bhlkd->bhlk', q_c, k_c) + jnp.einsum('bhld,blkd->bhlk', q_r, key_r)) * scale
            attn = jax.nn.softmax(scores.astype(jnp.float32), axis=-1).astype(v.dtype)
            out = jnp.einsum('bhlk,bhlkd->bhld', attn, v)
            out = out.transpose(0, 2, 1, 3).reshape(B_, L_, N_HEAD * D_HEAD)
            return out @ W_out
        return _forward(x, W_dkv, W_uk, W_uv, W_dq, W_uq, W_qr, W_kr, W_out, idx_wq, idx_wk, idx_w, raw_delta)

    def _L0_ffn_ref(x, w_router, w_gate, w_up, w_down):
        import math
        import jax, jax.numpy as jnp
        import numpy as np
        CAPACITY_FACTOR = 1.25
        B, S, H = x.shape
        E = w_gate.shape[0]
        T = B * S
        C = int(math.ceil(CAPACITY_FACTOR * T / E))
        xt = x.reshape(T, H)
        logits = xt @ w_router
        probs = jax.nn.softmax(logits, axis=-1)
        top1 = jnp.argmax(probs, axis=-1)
        gate = jnp.take_along_axis(probs, top1[:, None], axis=1)[:, 0]
        onehot = jax.nn.one_hot(top1, E, dtype=jnp.int32)
        pos = jnp.cumsum(onehot, axis=0)[jnp.arange(T), top1] - 1
        accepted = pos < C
        slot = jnp.where(accepted, top1 * C + pos, E * C)
        buf = jnp.zeros((E * C + 1, H), dtype=x.dtype).at[slot].set(xt)
        buf = buf[:E * C].reshape(E, C, H)
        g = jnp.einsum('ech,ehf->ecf', buf, w_gate)
        u = jnp.einsum('ech,ehf->ecf', buf, w_up)
        y = jnp.einsum('ecf,efh->ech', jax.nn.silu(g) * u, w_down)
        out_tok = y.reshape(E * C, H)[jnp.clip(slot, 0, E * C - 1)]
        out_tok = jnp.where(accepted[:, None], out_tok * gate[:, None], 0.0)
        return (xt + out_tok).reshape(B, S, H)

    def _L1_attn_ref(x, gate_W, value_W, gamma, beta):
        import jax, jax.numpy as jnp
        import numpy as np
        SHIFTS = (-32, -16, -4, -1, 1, 4, 16, 32)
        LN_EPS = 1e-05
        B, L, D = x.shape
        n = len(SHIFTS) + 1
        v = jnp.einsum('bld,ed->ble', x, value_W)
        stacked = jnp.stack([v] + [jnp.roll(v, -s, axis=1) for s in SHIFTS], axis=2)
        gates = jax.nn.sigmoid(jnp.einsum('bld,ed->ble', x, gate_W))
        gates = gates.reshape(B, L, n, D)
        out = jnp.sum(stacked * gates, axis=2)
        mu = jnp.mean(out, axis=-1, keepdims=True)
        var = jnp.mean(jnp.square(out - mu), axis=-1, keepdims=True)
        return (out - mu) * jax.lax.rsqrt(var + LN_EPS) * gamma + beta

    def _L1_ffn_ref(x, Wg, W1, W3, W2, Ws1, Ws3, Ws2):
        import jax, jax.numpy as jnp
        import numpy as np
        B, T, D = (2, 256, 128)
        E, K, H = (8, 2, 88)
        SH = 88 * 2
        EPS = 1e-20
        STD = 0.02
        b, t, d = x.shape
        n = b * t
        xf = x.reshape(n, d)
        gates = jax.nn.softmax(xf @ Wg.T, axis=-1)
        top_v, top_i = jax.lax.top_k(gates, K)
        masked = jnp.zeros_like(gates).at[jnp.arange(n)[:, None], top_i].set(top_v)
        masked = masked / (masked.sum(-1, keepdims=True) + EPS)
        h = jnp.einsum('nd,edh->enh', xf, W1)
        g = jnp.einsum('nd,edh->enh', xf, W3)
        y = jnp.einsum('enh,ehd->end', jax.nn.silu(h) * g, W2)
        routed = jnp.einsum('ne,end->nd', masked, y)
        shared = jax.nn.silu(xf @ Ws1) * (xf @ Ws3) @ Ws2
        return (routed + shared).reshape(b, t, d)
    x = L0_attn_x
    x = _layernorm(x + _L0_attn_ref(x, L0_attn_W_dkv, L0_attn_W_uk, L0_attn_W_uv, L0_attn_W_dq, L0_attn_W_uq, L0_attn_W_qr, L0_attn_W_kr, L0_attn_W_out, L0_attn_idx_wq, L0_attn_idx_wk, L0_attn_idx_w, L0_attn_raw_delta), axis=-1)
    x = _layernorm(x + _L0_ffn_ref(x, L0_ffn_w_router, L0_ffn_w_gate, L0_ffn_w_up, L0_ffn_w_down), axis=-1)
    x = _layernorm(x + _L1_attn_ref(x, L1_attn_gate_W, L1_attn_value_W, L1_attn_gamma, L1_attn_beta), axis=-1)
    x = _layernorm(x + _L1_ffn_ref(x, L1_ffn_Wg, L1_ffn_W1, L1_ffn_W3, L1_ffn_W2, L1_ffn_Ws1, L1_ffn_Ws3, L1_ffn_Ws2), axis=-1)
    return x

_drawn_inputs = setup_inputs


def setup_inputs(seed=0):
    import zlib

    import numpy as np

    out = dict(_drawn_inputs(seed))
    spreads = {'L0_attn_idx_w': (1.0, 0.2), 'L1_attn_gamma': (1.0, 0.2), 'L1_attn_beta': (0.0, 0.1)}
    factors = {'L0_attn_raw_delta': 8.0,
     'L1_ffn_Wg': 8.0,
     'L1_ffn_W1': 8.0,
     'L1_ffn_W3': 8.0,
     'L1_ffn_W2': 8.0,
     'L1_ffn_Ws1': 8.0,
     'L1_ffn_Ws3': 8.0,
     'L1_ffn_Ws2': 8.0}
    for name, (base, spread) in spreads.items():
        noise = np.random.default_rng([zlib.crc32(name.encode()), seed]).standard_normal(out[name].shape)
        drawn = base * np.exp(spread * noise) if base else spread * noise
        out[name] = jnp.asarray(drawn.astype(out[name].dtype))
    for name, factor in factors.items():
        out[name] = (out[name] * factor).astype(out[name].dtype)
    return out
```

```python
from contextlib import ExitStack

import numpy as np

import concourse.bass as bass
from concourse import mybir

F32 = mybir.dt.float32
U32 = mybir.dt.uint32
ALU = mybir.AluOpType
ACT = mybir.ActivationFunctionType

P = 128
L = 2048
D = 128
NT = L // P
CKV, CQ = 32, 64
NH, DH, DR = 8, 64, 32
HALF = DR // 2
NIH = 4
KTS, LW = 96, 64
NSEL = KTS - LW
SCALE = (DH + DR) ** -0.5
ROPE_BASE = 10000.0
QB = 16
NB = P // QB
GPB = 4
NG = NB * GPB
WIN = QB + LW
NS = P + WIN
PAD = LW
BIG = 1.0e30
LOW = -3.0e38
E0, C0 = 32, 80
NSLOT = E0 * C0
EG = 4
NEG = E0 // EG
SHIFTS = (0, -32, -16, -4, -1, 1, 4, 16, 32)
NGATE = len(SHIFTS)
ROLL = 32
E1, H1 = 8, 88
NHC = E1 + 2
CH = 512
NCH = L // CH
TPC = CH // P
LN_EPS = 1e-5
SUM_EPS = 1e-20


def keys_of(t):
    return P if t == 0 else P * t + LW


def chunks_of(t):
    return -(-keys_of(t) // CH)


def chunk_base(t):
    return sum(chunks_of(u) for u in range(t))


C_ID = 0
C_MASK = C_ID + P
C_MASK0 = C_MASK + NS
C_IM = C_MASK0 + NS
C_IM0 = C_IM + P
C_TRI = C_IM0 + P
C_IOTA = C_TRI + P
C_RA = C_IOTA + E0
C_RB = C_RA + NSEL
C_RC = C_RB + NSEL
C_ONES = C_RC + NSEL
C_EPS = C_ONES + P
C_PI = C_EPS + 1
C_N = C_PI + 1


def shape_constants():
    c = np.zeros((P, C_N), np.float32)
    c[:, C_ID:C_ID + P] = np.eye(P)
    row = np.arange(P)
    ql = row // NH
    col = np.arange(P)
    sel = (ql[:, None] % GPB) == (col[None, :] // NSEL)
    w = np.arange(WIN)
    local = (w[None, :] >= ql[:, None] + 1) & (w[None, :] <= ql[:, None] + LW)
    first = np.broadcast_to(w[None, :] < LW, (P, WIN))
    for base, loc in ((C_MASK, local), (C_MASK0, first)):
        c[:, base:base + P] = np.where(sel, 0, BIG)
        c[:, base + P:base + NS] = np.where(loc, 0, BIG)
    qi = 4 * (row % 32) + row // 32
    c[:, C_IM:C_IM + P] = np.where(col[None, :] <= qi[:, None], 0, -BIG)
    b = np.maximum(qi - (LW - 1), 0)[:, None]
    c[:, C_IM0:C_IM0 + P] = np.where(col[None, :] < b, 0, np.where(col[None, :] < b + LW, LOW, -BIG))
    c[:, C_TRI:C_TRI + P] = row[:, None] <= row[None, :]
    c[:, C_IOTA:C_IOTA + E0] = np.arange(E0)
    theta = (np.float32(1.0) / np.float32(ROPE_BASE) ** (np.float32(2.0) * np.arange(HALF, dtype=np.float32)
                                                        / np.float32(DR))).astype(np.float32)
    rank = (np.arange(LW, KTS, dtype=np.float32)[:, None] * theta[None, :]).astype(np.float64)
    cr, sr = np.cos(rank).T, np.sin(rank).T
    for k in range(2):
        c[HALF * k:HALF * (k + 1), C_RA:C_RA + NSEL] = cr
        c[HALF * k:HALF * (k + 1), C_RB:C_RB + NSEL] = -sr
        c[DR + HALF * k:DR + HALF * (k + 1), C_RA:C_RA + NSEL] = sr
        c[DR + HALF * k:DR + HALF * (k + 1), C_RB:C_RB + NSEL] = cr
    c[3 * DR:, C_RC:C_RC + NSEL] = 1.0
    c[:, C_ONES:C_ONES + P] = 1.0
    c[:, C_EPS] = LN_EPS
    c[:, C_PI] = np.pi
    q = np.arange(L)
    tq = (q.astype(np.float32)[:, None] * theta[None, :]).astype(np.float64)
    tk = q[:, None] * theta[None, :].astype(np.float64)
    tl = tq + np.maximum(q - (LW - 1), 0)[:, None] * theta[None, :].astype(np.float64)
    tab = np.stack([np.cos(tq), np.sin(tq), np.cos(tl), np.sin(tl), np.cos(tk), np.sin(tk)], 1)
    tab = tab.reshape(NT, P, 6, HALF).transpose(1, 2, 0, 3)
    return c, np.ascontiguousarray(tab.reshape(P, 6 * NT * HALF)).astype(np.float32)


def program(nc, dram, out):
    with ExitStack() as ctx:
        def sb(name, shape, dt=F32):
            return ctx.enter_context(nc.sbuf_tensor(name, shape, dt))

        def sem(name):
            return ctx.enter_context(nc.semaphore(name))

        key_rows = nc.dram_tensor("key_rows", (L, P), F32, kind="Internal").ap()
        val_rows_h = nc.dram_tensor("val_rows", (PAD + L, CKV), F32, kind="Internal")
        val_rows = val_rows_h.ap()
        xslots = nc.dram_tensor("xslots", (NSLOT, D), F32, kind="Internal").ap()
        yslots = nc.dram_tensor("yslots", (NSLOT, D), F32, kind="Internal").ap()

        cst = sb("cst", [P, C_N])
        ident = cst[:, C_ID:C_ID + P]
        ones = cst[:, C_ONES:C_ONES + P]
        tab = sb("tab", [P, 6, NT, HALF])
        rot = sb("rot", [P, 6, NT, HALF])
        rtmp = sb("rtmp", [P, 2, NT, HALF])
        rank_tab = sb("rank_tab", [P, NSEL])
        raw = sb("raw", [P, HALF + 1])
        dlt = sb("dlt", [P, 8, HALF + 1])
        xT = sb("xT", [P, L])
        xr = sb("xr", [P, NT, D])
        w_idxq = sb("w_idxq", [P, 2 * P])
        w_idxk = sb("w_idxk", [P, P])
        w_kv = sb("w_kv", [P, DR + CKV])
        w_dq = sb("w_dq", [P, CQ])
        w_uqT = sb("w_uqT", [DH, NH, CQ])
        w_ukT = sb("w_ukT", [DH, NH, CKV])
        w_uvT = sb("w_uvT", [DH, NH, CKV])
        w_out = sb("w_out", [DH, NH, D])
        w_q = sb("w_q", [CQ, 2 * NH * DR])
        w_vo = sb("w_vo", [CKV, NH, D])
        w_i = sb("w_i", [P, NIH])
        w_router = sb("w_router", [P, E0])
        kiT = sb("kiT", [P, L])
        qiT = sb("qiT", [P, 2, L])
        cq_region = sb("cq_region", [P, L])
        cqT = cq_region[0:CQ, :]
        klocT = sb("klocT", [P, PAD + L])
        kmu = sb("kmu", [P, NT, DR])
        G = sb("G", [P, 2, NG, P])
        grow = G[:, 1, 0:NT, :]
        lrow = G[:, 1, NT:2 * NT, :]
        idxf = sb("idxf", [P, NSEL], U32)
        idx = sb("idx", [P, 2, NG], U32)
        R = sb("R", [P, 2, NIH, CH])
        SC = sb("SC", [P, 2, L])
        top = sb("top", [P, 4, 8])
        QF = sb("QF", [P, NH, P])
        qe = sb("qe", [P, NH, 2, HALF])
        qmu = sb("qmu", [P, NH, 2, HALF])
        qt = sb("qt", [P, 4, NH * 2, HALF])
        Q = sb("Q", [P, 2, P, NH])
        KT = sb("KT", [P, 2, GPB, P])
        S = sb("S", [P, 2, NS])
        PR = sb("PR", [P, 2, 2 * P])
        PT = sb("PT", [P, 2, 2 * P])
        V = sb("V", [WIN, 2, NB, CKV])
        O = sb("O", [P, 2, CKV])
        ot_region = sb("ot_region", [P, 2 * NB * QB * NH])
        OT = ot_region[0:CKV, :].rearrange("p (a b q h) -> p a b q h", a=2, b=NB, q=QB)
        nmin = sb("nmin", [P, 2])
        psumr = sb("psumr", [P, 2])
        rinv = sb("rinv", [P, 2])
        xa = sb("xa", [P, D])
        stats = sb("stats", [P, TPC, 6])
        mv = sb("mv", [P, TPC, 2])
        lnv = sb("lnv", [P, 2, TPC])
        x1 = sb("x1", [P, 2, D])
        x1T = sb("x1T", [P, P])
        r8 = sb("r8", [P, 8])
        r8i = sb("r8i", [P, 8], U32)
        rex = sb("rex", [P, E0])
        rlog = sb("rlog", [P, E0])
        rsm = sb("rsm", [P, 8])
        onehot = sb("onehot", [P, E0])
        ohsum = sb("ohsum", [P, E0])
        rjunk = sb("rjunk", [P, E0])
        gm = sb("gm", [P, NT])
        slot_in = sb("slot_in", [P, NT], U32)
        slot_out = sb("slot_out", [P, NT], U32)
        zrow = sb("zrow", [P, 5 * P])

        w_value = kiT[:, 0:D]
        w_gates = kiT[:, D:D * (1 + NGATE)]
        w_ex = qiT[:, :, :].rearrange("p a n -> p (a n)")[:, 0:2 * 3 * EG * D].rearrange(
            "p (a i e n) -> p a i e n", a=2, i=3, e=EG)
        w_up = xT[:, 0:2 * NHC * H1].rearrange("p (a e n) -> p a e n", a=2, e=NHC)
        w_down = cq_region[0:H1, 0:NHC * D].rearrange("p (e n) -> p e n", e=NHC)
        gamma = cq_region[:, NHC * D:(NHC + 1) * D]
        beta = cq_region[:, (NHC + 1) * D:(NHC + 2) * D]
        w_g8 = cq_region[:, (NHC + 2) * D:(NHC + 2) * D + E1]

        psK = ctx.enter_context(nc.psum_tensor("psK", [P, CH], F32))
        psX = ctx.enter_context(nc.psum_tensor("psX", [P, CH], F32))
        psS = ctx.enter_context(nc.psum_tensor("psS", [P, CH], F32))
        psP = ctx.enter_context(nc.psum_tensor("psP", [P, CH], F32))
        psO = ctx.enter_context(nc.psum_tensor("psO", [P, CH], F32))
        psI = [ctx.enter_context(nc.psum_tensor(f"psI{i}", [P, CH], F32)) for i in range(2)]
        psM = ctx.enter_context(nc.psum_tensor("psM", [P, CH], F32))
        PX = psX[:, 0:P]

        names = """ld_cst ld_x ld_w ld_raw ld_late zeroed z_ready zslots kv_mm
            w_mm w_cp kproj kproj_cp lat_row mu_row key_l mu lrot kr_out val_out lT lT_cp rope rope_a
            i_mm i_relu comb im topk idx_ready q_mm q_a q_e q_chain qf_a q_t q_cp
            k_t k_ev s_mm s_min p_exp p_t p_cp pv orec onorm o_t o_cp v_ld
            y_mm y_add bn ln_a x1_n x1d x1_t x1_cp lg_mm lg_e rt_a rt cum_mm lg_cp rte plc slots_ready ld_l1""".split()
        s = {n: sem("s_" + n) for n in names}
        s_we = [sem(f"s_we{i}") for i in range(2)]
        s_sct = [sem(f"s_sct{i}") for i in range(2)]
        s_g = [[sem(f"s_g{i}_{b}") for b in range(NB)] for i in range(2)]

        CHUNKS = L // CH

        N0, N1 = -3 * NB, NT * NB + NB + NB

        def load_experts(sp, k):
            for i, w in enumerate(("w_gate", "w_up", "w_down")):
                sp.dma_start(w_ex[:, k % 2, i, :, :],
                             dram[w][EG * k:EG * (k + 1)].rearrange("e h f -> h e f")).then_inc(s_we[k % 2], 16)

        def scatter(pool, t):
            pool.wait_ge(s["slots_ready"], t + 1)
            pool.indirect_dma_start(
                xslots, bass.IndirectOffsetOnAxis(ap=slot_in[:, t:t + 1], axis=0), x1[:, t % 2, :], None,
                bounds_check=NSLOT - 1, oob_is_err=False).then_inc(s_sct[t % 2], 16)

        with nc.Block() as block:
            @block.sync
            def _(sp):
                sp.dma_start(cst[:, :], dram["cst"]).then_inc(s["ld_cst"], 16)
                sp.dma_start(raw[:, :], dram["raw"]).then_inc(s["ld_raw"], 16)
                sp.dma_start(w_idxk[:, 0:DH], dram["idx_wk"]).then_inc(s["ld_w"], 16)
                sp.dma_start(w_idxk[:, DH:P], dram["idx_wk"]).then_inc(s["ld_w"], 16)
                sp.dma_start(w_idxq[:, :], dram["idx_wq"]).then_inc(s["ld_w"], 16)
                sp.dma_start(xT[:, :], dram["xT"]).then_inc(s["ld_x"], 16)
                sp.dma_start(w_kv[:, 0:DR], dram["W_kr"]).then_inc(s["ld_w"], 16)
                sp.dma_start(w_kv[:, DR:DR + CKV], dram["W_dkv"]).then_inc(s["ld_w"], 16)
                sp.dma_start(w_dq[:, :], dram["W_dq"]).then_inc(s["ld_w"], 16)
                sp.dma_start(w_i[:, :], dram["idx_w"]).then_inc(s["ld_w"], 16)
                sp.dma_start(tab[:, :, :, :], dram["tab"]).then_inc(s["ld_late"], 16)
                sp.dma_start(w_uqT[:, :, :], dram["W_uqT"]).then_inc(s["ld_late"], 16)
                sp.dma_start(w_ukT[:, :, :], dram["W_ukT"]).then_inc(s["ld_late"], 16)
                sp.dma_start(w_uvT[:, :, :], dram["W_uvT"]).then_inc(s["ld_late"], 16)
                sp.dma_start(w_out[:, :, :], dram["W_out"]).then_inc(s["ld_late"], 16)
                sp.dma_start(w_q[:, NH * CKV:], dram["W_qr"]).then_inc(s["ld_late"], 16)
                sp.dma_start(w_router[:, :], dram["w_router"]).then_inc(s["ld_late"], 16)
                sp.dma_start(xr[:, :, :], dram["x"]).then_inc(s["ld_late"], 16)
                sp.wait_ge(s["z_ready"], 1)
                sp.dma_start(val_rows[0:PAD, :], zrow[0:PAD, 0:CKV]).then_inc(s["val_out"], 16)
                for i in range(4):
                    n = NSLOT // 4
                    sp.dma_start(xslots[n * i:n * (i + 1), :].rearrange("(p r) d -> p (r d)", p=P),
                                 zrow[:, :]).then_inc(s["zslots"], 16)
                sp.wait_ge(s["mu_row"], 3)
                sp.wait_ge(s["lat_row"], 4)
                sp.dma_start(key_rows.rearrange("(t p) d -> p t d", p=P), grow).then_inc(s["kr_out"], 16)
                sp.dma_start(val_rows[PAD:, :].rearrange("(t p) d -> p t d", p=P),
                             grow[:, :, 3 * DR:]).then_inc(s["val_out"], 16)
                sp.wait_ge(s["val_out"], 32)
                for t in range(NT):
                    if t >= 2:
                        sp.wait_ge(s["pv"], NB * (t - 1))
                    if t == 0:
                        for b in range(4):
                            sp.dma_start(V[:, 0, b, :], val_rows[PAD:PAD + WIN, :]).then_inc(s["v_ld"], 16)
                        src = bass.AP(val_rows_h, 4 * QB * CKV, [[CKV, WIN], [QB * CKV, NB - 4], [1, CKV]])
                        sp.dma_start(V[:, 0, 4:, :], src).then_inc(s["v_ld"], 16)
                    else:
                        src = bass.AP(val_rows_h, P * t * CKV, [[CKV, WIN], [QB * CKV, NB], [1, CKV]])
                        sp.wait_ge(s["v_ld"], 16 * (4 + t))
                        sp.dma_start(V[:, t % 2, :, :], src).then_inc(s["v_ld"], 16)
                sp.wait_ge(s["i_relu"], 4 * chunk_base(NT))
                sp.dma_start(w_value, dram["value_W"]).then_inc(s["ld_l1"], 16)
                sp.dma_start(w_gates, dram["gate_W"]).then_inc(s["ld_l1"], 16)
                sp.dma_start(w_up[:, 0, 0:E1, :], dram["W1"]).then_inc(s["ld_l1"], 16)
                sp.dma_start(w_up[:, 1, 0:E1, :], dram["W3"]).then_inc(s["ld_l1"], 16)
                sp.dma_start(w_up[:, 0, E1:, :], dram["Ws1"]).then_inc(s["ld_l1"], 16)
                sp.dma_start(w_up[:, 1, E1:, :], dram["Ws3"]).then_inc(s["ld_l1"], 16)
                for k in range(2):
                    load_experts(sp, k)
                sp.wait_ge(s["q_mm"], NT)
                sp.dma_start(w_down[:, 0:E1, :], dram["W2"]).then_inc(s["ld_l1"], 16)
                sp.dma_start(w_down[:, E1:, :], dram["Ws2"]).then_inc(s["ld_l1"], 16)
                sp.dma_start(gamma, dram["gamma"]).then_inc(s["ld_l1"], 16)
                sp.dma_start(beta, dram["beta"]).then_inc(s["ld_l1"], 16)
                sp.dma_start(w_g8, dram["Wg"]).then_inc(s["ld_l1"], 16)
                sp.wait_ge(s["ld_l1"], 16 * 11)
                for k in range(2):
                    sp.wait_ge(s_we[k], 16 * 3)

            @block.gpsimd
            def _(pool):
                pool.memset(zrow[:, :], 0.0).then_inc(s["z_ready"], 1)
                pool.memset(ohsum[:, :], 0.0).then_inc(s["zeroed"], 1)
                pool.memset(klocT[:, 0:PAD], 0.0).then_inc(s["zeroed"], 1)
                pool.memset(PR[:, :, NS:], 0.0).then_inc(s["zeroed"], 1)
                pool.memset(lrow[:, :, 0:2 * DR], 0.0).then_inc(s["zeroed"], 1)
                pool.wait_ge(s["kr_out"], 16)
                for t in range(NT):
                    pool.wait_ge(s["idx_ready"], t + 1)
                    if t == 1:
                        pool.wait_ge(s["lT"], NT)
                        pool.wait_ge(s["val_out"], 32)
                    for g in range(NG):
                        b = g // GPB
                        if t >= 2 and g % GPB == 0:
                            pool.wait_ge(s["pv"], NB * (t - 2) + b + 1)
                        pool.indirect_dma_start(
                            G[:, t % 2, g, :], None, key_rows,
                            bass.IndirectOffsetOnAxis(ap=idx[:, t % 2, g:g + 1], axis=0),
                        ).then_inc(s_g[t % 2][b], 16)
                    if t == 3:
                        pool.wait_ge(s["zslots"], 64)
                    if t >= 3:
                        scatter(pool, t - 3)
                for t in range(NT - 3, NT):
                    scatter(pool, t)
                for i in range(2):
                    pool.wait_ge(s_sct[i], 16 * NT // 2)

            @block.tensor
            def _(pe):
                pe.wait_ge(s["ld_w"], 16 * 7)
                pe.wait_ge(s["ld_x"], 16)
                banks = [psI[0], psI[1], psK, psX]
                n = 0
                for c in range(CHUNKS):
                    for lhs, rows in ((w_idxk[:, :], P), (w_idxq[:, 0:P], P), (w_idxq[:, P:2 * P], P),
                                      (w_dq[:, :], CQ)):
                        if n >= 4:
                            pe.wait_ge(s["kproj_cp"], n - 3)
                        pe.matmul(banks[n % 4][0:rows, :], lhs, xT[:, CH * c:CH * (c + 1)],
                                  start=True, stop=True).then_inc(s["kproj"], 1)
                        n += 1
                for h in range(2):
                    for i in range(8):
                        t = 8 * h + i
                        mm = pe.matmul([psS, psM][h][:, 64 * i:64 * i + 64], xT[:, P * t:P * (t + 1)], w_kv[:, :],
                                       start=True, stop=True, skip_group_check=True)
                    mm.then_inc(s["kv_mm"], 1)
                pe.wait_ge(s["ld_late"], 16 * 8)
                for h in range(NH):
                    mm = pe.matmul(psP[0:CQ, CKV * h:CKV * (h + 1)], w_uqT[:, h, :], w_ukT[:, h, :],
                                   start=True, stop=True, skip_group_check=True)
                mm.then_inc(s["w_mm"], 1)
                for j in range(2):
                    pe.wait_ge(s["w_cp"], 1 + j)
                    for h in range(4):
                        mm = pe.matmul(psP[0:CKV, D * h:D * (h + 1)], w_uvT[:, 4 * j + h, :], w_out[:, 4 * j + h, :],
                                       start=True, stop=True, skip_group_check=True)
                    mm.then_inc(s["w_mm"], 1)

                def index_pair(t, u):
                    c, pair = u // 2, u % 2
                    w = min(CH, keys_of(t) - CH * c)
                    m = 2 * chunk_base(t) + u
                    if m == 0:
                        pe.wait_ge(s["kproj_cp"], 4 * CHUNKS)
                    else:
                        pe.wait_ge(s["i_relu"], 2 * m)
                    for i in range(2):
                        lhs = qiT[64 * i:64 * i + 64, pair, P * t:P * (t + 1)]
                        pe.matmul(psI[i][:, 0:w], lhs, kiT[64 * i:64 * i + 64, CH * c:CH * c + w],
                                  start=True, stop=True).then_inc(s["i_mm"], 1)

                def q_project(t):
                    if t == 0:
                        pe.wait_ge(s["w_cp"], 3)
                        pe.wait_ge(s["kproj_cp"], 4 * CHUNKS)
                        pe.wait_ge(s["lat_row"], 4)
                        pe.wait_ge(s["mu"], 4)
                    if t >= 1:
                        pe.wait_ge(s["q_cp"], 2 * t)
                    pe.matmul(psM[:, :], cqT[:, P * t:P * (t + 1)], w_q[:, :], start=True,
                              stop=True).then_inc(s["q_mm"], 1)

                def q_transpose(t, j):
                    if j == 0:
                        pe.wait_ge(s["q_chain"], 10 * (t + 1))
                        pe.wait_ge(s["qf_a"], 3 * (t + 1))
                    else:
                        pe.wait_ge(s["q_cp"], 2 * t + 1)
                    for h in range(4):
                        mm = pe.transpose(psM[:, P * h:P * (h + 1)], QF[:, 4 * j + h, :], ident)
                    mm.then_inc(s["q_t"], 1)

                def front(n):
                    t, b = divmod(n, NB)
                    pe.wait_ge(s_g[t % 2][b], 64 * (t // 2 + 1))
                    if n >= 1:
                        pe.wait_ge(s["k_ev"], n)
                    else:
                        pe.wait_ge(s["lT_cp"], NT // 4)
                    for j in range(GPB):
                        mm = pe.transpose(psK[:, P * j:P * (j + 1)], G[:, t % 2, GPB * b + j, :], ident)
                    mm.then_inc(s["k_t"], 1)

                def scores(n):
                    t, b = divmod(n, NB)
                    pe.wait_ge(s["k_ev"], n + 1)
                    pe.wait_ge(s["q_cp"], 2 * t + 2)
                    if n >= 1:
                        pe.wait_ge(s["s_min"], n)
                    qb = Q[:, t % 2, QB * b:QB * (b + 1), :].rearrange("p q h -> p (q h)")
                    for j in range(GPB):
                        pe.matmul(psS[32 * j:32 * j + 32, 0:P], qb[:, 32 * j:32 * j + 32], KT[:, n % 2, j, :],
                                  start=True, stop=True, skip_group_check=True)
                    w0 = PAD if t == 0 and b < 4 else P * t + QB * b
                    pe.matmul(psS[:, P:NS], qb, klocT[:, w0:w0 + WIN],
                              start=True, stop=True, skip_group_check=True).then_inc(s["s_mm"], 1)

                def p_transpose(n):
                    pe.wait_ge(s["p_exp"], n + 1)
                    if n >= 1:
                        pe.wait_ge(s["p_cp"], n)
                    for i in range(2):
                        mm = pe.transpose(psP[:, P * i:P * (i + 1)], PR[:, n % 2, P * i:P * (i + 1)], ident)
                    mm.then_inc(s["p_t"], 1)

                def weighted(n):
                    t, b = divmod(n, NB)
                    pe.wait_ge(s["p_cp"], n + 1)
                    pe.wait_ge(s["v_ld"], 16 * (5 + t))
                    if n >= 1:
                        pe.wait_ge(s["o_cp"], n)
                    o = psO[:, 0:CKV]
                    pe.matmul(o, PT[0:WIN, n % 2, P:2 * P], V[:, t % 2, b, :], start=True, stop=False,
                              skip_group_check=True)
                    for j in range(GPB):
                        mm = pe.matmul(o[32 * j:32 * j + 32, :], PT[:, n % 2, 32 * j:32 * j + 32],
                                       G[:, t % 2, GPB * b + j, 3 * DR:], start=False, stop=True,
                                       skip_group_check=True)
                    mm.then_inc(s["pv"], 1)

                def o_transpose(n):
                    pe.wait_ge(s["onorm"], n + 1)
                    pe.transpose(psO[0:CKV, P:2 * P], O[:, n % 2, :], ident).then_inc(s["o_t"], 1)

                def out_project(t):
                    pe.wait_ge(s["o_cp"], NB * (t + 1))
                    if t >= 1:
                        pe.wait_ge(s["rte"], t)
                    for h in range(NH):
                        mm = pe.matmul(PX, OT[:, t % 2, :, :, h].rearrange("p b q -> p (b q)"), w_vo[:, h, :],
                                       start=(h == 0), stop=(h == NH - 1), skip_group_check=True)
                    mm.then_inc(s["y_mm"], 1)

                def x1_transpose(t):
                    pe.wait_ge(s["x1_n"], t + 1)
                    pe.transpose(PX, x1[:, t % 2, :], ident).then_inc(s["x1_t"], 1)

                def router(t):
                    pe.wait_ge(s["x1_cp"], t + 1)
                    pe.matmul(PX[:, 0:E0], x1T[:, :], w_router[:, :], start=True, stop=True,
                              skip_group_check=True).then_inc(s["lg_mm"], 1)

                def cumulate(t):
                    pe.wait_ge(s["rt"], 5 * t + 4)
                    pe.matmul(PX[:, E0:2 * E0], cst[:, C_TRI:C_TRI + P], onehot[:, :], start=True, stop=False,
                              skip_group_check=True)
                    pe.matmul(PX[:, E0:2 * E0], ones, ohsum[:, :], start=False, stop=True,
                              skip_group_check=True).then_inc(s["cum_mm"], 1)

                for n in range(N0, N1):
                    st, b = divmod(n, NB)
                    if 0 <= n - 4 < NT * NB:
                        o_transpose(n - 4)
                    if 0 <= n < NT * NB:
                        front(n)
                    if 0 <= n - 1 < NT * NB:
                        scores(n - 1)
                    if 0 <= n - 2 < NT * NB:
                        p_transpose(n - 2)
                    if 0 <= n - 3 < NT * NB:
                        weighted(n - 3)
                    if 0 <= st + 3 < NT and b < 2 * chunks_of(st + 3):
                        index_pair(st + 3, b)
                    if n == N0 + 1:
                        for i in range(NT // 4):
                            if i == 0:
                                pe.wait_ge(s["lrot"], 2)
                                pe.wait_ge(s["lat_row"], 4)
                                pe.wait_ge(s["zeroed"], 4)
                            if i >= 2:
                                pe.wait_ge(s["lT_cp"], i - 1)
                            for j in range(4):
                                pe.transpose([psK, psO][i % 2][:, P * j:P * (j + 1)], lrow[:, 4 * i + j, :],
                                             ident).then_inc(s["lT"], 1)
                    if 0 <= st + 1 < NT:
                        if b == 0:
                            q_project(st + 1)
                        if b == 4:
                            q_transpose(st + 1, 0)
                        if b == 6:
                            q_transpose(st + 1, 1)
                    if 0 <= st - 1 < NT and b == 5:
                        out_project(st - 1)
                    if 0 <= st - 2 < NT:
                        if b == 0:
                            x1_transpose(st - 2)
                        if b == 1:
                            router(st - 2)
                        if b == 3:
                            cumulate(st - 2)

            @block.scalar
            def _(act):
                act.wait_ge(s["ld_raw"], 16)
                act.activation(dlt[:, 0, :], raw[:, :], ACT.Exp, scale=-1.0).then_inc(s["rope_a"], 1)
                act.wait_ge(s["rope"], 3)
                act.activation(dlt[:, 3, :], dlt[:, 2, :], ACT.Sin).then_inc(s["rope_a"], 1)
                act.activation(dlt[:, 4, :], dlt[:, 2, :], ACT.Sin, scale=0.5).then_inc(s["rope_a"], 1)
                n = 0
                banks = [psI[0], psI[1], psK, psX]
                for c in range(CHUNKS):
                    for dst, rows in ((kiT[:, :], P), (qiT[:, 0, :], P), (qiT[:, 1, :], P), (cqT[:, :], CQ)):
                        act.wait_ge(s["kproj"], n + 1)
                        to, src = dst[:, CH * c:CH * (c + 1)], banks[n % 4][0:rows, :]
                        if n % 4 in (1, 2):
                            to = to.rearrange("p (t a g) -> p t a g", t=TPC, a=GPB)
                            src = src.rearrange("p (t g a) -> p t a g", t=TPC, a=GPB)
                        act.activation(to, src, ACT.Copy).then_inc(s["kproj_cp"], 1)
                        n += 1
                act.wait_ge(s["mu"], 2)
                for h in range(2):
                    src = [psS, psM][h][:, :].rearrange("p (t d) -> p t d", d=64)[:, :, DR:]
                    for dst in (grow, lrow):
                        act.activation(dst[:, 8 * h:8 * h + 8, 3 * DR:], src, ACT.Copy).then_inc(s["lat_row"], 1)
                for h in range(2):
                    act.wait_ge(s["mu"], h + 1)
                    m = kmu[:, 8 * h:8 * h + 8, :]
                    act.activation(m, m, ACT.Exp).then_inc(s["key_l"], 1)
                    act.wait_ge(s["key_l"], 2 * h + 1)
                    act.activation(m, m, ACT.Ln, bias=1.0).then_inc(s["key_l"], 1)
                act.wait_ge(s["w_mm"], 1)
                act.activation(w_q[:, 0:NH * CKV], psP[0:CQ, 0:NH * CKV], ACT.Copy).then_inc(s["w_cp"], 1)
                for j in range(2):
                    act.wait_ge(s["w_mm"], 2 + j)
                    act.activation(w_vo[:, 4 * j:4 * j + 4, :].rearrange("p h d -> p (h d)"), psP[0:CKV, :],
                                   ACT.Copy).then_inc(s["w_cp"], 1)

                def relu_pair(t, u):
                    c, pair = u // 2, u % 2
                    w = min(CH, keys_of(t) - CH * c)
                    m = 2 * chunk_base(t) + u
                    if m // 2 >= 2:
                        act.wait_ge(s["comb"], 4 * (m // 2 - 1))
                    for i in range(2):
                        act.wait_ge(s["i_mm"], 2 * m + i + 1)
                        act.activation(R[:, (m // 2) % 2, 2 * pair + i, 0:w], psI[i][:, 0:w],
                                       ACT.Relu).then_inc(s["i_relu"], 1)

                def q_softplus(t):
                    act.wait_ge(s["q_chain"], 10 * t + 1)
                    if t >= 1:
                        act.wait_ge(s["q_t"], 2 * t)
                    act.activation(QF[:, :, 3 * DR:], psM[:, 0:NH * CKV].rearrange("p (h d) -> p h d", h=NH),
                                   ACT.Copy, scale=-SCALE).then_inc(s["qf_a"], 1)
                    act.activation(qe[:, :, :, :], qe[:, :, :, :], ACT.Exp).then_inc(s["q_e"], 1)
                    act.wait_ge(s["q_e"], 2 * t + 1)
                    act.activation(qe[:, :, :, :], qe[:, :, :, :], ACT.Ln, bias=1.0).then_inc(s["q_e"], 1)

                def q_copies(t):
                    act.wait_ge(s["q_chain"], 10 * t + 6)
                    act.activation(QF[:, :, DR:DR + HALF], QF[:, :, HALF:DR], ACT.Copy).then_inc(s["qf_a"], 1)
                    act.activation(QF[:, :, DR + HALF:2 * DR], QF[:, :, 0:HALF], ACT.Copy,
                                   scale=-1.0).then_inc(s["qf_a"], 1)

                def q_evac(t, j):
                    act.wait_ge(s["q_t"], 2 * t + j + 1)
                    if t >= 2 and j == 0:
                        act.wait_ge(s["s_mm"], NB * (t - 1))
                    act.activation(Q[:, t % 2, :, 4 * j:4 * j + 4].rearrange("p q h -> p h q"),
                                   psM[:, :].rearrange("p (h q) -> p h q", h=4), ACT.Copy).then_inc(s["q_cp"], 1)

                def exps(n):
                    act.wait_ge(s["s_min"], n + 1)
                    if n == 0:
                        act.wait_ge(s["zeroed"], 4)
                    if n >= 2:
                        act.wait_ge(s["p_t"], n - 1)
                        act.wait_ge(s["orec"], n - 1)
                    act.activation(PR[:, n % 2, 0:NS], S[:, n % 2, :], ACT.Exp, bias=nmin[:, n % 2:n % 2 + 1],
                                   scale=-1.0, accum_out=psumr[:, n % 2:n % 2 + 1]).then_inc(s["p_exp"], 1)

                def p_copy(n):
                    act.wait_ge(s["p_t"], n + 1)
                    if n >= 2:
                        act.wait_ge(s["pv"], n - 1)
                    act.activation(PT[:, n % 2, :], psP[:, 0:2 * P], ACT.Copy).then_inc(s["p_cp"], 1)

                def o_copy(n):
                    t, b = divmod(n, NB)
                    act.wait_ge(s["o_t"], n + 1)
                    if b == 0 and t >= 2:
                        act.wait_ge(s["y_mm"], t - 1)
                    act.activation(OT[:, t % 2, b, :, :].rearrange("p q h -> p (q h)"), psO[0:CKV, P:2 * P],
                                   ACT.Copy).then_inc(s["o_cp"], 1)

                def norm_scale(t):
                    act.wait_ge(s["bn"], 2 * t + 2)
                    act.activation(lnv[:, 0, 0:1], mv[:, 0, 1:2], ACT.Ln,
                                   bias=cst[:, C_EPS:C_EPS + 1]).then_inc(s["ln_a"], 1)
                    act.wait_ge(s["ln_a"], 2 * t + 1)
                    act.activation(lnv[:, 1, 0:1], lnv[:, 0, 0:1], ACT.Exp, scale=-0.5).then_inc(s["ln_a"], 1)

                def x1_copy(t):
                    act.wait_ge(s["x1_n"], t + 1)
                    act.activation(xr[:, t, :], x1[:, t % 2, :], ACT.Copy, scale=2.0).then_inc(s["x1d"], 1)
                    act.wait_ge(s["x1_t"], t + 1)
                    act.activation(x1T[:, :], PX, ACT.Copy).then_inc(s["x1_cp"], 1)

                def gate_exp(t):
                    act.wait_ge(s["rt"], 5 * t + 1)
                    act.activation(rex[:, :], rlog[:, :], ACT.Exp, bias=rsm[:, 0:1],
                                   accum_out=rsm[:, 1:2]).then_inc(s["lg_e"], 1)

                for n in range(N0, N1):
                    st, b = divmod(n, NB)
                    if 0 <= n - 4 < NT * NB:
                        o_copy(n - 4)
                    if 0 <= n - 3 < NT * NB:
                        p_copy(n - 3)
                    if 0 <= n - 2 < NT * NB:
                        exps(n - 2)
                    if 0 <= st + 3 < NT and b < 2 * chunks_of(st + 3):
                        relu_pair(st + 3, b)
                    if n == N0 + 1:
                        for i in range(NT // 4):
                            act.wait_ge(s["lT"], 4 * i + 4)
                            act.activation(klocT[:, PAD + CH * i:PAD + CH * (i + 1)], [psK, psO][i % 2][:, :],
                                           ACT.Copy).then_inc(s["lT_cp"], 1)
                    if 0 <= st + 1 < NT:
                        if b == 1:
                            q_softplus(st + 1)
                        if b == 3:
                            q_copies(st + 1)
                        if b == 5:
                            q_evac(st + 1, 0)
                        if b == 6:
                            q_evac(st + 1, 1)
                    if 0 <= st - 1 < NT and b == 6:
                        norm_scale(st - 1)
                    if 0 <= st - 2 < NT:
                        if b == 0:
                            x1_copy(st - 2)
                        if b == 2:
                            gate_exp(st - 2)

            @block.vector
            def _(dve):
                rope = [0]

                def link(ins):
                    rope[0] += 1
                    ins.then_inc(s["rope"], 1)
                    dve.wait_ge(s["rope"], rope[0])

                dve.wait_ge(s["rope_a"], 1)
                link(dve.tensor_scalar(dlt[:, 0, :], dlt[:, 0, :], 1.0, None, ALU.add))
                link(dve.reciprocal(dlt[:, 1, :], dlt[:, 0, :]))
                link(dve.tensor_scalar(dlt[:, 2, :], dlt[:, 1, :], float(-2 * np.pi), float(np.pi),
                                       ALU.mult, ALU.add))
                dve.wait_ge(s["rope_a"], 3)
                link(dve.tensor_tensor(dlt[:, 5, :], dlt[:, 4, :], dlt[:, 4, :], ALU.mult))
                link(dve.tensor_scalar(dlt[:, 6, :], dlt[:, 5, :], 2.0, -1.0, ALU.mult, ALU.add))
                link(dve.tensor_scalar(dlt[:, 7, :], dlt[:, 3, :], -1.0, None, ALU.mult))
                dve.wait_ge(s["ld_late"], 16 * 8)
                dve.wait_ge(s["ld_cst"], 16)
                cd, sd = dlt[:, 6, HALF:HALF + 1], dlt[:, 7, HALF:HALF + 1]
                link(dve.scalar_tensor_tensor(out=rank_tab[:, :], in0=cst[:, C_RA:C_RA + NSEL], scalar=cd,
                                              in1=cst[:, C_RC:C_RC + NSEL], op0=ALU.mult, op1=ALU.add))
                link(dve.scalar_tensor_tensor(out=rank_tab[:, :], in0=cst[:, C_RB:C_RB + NSEL], scalar=sd,
                                              in1=rank_tab[:, :], op0=ALU.mult, op1=ALU.add))
                cdr = dlt[:, 6:7, 0:HALF].to_broadcast([P, NT, HALF])
                sdr = dlt[:, 7:8, 0:HALF].to_broadcast([P, NT, HALF])
                for k in range(3):
                    c, sn = tab[:, 2 * k, :, :], tab[:, 2 * k + 1, :, :]
                    for dst, a, b, op in ((2 * k, c, sn, ALU.subtract), (2 * k + 1, sn, c, ALU.add)):
                        link(dve.tensor_tensor(rtmp[:, 0, :, :], a, cdr, ALU.mult))
                        link(dve.tensor_tensor(rtmp[:, 1, :, :], b, sdr, ALU.mult))
                        link(dve.tensor_tensor(rot[:, dst, :, :], rtmp[:, 0, :, :], rtmp[:, 1, :, :], op))
                link(dve.tensor_scalar(rot[:, 0:4, :, :].rearrange("p a t f -> p (a t f)"),
                                       rot[:, 0:4, :, :].rearrange("p a t f -> p (a t f)"), -SCALE, None, ALU.mult))
                for h in range(2):
                    dve.wait_ge(s["kv_mm"], h + 1)
                    kr = [psS, psM][h][:, :].rearrange("p (t d) -> p t d", d=64)[:, :, 0:DR]
                    dve.tensor_scalar(kmu[:, 8 * h:8 * h + 8, :], kr, 30.0, None, ALU.min).then_inc(s["mu"], 1)
                for h in range(2):
                    dve.wait_ge(s["key_l"], 2 * h + 2)
                    dve.wait_ge(s["lat_row"], 4)
                    m = kmu[:, 8 * h:8 * h + 8, :]
                    kr = [psS, psM][h][:, :].rearrange("p (t d) -> p t d", d=64)[:, :, 0:DR]
                    dve.tensor_tensor(m, m, kr, ALU.max).then_inc(s["mu"], 1)
                dve.wait_ge(s["mu"], 4)
                for i in range(3):
                    dve.tensor_copy(grow[:, :, DR * i:DR * (i + 1)], kmu[:, :, :]).then_inc(s["mu_row"], 1)
                m1, m2 = kmu[:, :, 0:HALF], kmu[:, :, HALF:DR]
                ck, sk = rot[:, 4, :, :], rot[:, 5, :, :]
                for i, (a, b, op) in enumerate(((m1, m2, ALU.subtract), (m2, m1, ALU.add))):
                    link(dve.tensor_tensor(rtmp[:, 0, :, :], a, ck, ALU.mult))
                    link(dve.tensor_tensor(rtmp[:, 1, :, :], b, sk, ALU.mult))
                    dve.tensor_tensor(lrow[:, :, 2 * DR + HALF * i:2 * DR + HALF * (i + 1)], rtmp[:, 0, :, :],
                                      rtmp[:, 1, :, :], op).then_inc(s["lrot"], 1)
                    dve.wait_ge(s["lrot"], i + 1)

                def combine(t, c):
                    w = min(CH, keys_of(t) - CH * c)
                    m = chunk_base(t) + c
                    dst = SC[:, t % 2, CH * c:CH * c + w]
                    if c == 0 and t >= 2:
                        dve.wait_ge(s["topk"], 12 * (t - 1))
                    dve.wait_ge(s["i_relu"], 4 * (m + 1))
                    dve.tensor_scalar(dst, R[:, m % 2, 0, 0:w], w_i[:, 0:1], None, ALU.mult).then_inc(s["comb"], 1)
                    for h in range(1, NIH):
                        dve.wait_ge(s["comb"], 4 * m + h)
                        dve.scalar_tensor_tensor(out=dst, in0=R[:, m % 2, h, 0:w], scalar=w_i[:, h:h + 1], in1=dst,
                                                 op0=ALU.mult, op1=ALU.add).then_inc(s["comb"], 1)

                def index_mask(t):
                    dve.wait_ge(s["comb"], 4 * chunk_base(t + 1))
                    lo = keys_of(t) - P
                    m = C_IM0 if t == 0 else C_IM
                    dst = SC[:, t % 2, lo:lo + P]
                    dve.tensor_tensor(dst, dst, cst[:, m:m + P], ALU.add).then_inc(s["im"], 1)

                def topk_step(t, k):
                    r, what = divmod(k, 3)
                    a = SC[:, t % 2, 0:keys_of(t)]
                    if k == 0:
                        dve.wait_ge(s["im"], t + 1)
                    if k > 0:
                        dve.wait_ge(s["topk"], 12 * t + k)
                    if k == 11:
                        if t >= 2:
                            for b in range(NB):
                                dve.wait_ge(s_g[t % 2][b], 64 * (t // 2))
                        dve.transpose(idx[:, t % 2, :], idxf[:, :]).then_inc(s["topk"], 1)
                        dve.wait_ge(s["topk"], 12 * t + 12)
                        dve.sem_inc(s["idx_ready"], 1)
                        return
                    if what == 0:
                        ins = dve.max(out=top[:, r, :], in_=a)
                    elif what == 1:
                        ins = dve.max_index(out=idxf[:, 8 * r:8 * r + 8], in_max=top[:, r, :], in_values=a)
                    else:
                        ins = dve.match_replace(out=a, in_to_replace=top[:, r, :], in_values=a, imm_value=LOW)
                    ins.then_inc(s["topk"], 1)

                def q_min(t):
                    dve.wait_ge(s["q_mm"], t + 1)
                    if t >= 1:
                        dve.wait_ge(s["q_chain"], 10 * t)
                    dve.tensor_scalar(qe[:, :, :, :], psM[:, NH * CKV:].rearrange("p (h k f) -> p h k f", h=NH, k=2),
                                      30.0, None, ALU.min).then_inc(s["q_chain"], 1)

                def q_rotate(t, part):
                    base = 10 * t
                    if part == 0:
                        dve.wait_ge(s["q_e"], 2 * t + 2)
                        dve.wait_ge(s["qf_a"], 3 * t + 1)
                        dve.tensor_tensor(qmu[:, :, :, :], qe[:, :, :, :],
                                          psM[:, NH * CKV:].rearrange("p (h k f) -> p h k f", h=NH, k=2),
                                          ALU.max).then_inc(s["q_chain"], 1)
                        dve.wait_ge(s["q_chain"], base + 2)
                    mu2d = qmu[:, :, :, :].rearrange("p h k f -> p (h k) f")
                    for k in (2 * part, 2 * part + 1):
                        dve.tensor_tensor(qt[:, k, :, :], mu2d,
                                          rot[:, k:k + 1, t, :].to_broadcast([P, NH * 2, HALF]),
                                          ALU.mult).then_inc(s["q_chain"], 1)
                    dve.wait_ge(s["q_chain"], base + (4 if part == 0 else 8))
                    tc = qt[:, 2 * part, :, :].rearrange("p (h k) f -> p h k f", k=2)
                    ts = qt[:, 2 * part + 1, :, :].rearrange("p (h k) f -> p h k f", k=2)
                    o = 2 * DR * part
                    if t >= 1:
                        dve.wait_ge(s["q_t"], 2 * t)
                    dve.tensor_tensor(QF[:, :, o:o + HALF], tc[:, :, 0, :], ts[:, :, 1, :],
                                      ALU.subtract).then_inc(s["q_chain"], 1)
                    dve.tensor_tensor(QF[:, :, o + HALF:o + DR], ts[:, :, 0, :], tc[:, :, 1, :],
                                      ALU.add).then_inc(s["q_chain"], 1)

                def k_rotate(n):
                    dve.wait_ge(s["k_t"], n + 1)
                    if n >= 2:
                        dve.wait_ge(s["s_mm"], n - 1)
                    dve.tensor_tensor(KT[:, n % 2, :, :].rearrange("p g (a i) -> p (g a) i", i=NSEL),
                                      psK[:, :].rearrange("p (g i) -> p g i", i=NSEL),
                                      rank_tab[:, None, :].to_broadcast([P, 4 * GPB, NSEL]),
                                      ALU.mult).then_inc(s["k_ev"], 1)

                def s_minimum(n):
                    t, b = divmod(n, NB)
                    dve.wait_ge(s["s_mm"], n + 1)
                    if n >= 2:
                        dve.wait_ge(s["p_exp"], n - 1)
                    m = C_MASK0 if t == 0 and b < 4 else C_MASK
                    dve.tensor_tensor_reduce(out=S[:, n % 2, :], in0=psS[:, 0:NS], in1=cst[:, m:m + NS],
                                             scale=1.0, scalar=3.0e38, op0=ALU.add, op1=ALU.min,
                                             accum_out=nmin[:, n % 2:n % 2 + 1]).then_inc(s["s_min"], 1)

                def o_norm(n):
                    dve.wait_ge(s["p_exp"], n + 1)
                    dve.reciprocal(rinv[:, n % 2:n % 2 + 1], psumr[:, n % 2:n % 2 + 1]).then_inc(s["orec"], 1)
                    dve.wait_ge(s["orec"], n + 1)
                    dve.wait_ge(s["pv"], n + 1)
                    if n >= 2:
                        dve.wait_ge(s["o_t"], n - 1)
                    dve.tensor_scalar(O[:, n % 2, :], psO[:, 0:CKV],
                                      rinv[:, n % 2:n % 2 + 1], None, ALU.mult).then_inc(s["onorm"], 1)

                def add_and_stats(t):
                    dve.wait_ge(s["y_mm"], t + 1)
                    dve.tensor_tensor(xa[:, :], PX, xr[:, t, :], ALU.add).then_inc(s["y_add"], 1)
                    dve.wait_ge(s["y_add"], t + 1)
                    dve.bn_stats(out=stats[:, 0, :], in_=xa[:, :]).then_inc(s["bn"], 1)
                    dve.wait_ge(s["bn"], 2 * t + 1)
                    dve.bn_aggr(out=mv[:, 0, :], in_=stats[:, 0, :]).then_inc(s["bn"], 1)

                def normalize(t):
                    dve.wait_ge(s["ln_a"], 2 * t + 2)
                    if t >= 2:
                        dve.wait_ge(s_sct[t % 2], 16 * (t // 2))
                        dve.wait_ge(s["x1d"], t - 1)
                        dve.wait_ge(s["x1_cp"], t - 1)
                    dve.tensor_scalar(x1[:, t % 2, :], xa[:, :], mv[:, 0, 0:1], lnv[:, 1, 0:1], ALU.subtract,
                                      ALU.mult).then_inc(s["x1_n"], 1)

                def route(t):
                    dve.wait_ge(s["lg_mm"], t + 1)
                    if t >= 1:
                        dve.wait_ge(s["lg_e"], t)
                    dve.tensor_copy(rlog[:, :], PX[:, 0:E0]).then_inc(s["lg_cp"], 1)
                    dve.wait_ge(s["lg_cp"], t + 1)
                    dve.max(out=r8[:, :], in_=rlog[:, :]).then_inc(s["rt_a"], 1)
                    dve.wait_ge(s["rt_a"], 4 * t + 1)
                    dve.tensor_scalar(rsm[:, 0:1], r8[:, 0:1], -1.0, None, ALU.mult).then_inc(s["rt"], 1)
                    dve.max_index(out=r8i[:, :], in_max=r8[:, :], in_values=rlog[:, :]).then_inc(s["rt"], 1)
                    dve.wait_ge(s["rt"], 5 * t + 2)
                    dve.tensor_copy(rsm[:, 2:3], r8i[:, 0:1]).then_inc(s["rt"], 1)
                    dve.wait_ge(s["rt"], 5 * t + 3)
                    dve.tensor_scalar(onehot[:, :], cst[:, C_IOTA:C_IOTA + E0], rsm[:, 2:3], None,
                                      ALU.is_equal).then_inc(s["rt"], 1)

                def place(t):
                    dve.wait_ge(s["cum_mm"], t + 1)
                    dve.tensor_tensor(ohsum[:, :], ohsum[:, :], onehot[:, :], ALU.add).then_inc(s["rt"], 1)
                    dve.tensor_tensor_reduce(out=rjunk[:, :], in0=PX[:, E0:2 * E0], in1=onehot[:, :], scale=1.0,
                                             scalar=0.0, op0=ALU.mult, op1=ALU.add,
                                             accum_out=rsm[:, 3:4]).then_inc(s["rte"], 1)
                    dve.wait_ge(s["rte"], t + 1)
                    dve.wait_ge(s["lg_e"], t + 1)
                    dve.tensor_scalar(rsm[:, 4:5], rsm[:, 3:4], float(C0), None, ALU.is_le).then_inc(s["rt_a"], 1)
                    dve.reciprocal(rsm[:, 5:6], rsm[:, 1:2]).then_inc(s["rt_a"], 1)
                    dve.scalar_tensor_tensor(out=rsm[:, 6:7], in0=rsm[:, 2:3], scalar=float(C0), in1=rsm[:, 3:4],
                                             op0=ALU.mult, op1=ALU.add).then_inc(s["rt_a"], 1)
                    dve.wait_ge(s["rt_a"], 4 * t + 4)
                    dve.tensor_tensor(gm[:, t:t + 1], rsm[:, 5:6], rsm[:, 4:5], ALU.mult).then_inc(s["plc"], 1)
                    dve.tensor_scalar(rsm[:, 7:8], rsm[:, 4:5], -2.0 * NSLOT, 2.0 * NSLOT - 1.0, ALU.mult,
                                      ALU.add).then_inc(s["plc"], 1)
                    dve.tensor_scalar(slot_out[:, t:t + 1], rsm[:, 6:7], -1.0, float(NSLOT - 1), ALU.add,
                                      ALU.min).then_inc(s["plc"], 1)
                    dve.wait_ge(s["plc"], 3 * (t + 1))
                    dve.tensor_tensor(slot_in[:, t:t + 1], rsm[:, 6:7], rsm[:, 7:8],
                                      ALU.add).then_inc(s["slots_ready"], 1)

                for n in range(N0, N1):
                    st, b = divmod(n, NB)
                    if 0 <= n < NT * NB:
                        k_rotate(n)
                    if 0 <= n - 1 < NT * NB:
                        s_minimum(n - 1)
                    if 0 <= n - 3 < NT * NB:
                        o_norm(n - 3)
                    if 0 <= st + 3 < NT:
                        t = st + 3
                        for c in range(chunks_of(t)):
                            if b == min(2 * c + 2, NB - 1):
                                combine(t, c)
                                if c == chunks_of(t) - 1:
                                    index_mask(t)
                    if 0 <= st + 2 < NT and b < 6:
                        topk_step(st + 2, 2 * b)
                        topk_step(st + 2, 2 * b + 1)
                    if 0 <= st + 1 < NT:
                        if b == 0:
                            q_min(st + 1)
                        if b == 2:
                            q_rotate(st + 1, 0)
                        if b == 3:
                            q_rotate(st + 1, 1)
                    if 0 <= st - 1 < NT:
                        if b == 6:
                            add_and_stats(st - 1)
                        if b == 7:
                            normalize(st - 1)
                    if 0 <= st - 2 < NT:
                        if b == 2:
                            route(st - 2)
                        if b == 4:
                            place(st - 2)

        flat = G[:, :, :, :].rearrange("p a g n -> p (a g n)")
        strips = {}
        for region, view, parts in (
                ("G", flat, (("x2", NT * D), ("x2T", L), ("vT", L + 2 * ROLL), ("acc", CH), ("tmp", CH), ("mvs", 64))),
                ("R", R[:, :, :, :].rearrange("p a h n -> p (a h n)"), (("yg", NT * D), ("sig", 4 * CH))),
                ("SC", SC[:, :, :].rearrange("p a n -> p (a n)"),
                 (("xb", 2 * EG * D), ("xbT", 2 * EG * C0), ("hid", EG * C0), ("sil", EG * C0), ("yb", 2 * EG * D))),
                ("Q", Q[:, :, :, :].rearrange("p a q h -> p (a q h)"), (("x3", 2 * CH), ("x3T", 2 * CH))),
                ("OT", ot_region[:, :], (("sl", 2 * CH), ("hd", 2 * CH))),
                ("KT", KT[:, :, :, :].rearrange("p a g n -> p (a g n)"), (("n1", CH), ("s2", CH))),
                ("QF", QF[:, :, :].rearrange("p h n -> p (h n)"), (("accf", CH), ("res", CH))),
                ("PT", PT[:, :, :].rearrange("p a n -> p (a n)"), (("tmpP", CH),)),
                ("PR", PR[:, :, :].rearrange("p a n -> p (a n)"), (("accP", CH),))):
            at = 0
            for name, size in parts:
                strips[name] = view[:, at:at + size]
                at += size
            assert at <= view.shape[1], (region, at)
        second_part(nc, dram, out, ctx, sem, strips, dict(
            cst=cst, ident=ident, xr=xr, gm=gm, slot_out=slot_out, w_ex=w_ex, s_we=s_we, load_experts=load_experts,
            w_value=w_value, w_gates=w_gates, w_up=w_up, w_down=w_down, gamma=gamma, beta=beta, w_g8=w_g8,
            xslots=xslots, yslots=yslots, banks=[psK, psX, psI[0], psI[1], psS, psP, psO, psM]))


def second_part(nc, dram, out, ctx, sem, m, k):
    cst, ident, xr, gm, w_ex, s_we = k["cst"], k["ident"], k["xr"], k["gm"], k["w_ex"], k["s_we"]
    w_value, w_gates, w_up, w_down = k["w_value"], k["w_gates"], k["w_up"], k["w_down"]
    gamma, beta, w_g8 = k["gamma"], k["beta"], k["w_g8"]
    bank = k["banks"]
    GC = EG * C0
    xb = m["xb"].rearrange("p (a e n) -> p a e n", a=2, e=EG)
    yb = m["yb"].rearrange("p (a e n) -> p a e n", a=2, e=EG)
    xbT = m["xbT"].rearrange("p (a n) -> p a n", a=2)
    hid, sil = m["hid"], m["sil"]
    yg = m["yg"].rearrange("p (t n) -> p t n", t=NT)
    x2 = m["x2"].rearrange("p (t n) -> p t n", t=NT)
    x2T, vT = m["x2T"], m["vT"]
    sig = m["sig"].rearrange("p (a n) -> p a n", a=4)
    acc, tmp, accP, tmpP = m["acc"], m["tmp"], m["accP"], m["tmpP"]
    x3 = m["x3"].rearrange("p (a t n) -> p a t n", a=2, t=TPC)
    x3T = m["x3T"].rearrange("p (a n) -> p a n", a=2)
    sl = m["sl"].rearrange("p (a n) -> p a n", a=2)
    hd = m["hd"].rearrange("p (a n) -> p a n", a=2)
    n1 = m["n1"].rearrange("p (t n) -> p t n", t=TPC)
    s2 = m["s2"].rearrange("p (t n) -> p t n", t=TPC)
    accf = m["accf"].rearrange("p (t n) -> p t n", t=TPC)
    res = m["res"].rearrange("p (t n) -> p t n", t=TPC)

    def sb(name, shape, dt=F32):
        return ctx.enter_context(nc.sbuf_tensor(name, shape, dt))

    stt = sb("stt", [P, TPC, 6])
    mv = sb("mv2", [P, TPC, 2])
    rstd = sb("rstd", [P, TPC])
    half = sb("half", [P, TPC])
    lg = sb("lg", [P, TPC, E1])
    lmax = sb("lmax", [P, TPC])
    lsum = sb("lsum", [P, TPC])
    t8 = sb("t8", [P, TPC, 8])
    t8i = sb("t8i", [P, TPC, 8], U32)
    t8f = sb("t8f", [P, TPC, 8])
    oh = sb("oh", [P, 2, TPC, E1])
    wt = sb("wt", [P, 2, TPC, E1])
    den = sb("den", [P, 2, TPC])
    out_rows = out.rearrange("(c t p) d -> c p t d", t=TPC, p=P)

    names = """xbt xbt_cp gate up silu hid y_mm y_cp y_st z ln pool_r x2_n x2_t x2_cp v_mm v_cp wrap
        x2b gt_mm sig prod prodP acc_done o_t lnc x3_t x3_cp lg_mm rt lexp wts h_mm g_mm sl hd d_mm dacc fin st_out
        halfset""".split()
    s = {n: sem("t_" + n) for n in names}
    s_xb = [sem(f"t_xb{i}") for i in range(2)]
    s_yst = [sem(f"t_yst{i}") for i in range(2)]
    s_yg = [sem(f"t_yg{c}") for c in range(NCH)]
    s_out = [sem(f"t_out{i}") for i in range(2)]

    POOL_GATES = (2, 5, 8)
    NPG = len(POOL_GATES)
    DVE_GATES = tuple(i for i in range(NGATE) if i not in POOL_GATES)
    NDG = len(DVE_GATES)
    ORDER = (E1, E1 + 1) + tuple(range(E1))

    with nc.Block() as block:
        @block.sync
        def _(sp):
            for g in range(NEG):
                if g >= 2:
                    sp.wait_ge(s["xbt"], g - 1)
                    sp.wait_ge(s_xb[g % 2], 16 * (g // 2))
                sp.dma_start(xb[0:C0, g % 2, :, :],
                             k["xslots"][GC * g:GC * (g + 1), :].rearrange("(e c) d -> c e d", c=C0)
                             ).then_inc(s_xb[g % 2], 16)
                if g >= 2:
                    sp.wait_ge(s["y_mm"], g - 1)
                    k["load_experts"](sp, g)
            for c in range(NCH):
                sp.wait_ge(s["fin"], c + 1)
                sp.dma_start(out_rows[c], res).then_inc(s_out[c % 2], 16)
                sp.wait_ge(s_out[c % 2], 16 * (c // 2 + 1))

        @block.gpsimd
        def _(pool):
            pool.memset(half[:, :], -0.5).then_inc(s["halfset"], 1)
            pool.wait_ge(s["halfset"], 1)
            for i in range(2):
                pool.wait_ge(s_yst[i], 16 * NEG // 2)
            for t in range(NT):
                pool.indirect_dma_start(yg[:, t, :], None, k["yslots"],
                                        bass.IndirectOffsetOnAxis(ap=k["slot_out"][:, t:t + 1], axis=0)
                                        ).then_inc(s_yg[t // TPC], 16)
            done = [0]

            def root(n_stats):
                pool.wait_ge(s["ln"], n_stats)
                pool.tensor_scalar(rstd[:, :], mv[:, :, 1], LN_EPS, None, ALU.add).then_inc(s["pool_r"], 1)
                done[0] += 1
                pool.wait_ge(s["pool_r"], done[0])
                pool.tensor_tensor(rstd[:, :], rstd[:, :], half[:, :], ALU.pow).then_inc(s["pool_r"], 1)
                done[0] += 1

            for c in range(NCH):
                root(8 * (c + 1))
            pool.wait_ge(s["x2_t"], NCH)
            for c in range(NCH):
                pool.tensor_tensor(x2[:, TPC * c:TPC * (c + 1), :], x2[:, TPC * c:TPC * (c + 1), :],
                                   beta[:, None, :].to_broadcast([P, TPC, D]), ALU.add).then_inc(s["x2b"], 1)
            pool.wait_ge(s["wrap"], 2)
            seen = 8 * NCH
            for j in range(-1, NCH):
                if j + 1 < NCH:
                    c = j + 1
                    for i, g in enumerate(POOL_GATES):
                        n = NGATE * c + g
                        base = (2 * NPG - 1) * c
                        v = vT[:, ROLL + SHIFTS[g] + CH * c:ROLL + SHIFTS[g] + CH * (c + 1)]
                        pool.wait_ge(s["sig"], n + 1)
                        if i == 0:
                            if c >= 1:
                                pool.wait_ge(s["acc_done"], c)
                            pool.tensor_tensor(accP, v, sig[:, n % 4, :], ALU.mult).then_inc(s["prodP"], 1)
                        else:
                            pool.wait_ge(s["prodP"], base + 2 * i - 1)
                            pool.tensor_tensor(tmpP, v, sig[:, n % 4, :], ALU.mult).then_inc(s["prodP"], 1)
                            pool.wait_ge(s["prodP"], base + 2 * i)
                            pool.tensor_tensor(accP, accP, tmpP, ALU.add).then_inc(s["prodP"], 1)
                    for _ in range(2):
                        seen += 8
                        root(seen)
                if j >= 0:
                    seen += 8
                    root(seen)

        @block.tensor
        def _(pe):
            def expert_front(g):
                pe.wait_ge(s_xb[g % 2], 16 * (g // 2 + 1))
                if g >= 2:
                    pe.wait_ge(s["xbt_cp"], g - 1)
                for e in range(EG):
                    mm = pe.transpose(bank[g % 2][:, C0 * e:C0 * (e + 1)], xb[0:C0, g % 2, e, :], ident[0:C0, 0:C0])
                mm.then_inc(s["xbt"], 1)
                pe.wait_ge(s["xbt_cp"], g + 1)
                pe.wait_ge(s_we[g % 2], 48 * (g // 2 + 1))
                if g >= 1:
                    pe.wait_ge(s["silu"], g)
                for e in range(EG):
                    mm = pe.matmul(bank[2][:, C0 * e:C0 * (e + 1)], w_ex[:, g % 2, 0, e, :],
                                   xbT[:, g % 2, C0 * e:C0 * (e + 1)], start=True, stop=True, skip_group_check=True)
                mm.then_inc(s["gate"], 1)
                if g >= 1:
                    pe.wait_ge(s["hid"], g)
                for e in range(EG):
                    mm = pe.matmul(bank[3][:, C0 * e:C0 * (e + 1)], w_ex[:, g % 2, 1, e, :],
                                   xbT[:, g % 2, C0 * e:C0 * (e + 1)], start=True, stop=True, skip_group_check=True)
                mm.then_inc(s["up"], 1)

            def expert_down(g):
                pe.wait_ge(s["hid"], g + 1)
                if g >= 2:
                    pe.wait_ge(s["y_cp"], g - 1)
                for e in range(EG):
                    mm = pe.matmul(bank[4 + g % 2][0:C0, D * e:D * (e + 1)], hid[:, C0 * e:C0 * (e + 1)],
                                   w_ex[:, g % 2, 2, e, :], start=True, stop=True, skip_group_check=True)
                mm.then_inc(s["y_mm"], 1)

            for g in range(NEG):
                expert_front(g)
                expert_down(g)
            for c in range(NCH):
                pe.wait_ge(s["x2_n"], TPC * (c + 1))
                if c >= 2:
                    pe.wait_ge(s["x2_cp"], c - 1)
                for t in range(TPC):
                    mm = pe.transpose(bank[c % 2][:, P * t:P * (t + 1)], x2[:, TPC * c + t, :], ident)
                mm.then_inc(s["x2_t"], 1)
            for c in range(NCH):
                pe.wait_ge(s["x2_cp"], c + 1)
                pe.matmul(bank[2 + c][:, :], w_value, x2T[:, CH * c:CH * (c + 1)], start=True,
                          stop=True).then_inc(s["v_mm"], 1)

            def gates(c):
                for g in range(NGATE):
                    n = NGATE * c + g
                    if n == 0:
                        pe.wait_ge(s["x2_cp"], NCH)
                    if n >= 2:
                        pe.wait_ge(s["sig"], n - 1)
                    if g == 0 and c >= 1:
                        pe.wait_ge(s["x3_cp"], c)
                        pe.wait_ge(s["rt"], 14 * c - 12)
                    pe.matmul(bank[n % 2][:, :], w_gates[:, D * g:D * (g + 1)], x2T[:, CH * c:CH * (c + 1)],
                              start=True, stop=True).then_inc(s["gt_mm"], 1)

            def mixed_transpose(c):
                pe.wait_ge(s["acc_done"], c + 1)
                pe.wait_ge(s["sig"], NGATE * (c + 1))
                for t in range(TPC):
                    mm = pe.transpose(bank[0][:, P * t:P * (t + 1)], acc[:, P * t:P * (t + 1)], ident)
                mm.then_inc(s["o_t"], 1)

            def x3_transpose(c):
                pe.wait_ge(s["lnc"], 10 * (c + 1))
                for t in range(TPC):
                    mm = pe.transpose(bank[0][:, P * t:P * (t + 1)], x3[:, c % 2, t, :], ident)
                mm.then_inc(s["x3_t"], 1)

            def route_logits(c):
                pe.wait_ge(s["x3_cp"], c + 1)
                for t in range(TPC):
                    mm = pe.matmul(bank[1][:, E1 * t:E1 * (t + 1)], x3T[:, c % 2, P * t:P * (t + 1)], w_g8,
                                   start=True, stop=True, skip_group_check=True)
                mm.then_inc(s["lg_mm"], 1)

            def ffn_up(c, i):
                n = NHC * c + i
                if n == 0:
                    pe.wait_ge(s["v_cp"], NCH)
                if n >= 2:
                    pe.wait_ge(s["sl"], n - 1)
                    pe.wait_ge(s["hd"], n - 1)
                e = ORDER[i]
                pe.matmul(bank[2 + 2 * (n % 2)][0:H1, :], w_up[:, 0, e, :], x3T[:, c % 2, :], start=True,
                          stop=True).then_inc(s["h_mm"], 1)
                pe.matmul(bank[3 + 2 * (n % 2)][0:H1, :], w_up[:, 1, e, :], x3T[:, c % 2, :], start=True,
                          stop=True).then_inc(s["g_mm"], 1)

            def ffn_down(c, i):
                n = NHC * c + i
                m_ = 9 * c + i - 1
                if m_ >= 2:
                    pe.wait_ge(s["dacc"], m_ - 1)
                pe.wait_ge(s["hd"], n + 1)
                parts = (0, 1) if i == 1 else (i,)
                for t in range(TPC):
                    for p in parts:
                        mm = pe.matmul(bank[6 + m_ % 2][:, D * t:D * (t + 1)],
                                       hd[0:H1, (NHC * c + p) % 2, P * t:P * (t + 1)], w_down[:, ORDER[p], :],
                                       start=(p == parts[0]), stop=(p == parts[-1]), skip_group_check=True)
                mm.then_inc(s["d_mm"], 1)

            for j in range(-1, NCH):
                if j + 1 < NCH:
                    gates(j + 1)
                for i in range(NHC + 1):
                    if j >= 0 and i < NHC:
                        ffn_up(j, i)
                    if j >= 0 and i >= 2:
                        ffn_down(j, i - 1)
                    if j + 1 < NCH:
                        if i == 1:
                            mixed_transpose(j + 1)
                        if i == 6:
                            x3_transpose(j + 1)
                        if i == 8:
                            route_logits(j + 1)

        @block.scalar
        def _(act):
            for g in range(NEG):
                act.wait_ge(s["gate"], g + 1)
                if g >= 1:
                    act.wait_ge(s["hid"], g)
                act.activation(sil, bank[2][:, 0:GC], ACT.Silu).then_inc(s["silu"], 1)
                act.wait_ge(s["y_mm"], g + 1)
                if g >= 2:
                    act.wait_ge(s_yst[g % 2], 16 * (g // 2))
                act.activation(yb[0:C0, g % 2, :, :].rearrange("p e n -> p (e n)"), bank[4 + g % 2][0:C0, :],
                               ACT.Copy).then_inc(s["y_cp"], 1)
                act.wait_ge(s["y_cp"], g + 1)
                act.dma_start(k["yslots"][GC * g:GC * (g + 1), :].rearrange("(e c) d -> c e d", c=C0),
                              yb[0:C0, g % 2, :, :]).then_inc(s_yst[g % 2], 16)
            for c in range(NCH):
                act.wait_ge(s["x2_t"], c + 1)
                act.activation(x2T[:, CH * c:CH * (c + 1)], bank[c % 2][:, :], ACT.Copy).then_inc(s["x2_cp"], 1)
            for c in range(NCH):
                act.wait_ge(s["v_mm"], c + 1)
                act.activation(vT[:, ROLL + CH * c:ROLL + CH * (c + 1)], bank[2 + c][:, :],
                               ACT.Copy).then_inc(s["v_cp"], 1)
            act.wait_ge(s["v_cp"], NCH)
            act.activation(vT[:, 0:ROLL], vT[:, L:L + ROLL], ACT.Copy).then_inc(s["wrap"], 1)
            act.activation(vT[:, ROLL + L:], vT[:, ROLL:2 * ROLL], ACT.Copy).then_inc(s["wrap"], 1)
            for j in range(-1, NCH):
                if j + 1 < NCH:
                    c = j + 1
                    for g in range(NGATE):
                        n = NGATE * c + g
                        act.wait_ge(s["gt_mm"], n + 1)
                        if n >= 4:
                            wait_product(act, s, n - 4, DVE_GATES, POOL_GATES)
                        act.activation(sig[:, n % 4, :], bank[n % 2][:, :], ACT.Sigmoid).then_inc(s["sig"], 1)
                for i in range(NHC):
                    if j >= 0:
                        n = NHC * j + i
                        act.wait_ge(s["h_mm"], n + 1)
                        if n >= 2:
                            act.wait_ge(s["hd"], n - 1)
                        act.activation(sl[0:H1, n % 2, :], bank[2 + 2 * (n % 2)][0:H1, :],
                                       ACT.Silu).then_inc(s["sl"], 1)
                if j + 1 < NCH:
                    c = j + 1
                    act.wait_ge(s["rt"], 14 * c + 2)
                    act.activation(lg[:, :, :], lg[:, :, :], ACT.Exp).then_inc(s["lexp"], 1)

        @block.vector
        def _(dve):
            for g in range(NEG):
                dve.wait_ge(s["xbt"], g + 1)
                if g >= 2:
                    dve.wait_ge(s["up"], g - 1)
                dve.tensor_copy(xbT[:, g % 2, :], bank[g % 2][:, 0:GC]).then_inc(s["xbt_cp"], 1)
                dve.wait_ge(s["silu"], g + 1)
                dve.wait_ge(s["up"], g + 1)
                if g >= 1:
                    dve.wait_ge(s["y_mm"], g)
                dve.tensor_tensor(hid, sil, bank[3][:, 0:GC], ALU.mult).then_inc(s["hid"], 1)
            for c in range(NCH):
                dve.wait_ge(s_yg[c], 16 * TPC)
                for i in range(TPC):
                    t = TPC * c + i
                    dve.scalar_tensor_tensor(out=yg[:, t, :], in0=yg[:, t, :], scalar=gm[:, t:t + 1],
                                             in1=xr[:, t, :], op0=ALU.mult, op1=ALU.add).then_inc(s["z"], 1)
                for i in range(TPC):
                    t = TPC * c + i
                    dve.wait_ge(s["z"], t + 1)
                    if c >= 1 and i == 0:
                        dve.wait_ge(s["x2_n"], TPC * c)
                    dve.bn_stats(out=stt[:, i, :], in_=yg[:, t, :]).then_inc(s["ln"], 1)
                for i in range(TPC):
                    dve.wait_ge(s["ln"], 8 * c + i + 1)
                    dve.bn_aggr(out=mv[:, i, :], in_=stt[:, i, :]).then_inc(s["ln"], 1)
                dve.wait_ge(s["pool_r"], 2 * (c + 1))
                for i in range(TPC):
                    t = TPC * c + i
                    dve.tensor_scalar(x2[:, t, :], yg[:, t, :], mv[:, i, 0:1], rstd[:, i:i + 1], ALU.subtract,
                                      ALU.mult).then_inc(s["x2_n"], 1)
            lnn = [8 * NCH]
            pooln = [2 * NCH]

            def statistics(src, after):
                after()
                for i in range(TPC):
                    dve.bn_stats(out=stt[:, i, :], in_=src(i)).then_inc(s["ln"], 1)
                    lnn[0] += 1
                for i in range(TPC):
                    dve.wait_ge(s["ln"], lnn[0] - TPC + i + 1)
                    dve.bn_aggr(out=mv[:, i, :], in_=stt[:, i, :]).then_inc(s["ln"], 1)
                lnn[0] += TPC

            def wait_root():
                pooln[0] += 2
                dve.wait_ge(s["pool_r"], pooln[0])

            def product(c, g):
                i = DVE_GATES.index(g)
                n = NGATE * c + g
                base = (2 * NDG - 1) * c
                v = vT[:, ROLL + SHIFTS[g] + CH * c:ROLL + SHIFTS[g] + CH * (c + 1)]
                dve.wait_ge(s["sig"], n + 1)
                if i == 0:
                    if c == 0:
                        dve.wait_ge(s["wrap"], 2)
                    else:
                        dve.wait_ge(s["o_t"], c)
                    dve.tensor_tensor(acc, v, sig[:, n % 4, :], ALU.mult).then_inc(s["prod"], 1)
                else:
                    dve.tensor_tensor(tmp, v, sig[:, n % 4, :], ALU.mult).then_inc(s["prod"], 1)
                    dve.wait_ge(s["prod"], base + 2 * i)
                    dve.tensor_tensor(acc, acc, tmp, ALU.add).then_inc(s["prod"], 1)
                    dve.wait_ge(s["prod"], base + 2 * i + 1)

            def mix_sum(c):
                dve.wait_ge(s["prodP"], (2 * NPG - 1) * (c + 1))
                dve.tensor_tensor(acc, acc, accP, ALU.add).then_inc(s["acc_done"], 1)

            def norm1(c):
                statistics(lambda i: bank[0][:, P * i:P * (i + 1)], lambda: dve.wait_ge(s["o_t"], c + 1))

            def norm2(c):
                b = 10 * c
                wait_root()
                for i in range(TPC):
                    dve.tensor_scalar(n1[:, i, :], bank[0][:, P * i:P * (i + 1)], mv[:, i, 0:1], rstd[:, i:i + 1],
                                      ALU.subtract, ALU.mult).then_inc(s["lnc"], 1)
                dve.wait_ge(s["lnc"], b + 4)
                dve.tensor_tensor(n1, n1, gamma[:, None, :].to_broadcast([P, TPC, D]), ALU.mult).then_inc(s["lnc"], 1)
                dve.wait_ge(s["lnc"], b + 5)
                dve.wait_ge(s["x2b"], c + 1)
                dve.tensor_tensor(s2, n1, x2[:, TPC * c:TPC * (c + 1), :], ALU.add).then_inc(s["lnc"], 1)
                dve.wait_ge(s["lnc"], b + 6)
                statistics(lambda i: s2[:, i, :], lambda: None)

            def norm3(c):
                wait_root()
                for i in range(TPC):
                    dve.tensor_scalar(x3[:, c % 2, i, :], s2[:, i, :], mv[:, i, 0:1], rstd[:, i:i + 1],
                                      ALU.subtract, ALU.mult).then_inc(s["lnc"], 1)

            def x3_copy(c):
                dve.wait_ge(s["x3_t"], c + 1)
                dve.tensor_copy(x3T[:, c % 2, :], bank[0][:, :]).then_inc(s["x3_cp"], 1)

            def route_max(c):
                b = 14 * c
                dve.wait_ge(s["lg_mm"], c + 1)
                l4 = bank[1][:, 0:TPC * E1].rearrange("p (t e) -> p t e", t=TPC)
                dve.tensor_reduce(lmax[:, :], l4, mybir.AxisListType.X, ALU.max).then_inc(s["rt"], 1)
                dve.wait_ge(s["rt"], b + 1)
                dve.tensor_tensor(lg[:, :, :], l4, lmax[:, :, None].to_broadcast([P, TPC, E1]),
                                  ALU.subtract).then_inc(s["rt"], 1)

            def route_weights(c):
                b = 14 * c
                dve.wait_ge(s["lexp"], c + 1)
                dve.tensor_reduce(lsum[:, :], lg[:, :, :], mybir.AxisListType.X, ALU.add).then_inc(s["rt"], 1)
                dve.wait_ge(s["rt"], b + 3)
                dve.reciprocal(lsum[:, :], lsum[:, :]).then_inc(s["rt"], 1)
                dve.wait_ge(s["rt"], b + 4)
                dve.tensor_tensor(lg[:, :, :], lg[:, :, :], lsum[:, :, None].to_broadcast([P, TPC, E1]),
                                  ALU.mult).then_inc(s["rt"], 1)
                dve.wait_ge(s["rt"], b + 5)
                for i in range(TPC):
                    ins = dve.max(out=t8[:, i, :], in_=lg[:, i, :])
                ins.then_inc(s["rt"], 1)
                dve.wait_ge(s["rt"], b + 6)
                for i in range(TPC):
                    ins = dve.max_index(out=t8i[:, i, :], in_max=t8[:, i, :], in_values=lg[:, i, :])
                ins.then_inc(s["rt"], 1)
                dve.wait_ge(s["rt"], b + 7)
                dve.tensor_copy(t8f[:, :, :], t8i[:, :, :]).then_inc(s["rt"], 1)
                dve.tensor_tensor(den[:, 0, :], t8[:, :, 0], t8[:, :, 1], ALU.add).then_inc(s["rt"], 1)
                dve.wait_ge(s["rt"], b + 9)
                dve.tensor_scalar(den[:, 0, :], den[:, 0, :], SUM_EPS, None, ALU.add).then_inc(s["rt"], 1)
                iota = cst[:, None, C_IOTA:C_IOTA + E1].to_broadcast([P, TPC, E1])
                for i in range(2):
                    dve.tensor_tensor(oh[:, i, :, :], iota, t8f[:, :, i:i + 1].to_broadcast([P, TPC, E1]),
                                      ALU.is_equal).then_inc(s["rt"], 1)
                dve.wait_ge(s["rt"], b + 12)
                dve.reciprocal(den[:, 1, :], den[:, 0, :]).then_inc(s["rt"], 1)
                for i in range(2):
                    ins = dve.tensor_tensor(oh[:, i, :, :], oh[:, i, :, :],
                                            t8[:, :, i:i + 1].to_broadcast([P, TPC, E1]), ALU.mult)
                ins.then_inc(s["rt"], 1)
                dve.wait_ge(s["rt"], b + 14)
                dve.tensor_tensor(oh[:, 0, :, :], oh[:, 0, :, :], oh[:, 1, :, :], ALU.add).then_inc(s["wts"], 1)
                dve.wait_ge(s["wts"], 2 * c + 1)
                dve.tensor_tensor(wt[:, c % 2, :, :], oh[:, 0, :, :], den[:, 1, :, None].to_broadcast([P, TPC, E1]),
                                  ALU.mult).then_inc(s["wts"], 1)

            def hidden(c, i):
                n = NHC * c + i
                dve.wait_ge(s["sl"], n + 1)
                dve.wait_ge(s["g_mm"], n + 1)
                if n >= 2:
                    if i == 2:
                        dve.wait_ge(s["d_mm"], 9 * c + 1)
                    elif i < 2:
                        dve.wait_ge(s["d_mm"], 9 * (c - 1) + 8 + i)
                    else:
                        dve.wait_ge(s["d_mm"], 9 * c + i - 2)
                dve.tensor_tensor(hd[0:H1, n % 2, :], sl[0:H1, n % 2, :], bank[3 + 2 * (n % 2)][0:H1, :],
                                  ALU.mult).then_inc(s["hd"], 1)

            def accumulate(c, i):
                m_ = 9 * c + i - 1
                dve.wait_ge(s["d_mm"], m_ + 1)
                src = bank[6 + m_ % 2][:, :].rearrange("p (t n) -> p t n", t=TPC)
                if m_ >= 1:
                    dve.wait_ge(s["dacc"], m_)
                if i == 1:
                    dve.tensor_tensor(accf, src, x3[:, c % 2, :, :], ALU.add).then_inc(s["dacc"], 1)
                else:
                    e = ORDER[i]
                    if i == 2:
                        dve.wait_ge(s["wts"], 2 * c + 2)
                    for t in range(TPC):
                        ins = dve.scalar_tensor_tensor(out=accf[:, t, :], in0=src[:, t, :],
                                                       scalar=wt[:, c % 2, t, e:e + 1], in1=accf[:, t, :],
                                                       op0=ALU.mult, op1=ALU.add)
                    ins.then_inc(s["dacc"], 1)

            def finish(c):
                dve.wait_ge(s["dacc"], 9 * (c + 1))
                statistics(lambda i: accf[:, i, :], lambda: None)
                wait_root()
                if c >= 1:
                    dve.wait_ge(s_out[(c - 1) % 2], 16 * ((c - 1) // 2 + 1))
                for i in range(TPC):
                    ins = dve.tensor_scalar(res[:, i, :], accf[:, i, :], mv[:, i, 0:1], rstd[:, i:i + 1],
                                            ALU.subtract, ALU.mult)
                ins.then_inc(s["fin"], 1)

            for j in range(-1, NCH):
                nx = j + 1 < NCH
                if nx:
                    for g in DVE_GATES:
                        product(j + 1, g)
                    mix_sum(j + 1)
                for i in range(NHC + 1):
                    if j >= 0 and i < NHC:
                        hidden(j, i)
                    if j >= 0 and i >= 2:
                        accumulate(j, i - 1)
                    if nx:
                        if i == 1:
                            norm1(j + 1)
                        if i == 3:
                            norm2(j + 1)
                        if i == 5:
                            norm3(j + 1)
                        if i == 6:
                            x3_copy(j + 1)
                        if i == 8:
                            route_max(j + 1)
                if j >= 0:
                    finish(j)
                if nx:
                    route_weights(j + 1)


def wait_product(act, s, n, dve_gates, pool_gates):
    c, g = divmod(n, NGATE)
    if g in pool_gates:
        i = pool_gates.index(g)
        act.wait_ge(s["prodP"], (2 * len(pool_gates) - 1) * c + max(2 * i, 1))
    else:
        i = dve_gates.index(g)
        act.wait_ge(s["prod"], (2 * len(dve_gates) - 1) * c + max(2 * i, 1))


def kernel(**inputs):
    import concourse.bacc as _bacc
    from concourse.bass_utils import run_bass_kernel_spmd as _run

    def a(name):
        return np.asarray(inputs[name])

    consts, tables = shape_constants()
    raw = a("L0_attn_raw_delta")
    x = a("L0_attn_x").reshape(L, D)

    def heads(w, rows):
        return np.ascontiguousarray(w.reshape(rows, NH, DH).transpose(2, 1, 0))

    arrays = {
        "cst": consts,
        "tab": tables,
        "raw": np.concatenate([np.tile(raw, (P, 1)), np.tile(raw, P // HALF)[:, None]], 1),
        "xT": np.ascontiguousarray(x.T),
        "x": np.ascontiguousarray(x.reshape(NT, P, D).transpose(1, 0, 2)),
        "idx_wk": a("L0_attn_idx_wk"),
        "idx_wq": a("L0_attn_idx_wq"),
        "idx_w": np.tile(a("L0_attn_idx_w"), (P, 1)),
        "W_kr": a("L0_attn_W_kr"),
        "W_dkv": a("L0_attn_W_dkv"),
        "W_dq": a("L0_attn_W_dq"),
        "W_qr": a("L0_attn_W_qr"),
        "W_uqT": heads(a("L0_attn_W_uq"), CQ),
        "W_ukT": heads(a("L0_attn_W_uk"), CKV),
        "W_uvT": heads(a("L0_attn_W_uv"), CKV),
        "W_out": np.ascontiguousarray(a("L0_attn_W_out").reshape(NH, DH, D).transpose(1, 0, 2)),
        "w_router": a("L0_ffn_w_router"),
        "w_gate": a("L0_ffn_w_gate"),
        "w_up": a("L0_ffn_w_up"),
        "w_down": a("L0_ffn_w_down"),
        "gate_W": np.ascontiguousarray(a("L1_attn_gate_W").T),
        "value_W": np.ascontiguousarray(a("L1_attn_value_W").T),
        "gamma": np.tile(a("L1_attn_gamma"), (P, 1)),
        "beta": np.tile(a("L1_attn_beta"), (P, 1)),
        "Wg": np.ascontiguousarray(a("L1_ffn_Wg").T),
        "W1": np.ascontiguousarray(a("L1_ffn_W1").transpose(1, 0, 2)),
        "W3": np.ascontiguousarray(a("L1_ffn_W3").transpose(1, 0, 2)),
        "W2": np.ascontiguousarray(a("L1_ffn_W2").transpose(1, 0, 2)),
        "Ws1": np.ascontiguousarray(a("L1_ffn_Ws1").reshape(D, 2, H1)),
        "Ws3": np.ascontiguousarray(a("L1_ffn_Ws3").reshape(D, 2, H1)),
        "Ws2": np.ascontiguousarray(a("L1_ffn_Ws2").reshape(2, H1, D).transpose(1, 0, 2)),
    }
    nc = _bacc.Bacc("TRN2", target_bir_lowering=False, num_devices=1)
    sent = {f"in_{n}": np.ascontiguousarray(v) for n, v in arrays.items()}
    dram = {n: nc.dram_tensor(f"in_{n}", v.shape, F32, kind="ExternalInput").ap() for n, v in arrays.items()}
    out = nc.dram_tensor("out_0", (L, D), F32, kind="ExternalOutput").ap()
    program(nc, dram, out)
    r = _run(nc, [sent], core_ids=[0])
    return r.results[0]["out_0"].reshape(1, L, D)
```

```python
from contextlib import ExitStack

import numpy as np

import concourse.bass as bass
from concourse import mybir

F32 = mybir.dt.float32
U32 = mybir.dt.uint32
ALU = mybir.AluOpType
ACT = mybir.ActivationFunctionType

P = 128
L = 2048
D = 128
NT = L // P
CKV, CQ = 32, 64
NH, DH, DR = 8, 64, 32
HALF = DR // 2
NIH = 4
KTS, LW = 96, 64
NSEL = KTS - LW
SCALE = (DH + DR) ** -0.5
ROPE_BASE = 10000.0
QB = 16
NB = P // QB
GPB = 4
NG = NB * GPB
WIN = QB + LW
NS = P + WIN
PAD = LW
BIG = 1.0e30
LOW = -3.0e38
E0, C0 = 32, 80
NSLOT = E0 * C0
EG = 4
NEG = E0 // EG
SHIFTS = (0, -32, -16, -4, -1, 1, 4, 16, 32)
NGATE = len(SHIFTS)
ROLL = 32
E1, H1 = 8, 88
NHC = E1 + 2
CH = 512
NCH = L // CH
TPC = CH // P
LN_EPS = 1e-5
SUM_EPS = 1e-20


def keys_of(t):
    return P if t == 0 else P * t + LW


def chunks_of(t):
    return -(-keys_of(t) // CH)


def chunk_base(t):
    return sum(chunks_of(u) for u in range(t))


N0, N1 = -2 * NB, NT * NB + 2 * NB
INDEX_END = NB * (NT - 2) - 2
START_ROOM = 0.6
TOP_STEPS = 12


def index_plan():
    items = [("sum", 0, c) for c in range(chunks_of(0))]
    for t in range(NT):
        nxt = chunks_of(t + 1) if t + 1 < NT else 0
        at = [TOP_STEPS if t == 0 else (c + 1) * TOP_STEPS // (nxt + 1) for c in range(nxt)]
        for k in range(TOP_STEPS):
            items.append(("top", t, k))
            items += [("sum", t + 1, c) for c in range(nxt) if at[c] == k + 1]

    def cost(item):
        kind, t, i = item
        if kind == "sum":
            return 3 * 1.16 * min(CH, keys_of(t) - CH * i) / 1000 + 0.2
        return (1.04 * keys_of(t) / 1000 + 0.07) if i < TOP_STEPS - 1 else 0.1

    other = (0.0, 0.9, 1.9, 1.3, 0.0, 0.6, 0.0, 0.8)

    def lay(level):
        plan, done_at, top_end, n, left = {}, {}, {}, N0 + 2, 0.0
        for item in items:
            m = chunk_base(item[1]) + item[2]
            first = N0
            if item[0] == "sum" and m >= 1:
                first = done_at[m - 1] + 2 if n >= -6 else done_at[m - 2] + 2 if m >= 2 else N0
            if item[0] == "sum" and item[2] == 0 and item[1] >= 2:
                first = max(first, top_end[item[1] - 2] + 3)
            while left <= 0 or n < first:
                n += 1
                if n < 0:
                    left = min(left, 0.0) + START_ROOM
                else:
                    left = min(left, 0.0) + max(0.0, level - (0.7 if n >= 3 else 0.0) - other[n % NB])
            plan.setdefault(n, []).append(item)
            if item[0] == "sum":
                done_at[m] = n
            else:
                top_end[item[1]] = n
            left -= cost(item)
        return plan, done_at, n

    level = 2.0
    while lay(level)[2] > INDEX_END:
        level += 0.02
    plan, done_at, _ = lay(level)
    pairs = {}
    for t in range(NT):
        for c in range(chunks_of(t)):
            m = chunk_base(t) + c
            last = done_at[m] - 2
            first = max(last - 1, done_at[m - 2] if m >= 2 else N0, done_at[m - 1] - 2 if m >= 1 else N0)
            for u, n in ((0, first), (1, last)):
                pairs.setdefault(n, []).append((t, 2 * c + u))
    for t in range(1, NT):
        ready = max(n for n, its in plan.items() if ("top", t, TOP_STEPS - 1) in its)
        assert ready < NB * (t - 1) + 3 or t <= 2
    return pairs, plan


C_ID = 0
C_MASK = C_ID + P
C_MASK0 = C_MASK + NS
C_IM = C_MASK0 + NS
C_IM0 = C_IM + P
C_TRI = C_IM0 + P
C_IOTA = C_TRI + P
C_RC = C_IOTA + E0
C_RS = C_RC + HALF
C_ONES = C_RS + HALF
C_EPS = C_ONES + P
C_PI = C_EPS + 1
C_N = C_PI + 1


def shape_constants():
    c = np.zeros((P, C_N), np.float32)
    c[:, C_ID:C_ID + P] = np.eye(P)
    row = np.arange(P)
    ql = row // NH
    col = np.arange(P)
    sel = (ql[:, None] % GPB) == (col[None, :] // NSEL)
    w = np.arange(WIN)
    local = (w[None, :] >= ql[:, None] + 1) & (w[None, :] <= ql[:, None] + LW)
    first = np.broadcast_to(w[None, :] < LW, (P, WIN))
    for base, loc in ((C_MASK, local), (C_MASK0, first)):
        c[:, base:base + P] = np.where(sel, 0, BIG)
        c[:, base + P:base + NS] = np.where(loc, 0, BIG)
    qi = 4 * (row % 32) + row // 32
    c[:, C_IM:C_IM + P] = np.where(col[None, :] <= qi[:, None], 0, -BIG)
    b = np.maximum(qi - (LW - 1), 0)[:, None]
    c[:, C_IM0:C_IM0 + P] = np.where(col[None, :] < b, 0, np.where(col[None, :] < b + LW, LOW, -BIG))
    c[:, C_TRI:C_TRI + P] = row[:, None] <= row[None, :]
    c[:, C_IOTA:C_IOTA + E0] = np.arange(E0)
    theta = (np.float32(1.0) / np.float32(ROPE_BASE) ** (np.float32(2.0) * np.arange(HALF, dtype=np.float32)
                                                        / np.float32(DR))).astype(np.float32)
    rank = ((LW + row % NSEL).astype(np.float32)[:, None] * theta[None, :]).astype(np.float64)
    c[:, C_RC:C_RC + HALF] = np.cos(rank)
    c[:, C_RS:C_RS + HALF] = np.sin(rank)
    c[:, C_ONES:C_ONES + P] = 1.0
    c[:, C_EPS] = LN_EPS
    c[:, C_PI] = np.pi
    q = np.arange(L)
    tq = (q.astype(np.float32)[:, None] * theta[None, :]).astype(np.float64)
    tk = q[:, None] * theta[None, :].astype(np.float64)
    tl = tq + np.maximum(q - (LW - 1), 0)[:, None] * theta[None, :].astype(np.float64)
    tab = np.stack([np.cos(tq), np.sin(tq), np.cos(tl), np.sin(tl), np.cos(tk), np.sin(tk)], 1)
    tab = tab.reshape(NT, P, 6, HALF).transpose(1, 2, 0, 3)
    return c, np.ascontiguousarray(tab.reshape(P, 6 * NT * HALF)).astype(np.float32)


def program(nc, dram, out):
    with ExitStack() as ctx:
        def sb(name, shape, dt=F32):
            return ctx.enter_context(nc.sbuf_tensor(name, shape, dt))

        def sem(name):
            return ctx.enter_context(nc.semaphore(name))

        key_rows = nc.dram_tensor("key_rows", (L, P), F32, kind="Internal").ap()
        val_rows_h = nc.dram_tensor("val_rows", (PAD + L, CKV), F32, kind="Internal")
        val_rows = val_rows_h.ap()
        xslots = nc.dram_tensor("xslots", (NSLOT, D), F32, kind="Internal").ap()
        yslots = nc.dram_tensor("yslots", (NSLOT, D), F32, kind="Internal").ap()

        cst = sb("cst", [P, C_N])
        ident = cst[:, C_ID:C_ID + P]
        ones = cst[:, C_ONES:C_ONES + P]
        tab = sb("tab", [P, 6, NT, HALF])
        rot = sb("rot", [P, 6, NT, HALF])
        rtmp = sb("rtmp", [P, 2, NT, HALF])
        rank_tab = sb("rank_tab", [P, 2, 2, HALF])
        raw = sb("raw", [P, HALF + 1])
        dlt = sb("dlt", [P, 8, HALF + 1])
        xT = sb("xT", [P, L])
        xr = sb("xr", [P, NT, D])
        w_idxq = sb("w_idxq", [P, 2 * P])
        w_idxk = sb("w_idxk", [P, P])
        w_kv = sb("w_kv", [P, DR + CKV])
        w_dq = sb("w_dq", [P, CQ])
        w_uqT = sb("w_uqT", [DH, NH, CQ])
        w_ukT = sb("w_ukT", [DH, NH, CKV])
        w_uvT = sb("w_uvT", [DH, NH, CKV])
        w_out = sb("w_out", [DH, NH, D])
        w_q = sb("w_q", [CQ, 2 * NH * DR])
        w_vo = sb("w_vo", [CKV, NH, D])
        w_i = sb("w_i", [P, NIH])
        w_router = sb("w_router", [P, E0])
        kiT = sb("kiT", [P, L])
        qiT = sb("qiT", [P, 2, L])
        cq_region = sb("cq_region", [P, L])
        cqT = cq_region[0:CQ, :]
        klocT = sb("klocT", [P, PAD + L])
        kmu = sb("kmu", [P, NT, DR])
        G = sb("G", [P, 2, NG, P])
        grow = G[:, 1, 0:NT, :]
        lrow = G[:, 1, NT:2 * NT, :]
        idxf = sb("idxf", [P, NSEL], U32)
        idx = sb("idx", [P, NT, NG], U32)
        R = sb("R", [P, 2, NIH, CH])
        SC = sb("SC", [P, 2, L])
        top = sb("top", [P, 4, 8])
        QF = sb("QF", [P, NH, P])
        qe = sb("qe", [P, NH, 2, HALF])
        qmu = sb("qmu", [P, NH, 2, HALF])
        qt = sb("qt", [P, 4, NH * 2, HALF])
        Q = sb("Q", [P, 2, P, NH])
        KT = sb("KT", [P, 2, GPB, P])
        S = sb("S", [P, 2, NS])
        PR = sb("PR", [P, 4, 2 * P])
        PT = sb("PT", [P, 2, 2 * P])
        V = sb("V", [WIN, 2, NB, CKV])
        ot_region = sb("ot_region", [P, 2 * NB * QB * NH])
        OT = ot_region[0:CKV, :].rearrange("p (a b q h) -> p a b q h", a=2, b=NB, q=QB)
        nmin = sb("nmin", [P, 2])
        psumr = sb("psumr", [P, 4])
        rinv = sb("rinv", [P, 2])
        xa = sb("xa", [P, D])
        stats = sb("stats", [P, TPC, 6])
        mv = sb("mv", [P, TPC, 2])
        lnv = sb("lnv", [P, 2, TPC])
        x1 = sb("x1", [P, 4, D])
        x1T = sb("x1T", [P, P])
        r8 = sb("r8", [P, 8])
        r8i = sb("r8i", [P, 8], U32)
        rex = sb("rex", [P, E0])
        rlog = sb("rlog", [P, E0])
        rsm = sb("rsm", [P, 8])
        onehot = sb("onehot", [P, E0])
        ohsum = sb("ohsum", [P, E0])
        rjunk = sb("rjunk", [P, E0])
        gm = sb("gm", [P, NT])
        slot_in = sb("slot_in", [P, NT], U32)
        slot_out = sb("slot_out", [P, NT], U32)
        zrow = sb("zrow", [P, 5 * P])

        w_value = kiT[:, 0:D]
        w_gates = kiT[:, D:D * (1 + NGATE)]
        w_ex = qiT[:, :, :].rearrange("p a n -> p (a n)")[:, 0:2 * 3 * EG * D].rearrange(
            "p (a i e n) -> p a i e n", a=2, i=3, e=EG)
        w_up = xT[:, 0:2 * NHC * H1].rearrange("p (a e n) -> p a e n", a=2, e=NHC)
        w_down = cq_region[0:H1, 0:NHC * D].rearrange("p (e n) -> p e n", e=NHC)
        gamma = cq_region[:, NHC * D:(NHC + 1) * D]
        beta = cq_region[:, (NHC + 1) * D:(NHC + 2) * D]
        w_g8 = cq_region[:, (NHC + 2) * D:(NHC + 2) * D + E1]

        psK = ctx.enter_context(nc.psum_tensor("psK", [P, CH], F32))
        psX = ctx.enter_context(nc.psum_tensor("psX", [P, CH], F32))
        psS = [ctx.enter_context(nc.psum_tensor(f"psS{i}", [P, CH], F32)) for i in range(2)]
        psP = ctx.enter_context(nc.psum_tensor("psP", [P, CH], F32))
        psI = [ctx.enter_context(nc.psum_tensor(f"psI{i}", [P, CH], F32)) for i in range(2)]
        psM = ctx.enter_context(nc.psum_tensor("psM", [P, CH], F32))
        PX = psX[:, 0:P]

        names = """ld_cst ld_x ld_w ld_raw ld_late zeroed z_ready zslots kv_mm
            w_mm w_cp kproj kproj_cp lat_row mu_row key_l mu lrot kr_out val_out g_rot lT lT_cp rope rope_a
            i_mm i_relu i_first comb im topk idx_ready q_mm q_a q_e q_chain qf_a q_t q_cp
            k_t k_ev s_mm s_min p_exp p_t p_cp pv orec p_nrm o_cp v_ld
            y_mm y_add bn ln_a x1_n x1d x1_t x1_cp lg_mm lg_e rt_a rt cum_mm lg_cp rte plc slots_ready ld_l1""".split()
        s = {n: sem("s_" + n) for n in names}
        s_we = [sem(f"s_we{i}") for i in range(2)]
        s_sct = [sem(f"s_sct{i}") for i in range(4)]
        s_g = [[sem(f"s_g{i}_{b}") for b in range(NB)] for i in range(2)]

        CHUNKS = L // CH

        index_pairs, index_steps = index_plan()

        def load_experts(sp, k):
            for i, w in enumerate(("w_gate", "w_up", "w_down")):
                sp.dma_start(w_ex[:, k % 2, i, :, :],
                             dram[w][EG * k:EG * (k + 1)].rearrange("e h f -> h e f")).then_inc(s_we[k % 2], 16)

        def scatter(pool, t):
            pool.wait_ge(s["slots_ready"], t + 1)
            pool.indirect_dma_start(
                xslots, bass.IndirectOffsetOnAxis(ap=slot_in[:, t:t + 1], axis=0), x1[:, t % 4, :], None,
                bounds_check=NSLOT - 1, oob_is_err=False).then_inc(s_sct[t % 4], 16)

        with nc.Block() as block:
            @block.sync
            def _(sp):
                sp.dma_start(cst[:, :], dram["cst"]).then_inc(s["ld_cst"], 16)
                sp.dma_start(raw[:, :], dram["raw"]).then_inc(s["ld_raw"], 16)
                sp.dma_start(w_idxk[:, 0:DH], dram["idx_wk"]).then_inc(s["ld_w"], 16)
                sp.dma_start(w_idxk[:, DH:P], dram["idx_wk"]).then_inc(s["ld_w"], 16)
                sp.dma_start(w_idxq[:, :], dram["idx_wq"]).then_inc(s["ld_w"], 16)
                sp.dma_start(xT[:, :], dram["xT"]).then_inc(s["ld_x"], 16)
                sp.dma_start(w_kv[:, 0:DR], dram["W_kr"]).then_inc(s["ld_w"], 16)
                sp.dma_start(w_kv[:, DR:DR + CKV], dram["W_dkv"]).then_inc(s["ld_w"], 16)
                sp.dma_start(w_dq[:, :], dram["W_dq"]).then_inc(s["ld_w"], 16)
                sp.dma_start(w_i[:, :], dram["idx_w"]).then_inc(s["ld_w"], 16)
                sp.dma_start(tab[:, :, :, :], dram["tab"]).then_inc(s["ld_late"], 16)
                sp.dma_start(w_uqT[:, :, :], dram["W_uqT"]).then_inc(s["ld_late"], 16)
                sp.dma_start(w_ukT[:, :, :], dram["W_ukT"]).then_inc(s["ld_late"], 16)
                sp.dma_start(w_uvT[:, :, :], dram["W_uvT"]).then_inc(s["ld_late"], 16)
                sp.dma_start(w_out[:, :, :], dram["W_out"]).then_inc(s["ld_late"], 16)
                sp.dma_start(w_q[:, NH * CKV:], dram["W_qr"]).then_inc(s["ld_late"], 16)
                sp.dma_start(w_router[:, :], dram["w_router"]).then_inc(s["ld_late"], 16)
                sp.dma_start(xr[:, :, :], dram["x"]).then_inc(s["ld_late"], 16)
                sp.wait_ge(s["z_ready"], 1)
                sp.dma_start(val_rows[0:PAD, :], zrow[0:PAD, 0:CKV]).then_inc(s["val_out"], 16)
                for i in range(4):
                    n = NSLOT // 4
                    sp.dma_start(xslots[n * i:n * (i + 1), :].rearrange("(p r) d -> p (r d)", p=P),
                                 zrow[:, :]).then_inc(s["zslots"], 16)
                sp.wait_ge(s["mu_row"], 2)
                sp.wait_ge(s["zeroed"], 5)
                sp.wait_ge(s["lat_row"], 4)
                sp.dma_start(key_rows.rearrange("(t p) d -> p t d", p=P), grow).then_inc(s["kr_out"], 16)
                sp.dma_start(val_rows[PAD:, :].rearrange("(t p) d -> p t d", p=P),
                             grow[:, :, 3 * DR:]).then_inc(s["val_out"], 16)
                sp.wait_ge(s["val_out"], 32)
                for t in range(NT):
                    if t >= 2:
                        sp.wait_ge(s["pv"], NB * (t - 1))
                    if t == 0:
                        for b in range(4):
                            sp.dma_start(V[:, 0, b, :], val_rows[PAD:PAD + WIN, :]).then_inc(s["v_ld"], 16)
                        src = bass.AP(val_rows_h, 4 * QB * CKV, [[CKV, WIN], [QB * CKV, NB - 4], [1, CKV]])
                        sp.dma_start(V[:, 0, 4:, :], src).then_inc(s["v_ld"], 16)
                    else:
                        src = bass.AP(val_rows_h, P * t * CKV, [[CKV, WIN], [QB * CKV, NB], [1, CKV]])
                        sp.wait_ge(s["v_ld"], 16 * (4 + t))
                        sp.dma_start(V[:, t % 2, :, :], src).then_inc(s["v_ld"], 16)
                sp.wait_ge(s["i_relu"], 4 * chunk_base(NT))
                sp.dma_start(w_value, dram["value_W"]).then_inc(s["ld_l1"], 16)
                sp.dma_start(w_gates, dram["gate_W"]).then_inc(s["ld_l1"], 16)
                sp.dma_start(w_up[:, 0, 0:E1, :], dram["W1"]).then_inc(s["ld_l1"], 16)
                sp.dma_start(w_up[:, 1, 0:E1, :], dram["W3"]).then_inc(s["ld_l1"], 16)
                sp.dma_start(w_up[:, 0, E1:, :], dram["Ws1"]).then_inc(s["ld_l1"], 16)
                sp.dma_start(w_up[:, 1, E1:, :], dram["Ws3"]).then_inc(s["ld_l1"], 16)
                for k in range(2):
                    load_experts(sp, k)
                sp.wait_ge(s["q_mm"], NT)
                sp.dma_start(w_down[:, 0:E1, :], dram["W2"]).then_inc(s["ld_l1"], 16)
                sp.dma_start(w_down[:, E1:, :], dram["Ws2"]).then_inc(s["ld_l1"], 16)
                sp.dma_start(gamma, dram["gamma"]).then_inc(s["ld_l1"], 16)
                sp.dma_start(beta, dram["beta"]).then_inc(s["ld_l1"], 16)
                sp.dma_start(w_g8, dram["Wg"]).then_inc(s["ld_l1"], 16)
                sp.wait_ge(s["ld_l1"], 16 * 11)
                for k in range(2):
                    sp.wait_ge(s_we[k], 16 * 3)

            @block.gpsimd
            def _(pool):
                pool.memset(zrow[:, :], 0.0).then_inc(s["z_ready"], 1)
                pool.memset(ohsum[:, :], 0.0).then_inc(s["zeroed"], 1)
                pool.memset(klocT[:, 0:PAD], 0.0).then_inc(s["zeroed"], 1)
                pool.memset(PR[:, :, NS:], 0.0).then_inc(s["zeroed"], 1)
                pool.memset(lrow[:, :, 0:2 * DR], 0.0).then_inc(s["zeroed"], 1)
                pool.memset(grow[:, :, 2 * DR:3 * DR], 0.0).then_inc(s["zeroed"], 1)
                pool.wait_ge(s["kr_out"], 16)
                for t in range(NT):
                    pool.wait_ge(s["idx_ready"], t + 1)
                    if t == 1:
                        pool.wait_ge(s["lT"], NT)
                        pool.wait_ge(s["val_out"], 32)
                    for g in range(NG):
                        b = g // GPB
                        if t >= 2 and g % GPB == 0:
                            pool.wait_ge(s["pv"], NB * (t - 2) + b + 1)
                        pool.indirect_dma_start(
                            G[:, t % 2, g, :], None, key_rows,
                            bass.IndirectOffsetOnAxis(ap=idx[:, t, g:g + 1], axis=0),
                        ).then_inc(s_g[t % 2][b], 16)
                    if t == 4:
                        pool.wait_ge(s["zslots"], 64)
                    if t >= 4:
                        scatter(pool, t - 4)
                for t in range(NT - 4, NT):
                    scatter(pool, t)
                for i in range(4):
                    pool.wait_ge(s_sct[i], 16 * NT // 4)

            @block.tensor
            def _(pe):
                pe.wait_ge(s["ld_w"], 16 * 7)
                pe.wait_ge(s["ld_x"], 16)
                banks = [psI[0], psI[1], psK, psX]
                n = 0
                for c in range(CHUNKS):
                    for lhs, rows in ((w_idxk[:, :], P), (w_idxq[:, 0:P], P), (w_idxq[:, P:2 * P], P),
                                      (w_dq[:, :], CQ)):
                        if n >= 4:
                            pe.wait_ge(s["kproj_cp"], n - 3)
                        pe.matmul(banks[n % 4][0:rows, :], lhs, xT[:, CH * c:CH * (c + 1)],
                                  start=True, stop=True).then_inc(s["kproj"], 1)
                        n += 1
                for h in range(2):
                    for i in range(8):
                        t = 8 * h + i
                        mm = pe.matmul([psS[0], psM][h][:, 64 * i:64 * i + 64], xT[:, P * t:P * (t + 1)], w_kv[:, :],
                                       start=True, stop=True, skip_group_check=True)
                    mm.then_inc(s["kv_mm"], 1)
                pe.wait_ge(s["ld_late"], 16 * 8)
                for h in range(NH):
                    mm = pe.matmul(psP[0:CQ, CKV * h:CKV * (h + 1)], w_uqT[:, h, :], w_ukT[:, h, :],
                                   start=True, stop=True, skip_group_check=True)
                mm.then_inc(s["w_mm"], 1)
                for j in range(2):
                    pe.wait_ge(s["w_cp"], 1 + j)
                    for h in range(4):
                        mm = pe.matmul(psP[0:CKV, D * h:D * (h + 1)], w_uvT[:, 4 * j + h, :], w_out[:, 4 * j + h, :],
                                       start=True, stop=True, skip_group_check=True)
                    mm.then_inc(s["w_mm"], 1)

                def index_pair(t, u):
                    c, pair = u // 2, u % 2
                    w = min(CH, keys_of(t) - CH * c)
                    m = 2 * chunk_base(t) + u
                    if m == 0:
                        pe.wait_ge(s["kproj_cp"], 4 * CHUNKS)
                    else:
                        pe.wait_ge(s["i_relu"], 2 * m)
                    for i in range(2):
                        lhs = qiT[64 * i:64 * i + 64, pair, P * t:P * (t + 1)]
                        pe.matmul(psI[i][:, 0:w], lhs, kiT[64 * i:64 * i + 64, CH * c:CH * c + w],
                                  start=True, stop=True).then_inc(s["i_mm"], 1)

                def q_project(t):
                    if t == 0:
                        pe.wait_ge(s["w_cp"], 3)
                        pe.wait_ge(s["kproj_cp"], 4 * CHUNKS)
                        pe.wait_ge(s["lat_row"], 4)
                        pe.wait_ge(s["mu"], 4)
                    if t >= 1:
                        pe.wait_ge(s["q_cp"], 2 * t)
                    pe.matmul(psM[:, :], cqT[:, P * t:P * (t + 1)], w_q[:, :], start=True,
                              stop=True).then_inc(s["q_mm"], 1)

                def q_transpose(t, j):
                    if j == 0:
                        pe.wait_ge(s["q_chain"], 10 * (t + 1))
                        pe.wait_ge(s["qf_a"], 3 * (t + 1))
                    else:
                        pe.wait_ge(s["q_cp"], 2 * t + 1)
                    for h in range(4):
                        mm = pe.transpose(psM[:, P * h:P * (h + 1)], QF[:, 4 * j + h, :], ident)
                    mm.then_inc(s["q_t"], 1)

                def front(n):
                    t, b = divmod(n, NB)
                    pe.wait_ge(s["g_rot"], n + 1)
                    if n >= 1:
                        pe.wait_ge(s["k_ev"], n)
                    else:
                        pe.wait_ge(s["lT_cp"], NT // 4)
                    for j in range(GPB):
                        mm = pe.transpose(psK[:, P * j:P * (j + 1)], G[:, t % 2, GPB * b + j, :], ident)
                    mm.then_inc(s["k_t"], 1)

                def scores(n):
                    t, b = divmod(n, NB)
                    pe.wait_ge(s["k_ev"], n + 1)
                    pe.wait_ge(s["q_cp"], 2 * t + 2)
                    if n >= 2:
                        pe.wait_ge(s["s_min"], n - 1)
                    ps = psS[n % 2]
                    qb = Q[:, t % 2, QB * b:QB * (b + 1), :].rearrange("p q h -> p (q h)")
                    for j in range(GPB):
                        pe.matmul(ps[32 * j:32 * j + 32, 0:P], qb[:, 32 * j:32 * j + 32], KT[:, n % 2, j, :],
                                  start=True, stop=True, skip_group_check=True)
                    w0 = PAD if t == 0 and b < 4 else P * t + QB * b
                    pe.matmul(ps[:, P:NS], qb, klocT[:, w0:w0 + WIN],
                              start=True, stop=True, skip_group_check=True).then_inc(s["s_mm"], 1)

                def p_transpose(n):
                    pe.wait_ge(s["p_nrm"], n + 1)
                    if n >= 1:
                        pe.wait_ge(s["p_cp"], n)
                    if n >= 2:
                        pe.wait_ge(s["o_cp"], n - 1)
                    for i in range(2):
                        mm = pe.transpose(psP[:, P * i:P * (i + 1)], PR[:, n % 4, P * i:P * (i + 1)], ident)
                    mm.then_inc(s["p_t"], 1)

                def weighted(n):
                    t, b = divmod(n, NB)
                    pe.wait_ge(s["p_cp"], n + 1)
                    pe.wait_ge(s["v_ld"], 16 * (5 + t))
                    if n >= 1:
                        pe.wait_ge(s["o_cp"], n)
                    o = psP[0:CKV, 2 * P:3 * P]
                    pe.matmul(o, V[:, t % 2, b, :], PT[0:WIN, n % 2, P:2 * P], start=True, stop=False,
                              skip_group_check=True)
                    for j in range(GPB):
                        mm = pe.matmul(o[:, 32 * j:32 * j + 32], G[:, t % 2, GPB * b + j, 3 * DR:],
                                       PT[:, n % 2, 32 * j:32 * j + 32], start=False, stop=(j == GPB - 1),
                                       skip_group_check=True)
                    mm.then_inc(s["pv"], 1)

                def out_project(t):
                    pe.wait_ge(s["o_cp"], NB * (t + 1))
                    if t >= 1:
                        pe.wait_ge(s["rte"], t)
                    for h in range(NH):
                        mm = pe.matmul(PX, OT[:, t % 2, :, :, h].rearrange("p b q -> p (b q)"), w_vo[:, h, :],
                                       start=(h == 0), stop=(h == NH - 1), skip_group_check=True)
                    mm.then_inc(s["y_mm"], 1)

                def x1_transpose(t):
                    pe.wait_ge(s["x1_n"], t + 1)
                    pe.transpose(PX, x1[:, t % 4, :], ident).then_inc(s["x1_t"], 1)

                def router(t):
                    pe.wait_ge(s["x1_cp"], t + 1)
                    pe.matmul(PX[:, 0:E0], x1T[:, :], w_router[:, :], start=True, stop=True,
                              skip_group_check=True).then_inc(s["lg_mm"], 1)

                def cumulate(t):
                    pe.wait_ge(s["rt"], 5 * t + 4)
                    pe.matmul(PX[:, E0:2 * E0], cst[:, C_TRI:C_TRI + P], onehot[:, :], start=True, stop=False,
                              skip_group_check=True)
                    pe.matmul(PX[:, E0:2 * E0], ones, ohsum[:, :], start=False, stop=True,
                              skip_group_check=True).then_inc(s["cum_mm"], 1)

                for n in range(N0, N1):
                    st, b = divmod(n, NB)
                    if 0 <= n - 7 < NT * NB:
                        p_transpose(n - 7)
                    if 0 <= n - 8 < NT * NB:
                        weighted(n - 8)
                    if 0 <= n < NT * NB:
                        front(n)
                    if 0 <= n - 2 < NT * NB:
                        scores(n - 2)
                    if n == -NB:
                        for i in range(NT // 4):
                            if i == 0:
                                pe.wait_ge(s["lrot"], 2)
                                pe.wait_ge(s["lat_row"], 4)
                                pe.wait_ge(s["zeroed"], 5)
                            if i >= 2:
                                pe.wait_ge(s["lT_cp"], i - 1)
                            for j in range(4):
                                pe.transpose([psK, psP][i % 2][:, P * j:P * (j + 1)], lrow[:, 4 * i + j, :],
                                             ident).then_inc(s["lT"], 1)
                    for t, u in index_pairs.get(n, ()):
                        index_pair(t, u)
                    if 0 <= st + 1 < NT:
                        if b == 4:
                            q_transpose(st + 1, 0)
                        if b == 5:
                            q_transpose(st + 1, 1)
                    if 0 <= st + 2 < NT and b == 7:
                        q_project(st + 2)
                    if 0 <= st - 2 < NT:
                        if b == 0:
                            out_project(st - 2)
                        if b == 3:
                            x1_transpose(st - 2)
                        if b == 4:
                            router(st - 2)
                        if b == 6:
                            cumulate(st - 2)

            @block.scalar
            def _(act):
                act.wait_ge(s["ld_raw"], 16)
                act.activation(dlt[:, 0, :], raw[:, :], ACT.Exp, scale=-1.0).then_inc(s["rope_a"], 1)
                act.wait_ge(s["rope"], 3)
                act.activation(dlt[:, 3, :], dlt[:, 2, :], ACT.Sin).then_inc(s["rope_a"], 1)
                act.activation(dlt[:, 4, :], dlt[:, 2, :], ACT.Sin, scale=0.5).then_inc(s["rope_a"], 1)
                act.preload_act_table_set("natural_log_exp_and_others")
                n = 0
                banks = [psI[0], psI[1], psK, psX]
                for c in range(CHUNKS):
                    for dst, rows in ((kiT[:, :], P), (qiT[:, 0, :], P), (qiT[:, 1, :], P), (cqT[:, :], CQ)):
                        act.wait_ge(s["kproj"], n + 1)
                        to, src = dst[:, CH * c:CH * (c + 1)], banks[n % 4][0:rows, :]
                        if n % 4 in (1, 2):
                            to = to.rearrange("p (t a g) -> p t a g", t=TPC, a=GPB)
                            src = src.rearrange("p (t g a) -> p t a g", t=TPC, a=GPB)
                        act.activation(to, src, ACT.Copy).then_inc(s["kproj_cp"], 1)
                        n += 1
                act.wait_ge(s["mu"], 2)
                for h in range(2):
                    src = [psS[0], psM][h][:, :].rearrange("p (t d) -> p t d", d=64)[:, :, DR:]
                    for dst in (grow, lrow):
                        act.activation(dst[:, 8 * h:8 * h + 8, 3 * DR:], src, ACT.Copy).then_inc(s["lat_row"], 1)
                for h in range(2):
                    act.wait_ge(s["mu"], h + 1)
                    m = kmu[:, 8 * h:8 * h + 8, :]
                    act.activation(m, m, ACT.Exp).then_inc(s["key_l"], 1)
                    act.wait_ge(s["key_l"], 2 * h + 1)
                    act.activation(m, m, ACT.Ln, bias=1.0).then_inc(s["key_l"], 1)
                act.wait_ge(s["w_mm"], 1)
                act.activation(w_q[:, 0:NH * CKV], psP[0:CQ, 0:NH * CKV], ACT.Copy).then_inc(s["w_cp"], 1)
                for j in range(2):
                    act.wait_ge(s["w_mm"], 2 + j)
                    act.activation(w_vo[:, 4 * j:4 * j + 4, :].rearrange("p h d -> p (h d)"), psP[0:CKV, :],
                                   ACT.Copy).then_inc(s["w_cp"], 1)

                def relu_pair(t, u):
                    c, pair = u // 2, u % 2
                    w = min(CH, keys_of(t) - CH * c)
                    m = 2 * chunk_base(t) + u
                    if m // 2 >= 2:
                        act.wait_ge(s["comb"], 3 * (m // 2 - 1))
                    for i in range(2):
                        act.wait_ge(s["i_mm"], 2 * m + i + 1)
                        act.activation(R[:, (m // 2) % 2, 2 * pair + i, 0:w], psI[i][:, 0:w],
                                       ACT.Relu).then_inc(s["i_relu"], 1)
                    if pair == 0:
                        if c == 0 and t >= 2:
                            act.wait_ge(s["topk"], TOP_STEPS * (t - 1))
                        act.wait_ge(s["i_relu"], 2 * m + 1)
                        act.activation(SC[:, t % 2, CH * c:CH * c + w], R[:, (m // 2) % 2, 0, 0:w], ACT.Copy,
                                       scale=w_i[:, 0:1]).then_inc(s["i_first"], 1)

                def q_softplus(t):
                    act.wait_ge(s["q_chain"], 10 * t + 1)
                    if t >= 1:
                        act.wait_ge(s["q_t"], 2 * t)
                    act.activation(QF[:, :, 3 * DR:], psM[:, 0:NH * CKV].rearrange("p (h d) -> p h d", h=NH),
                                   ACT.Copy, scale=-SCALE).then_inc(s["qf_a"], 1)
                    act.activation(qe[:, :, :, :], qe[:, :, :, :], ACT.Exp).then_inc(s["q_e"], 1)
                    act.wait_ge(s["q_e"], 2 * t + 1)
                    act.activation(qe[:, :, :, :], qe[:, :, :, :], ACT.Ln, bias=1.0).then_inc(s["q_e"], 1)

                def q_copies(t):
                    act.wait_ge(s["q_chain"], 10 * t + 6)
                    act.activation(QF[:, :, DR:DR + HALF], QF[:, :, HALF:DR], ACT.Copy).then_inc(s["qf_a"], 1)
                    act.activation(QF[:, :, DR + HALF:2 * DR], QF[:, :, 0:HALF], ACT.Copy,
                                   scale=-1.0).then_inc(s["qf_a"], 1)

                def q_evac(t, j):
                    act.wait_ge(s["q_t"], 2 * t + j + 1)
                    if t >= 2 and j == 0:
                        act.wait_ge(s["s_mm"], NB * (t - 1))
                    act.activation(Q[:, t % 2, :, 4 * j:4 * j + 4].rearrange("p q h -> p h q"),
                                   psM[:, :].rearrange("p (h q) -> p h q", h=4), ACT.Copy).then_inc(s["q_cp"], 1)

                def exps(n):
                    act.wait_ge(s["s_min"], n + 1)
                    if n == 0:
                        act.wait_ge(s["zeroed"], 5)
                    if n >= 4:
                        act.wait_ge(s["p_t"], n - 3)
                    act.activation(PR[:, n % 4, 0:NS], S[:, n % 2, :], ACT.Exp, bias=nmin[:, n % 2:n % 2 + 1],
                                   scale=-1.0, accum_out=psumr[:, n % 4:n % 4 + 1]).then_inc(s["p_exp"], 1)

                def p_norm(n):
                    act.wait_ge(s["orec"], n + 1)
                    pr = PR[:, n % 4, 0:NS]
                    act.activation(pr, pr, ACT.Copy, scale=rinv[:, n % 2:n % 2 + 1]).then_inc(s["p_nrm"], 1)

                def k_copy(n):
                    act.wait_ge(s["k_t"], n + 1)
                    if n >= 2:
                        act.wait_ge(s["s_mm"], n - 1)
                    act.activation(KT[:, n % 2, :, :].rearrange("p g i -> p (g i)"), psK[:, :],
                                   ACT.Copy).then_inc(s["k_ev"], 1)

                def p_copy(n):
                    act.wait_ge(s["p_t"], n + 1)
                    if n >= 1:
                        act.wait_ge(s["pv"], n)
                    act.activation(PT[:, n % 2, :], psP[:, 0:2 * P], ACT.Copy).then_inc(s["p_cp"], 1)

                def o_copy(n):
                    t, b = divmod(n, NB)
                    act.wait_ge(s["pv"], n + 1)
                    if b == 0 and t >= 2:
                        act.wait_ge(s["y_mm"], t - 1)
                    act.activation(OT[:, t % 2, b, :, :].rearrange("p q h -> p (q h)"), psP[0:CKV, 2 * P:3 * P],
                                   ACT.Copy).then_inc(s["o_cp"], 1)

                def norm_scale(t):
                    act.wait_ge(s["bn"], 2 * t + 2)
                    act.activation(lnv[:, 0, 0:1], mv[:, 0, 1:2], ACT.Ln,
                                   bias=cst[:, C_EPS:C_EPS + 1]).then_inc(s["ln_a"], 1)
                    act.wait_ge(s["ln_a"], 2 * t + 1)
                    act.activation(lnv[:, 1, 0:1], lnv[:, 0, 0:1], ACT.Exp, scale=-0.5).then_inc(s["ln_a"], 1)

                def x1_copy(t):
                    act.wait_ge(s["x1_n"], t + 1)
                    act.activation(xr[:, t, :], x1[:, t % 4, :], ACT.Copy, scale=2.0).then_inc(s["x1d"], 1)
                    act.wait_ge(s["x1_t"], t + 1)
                    act.activation(x1T[:, :], PX, ACT.Copy).then_inc(s["x1_cp"], 1)

                def gate_exp(t):
                    act.wait_ge(s["rt"], 5 * t + 1)
                    act.activation(rex[:, :], rlog[:, :], ACT.Exp, bias=rsm[:, 0:1],
                                   accum_out=rsm[:, 1:2]).then_inc(s["lg_e"], 1)

                for n in range(N0, N1):
                    st, b = divmod(n, NB)
                    if 0 <= n - 7 < NT * NB:
                        p_copy(n - 7)
                    if 0 <= n - 8 < NT * NB:
                        o_copy(n - 8)
                    for t, u in index_pairs.get(n - 1, ()):
                        relu_pair(t, u)
                    if 0 <= n - 4 < NT * NB:
                        exps(n - 4)
                    if 0 <= n - 6 < NT * NB:
                        p_norm(n - 6)
                    if 0 <= n < NT * NB:
                        k_copy(n)
                    if n == -NB:
                        for i in range(NT // 4):
                            act.wait_ge(s["lT"], 4 * i + 4)
                            act.activation(klocT[:, PAD + CH * i:PAD + CH * (i + 1)], [psK, psP][i % 2][:, :],
                                           ACT.Copy).then_inc(s["lT_cp"], 1)
                    if 0 <= st + 1 < NT:
                        if b == 1:
                            q_softplus(st + 1)
                        if b == 3:
                            q_copies(st + 1)
                        if b == 5:
                            q_evac(st + 1, 0)
                        if b == 6:
                            q_evac(st + 1, 1)
                    if 0 <= st - 2 < NT:
                        if b == 1:
                            norm_scale(st - 2)
                        if b == 4:
                            x1_copy(st - 2)
                        if b == 6:
                            gate_exp(st - 2)

            @block.vector
            def _(dve):
                rope = [0]

                def link(ins):
                    rope[0] += 1
                    ins.then_inc(s["rope"], 1)
                    dve.wait_ge(s["rope"], rope[0])

                dve.wait_ge(s["rope_a"], 1)
                link(dve.tensor_scalar(dlt[:, 0, :], dlt[:, 0, :], 1.0, None, ALU.add))
                link(dve.reciprocal(dlt[:, 1, :], dlt[:, 0, :]))
                link(dve.tensor_scalar(dlt[:, 2, :], dlt[:, 1, :], float(-2 * np.pi), float(np.pi),
                                       ALU.mult, ALU.add))
                dve.wait_ge(s["rope_a"], 3)
                link(dve.tensor_tensor(dlt[:, 5, :], dlt[:, 4, :], dlt[:, 4, :], ALU.mult))
                link(dve.tensor_scalar(dlt[:, 6, :], dlt[:, 5, :], 2.0, -1.0, ALU.mult, ALU.add))
                link(dve.tensor_scalar(dlt[:, 7, :], dlt[:, 3, :], -1.0, None, ALU.mult))
                dve.wait_ge(s["ld_late"], 16 * 8)
                dve.wait_ge(s["ld_cst"], 16)
                cr, sr = (cst[:, None, a:a + HALF].to_broadcast([P, 2, HALF]) for a in (C_RC, C_RS))
                cd, sd = (dlt[:, i:i + 1, 0:HALF].to_broadcast([P, 2, HALF]) for i in (6, 7))
                for k, (a, b, op) in enumerate(((cr, sr, ALU.subtract), (sr, cr, ALU.add))):
                    link(dve.tensor_tensor(rtmp[:, 0, 0:2, :], a, cd, ALU.mult))
                    link(dve.tensor_tensor(rtmp[:, 1, 0:2, :], b, sd, ALU.mult))
                    link(dve.tensor_tensor(rank_tab[:, k, :, :], rtmp[:, 0, 0:2, :], rtmp[:, 1, 0:2, :], op))
                cdr = dlt[:, 6:7, 0:HALF].to_broadcast([P, NT, HALF])
                sdr = dlt[:, 7:8, 0:HALF].to_broadcast([P, NT, HALF])
                for k in range(3):
                    c, sn = tab[:, 2 * k, :, :], tab[:, 2 * k + 1, :, :]
                    for dst, a, b, op in ((2 * k, c, sn, ALU.subtract), (2 * k + 1, sn, c, ALU.add)):
                        link(dve.tensor_tensor(rtmp[:, 0, :, :], a, cdr, ALU.mult))
                        link(dve.tensor_tensor(rtmp[:, 1, :, :], b, sdr, ALU.mult))
                        link(dve.tensor_tensor(rot[:, dst, :, :], rtmp[:, 0, :, :], rtmp[:, 1, :, :], op))
                link(dve.tensor_scalar(rot[:, 0:4, :, :].rearrange("p a t f -> p (a t f)"),
                                       rot[:, 0:4, :, :].rearrange("p a t f -> p (a t f)"), -SCALE, None, ALU.mult))
                for h in range(2):
                    dve.wait_ge(s["kv_mm"], h + 1)
                    kr = [psS[0], psM][h][:, :].rearrange("p (t d) -> p t d", d=64)[:, :, 0:DR]
                    dve.tensor_scalar(kmu[:, 8 * h:8 * h + 8, :], kr, 30.0, None, ALU.min).then_inc(s["mu"], 1)
                for h in range(2):
                    dve.wait_ge(s["key_l"], 2 * h + 2)
                    dve.wait_ge(s["lat_row"], 4)
                    m = kmu[:, 8 * h:8 * h + 8, :]
                    kr = [psS[0], psM][h][:, :].rearrange("p (t d) -> p t d", d=64)[:, :, 0:DR]
                    dve.tensor_tensor(m, m, kr, ALU.max).then_inc(s["mu"], 1)
                dve.wait_ge(s["mu"], 4)
                for i in range(2):
                    dve.tensor_copy(grow[:, :, DR * i:DR * (i + 1)], kmu[:, :, :]).then_inc(s["mu_row"], 1)
                m1, m2 = kmu[:, :, 0:HALF], kmu[:, :, HALF:DR]
                ck, sk = rot[:, 4, :, :], rot[:, 5, :, :]
                for i, (a, b, op) in enumerate(((m1, m2, ALU.subtract), (m2, m1, ALU.add))):
                    link(dve.tensor_tensor(rtmp[:, 0, :, :], a, ck, ALU.mult))
                    link(dve.tensor_tensor(rtmp[:, 1, :, :], b, sk, ALU.mult))
                    dve.tensor_tensor(lrow[:, :, 2 * DR + HALF * i:2 * DR + HALF * (i + 1)], rtmp[:, 0, :, :],
                                      rtmp[:, 1, :, :], op).then_inc(s["lrot"], 1)
                    dve.wait_ge(s["lrot"], i + 1)

                def combine(t, c):
                    w = min(CH, keys_of(t) - CH * c)
                    m = chunk_base(t) + c
                    dst = SC[:, t % 2, CH * c:CH * c + w]
                    dve.wait_ge(s["i_first"], m + 1)
                    dve.wait_ge(s["i_relu"], 4 * (m + 1))
                    for h in range(1, NIH):
                        if h > 1:
                            dve.wait_ge(s["comb"], 3 * m + h - 1)
                        dve.scalar_tensor_tensor(out=dst, in0=R[:, m % 2, h, 0:w], scalar=w_i[:, h:h + 1], in1=dst,
                                                 op0=ALU.mult, op1=ALU.add).then_inc(s["comb"], 1)

                def index_mask(t):
                    dve.wait_ge(s["comb"], 3 * chunk_base(t + 1))
                    lo = keys_of(t) - P
                    m = C_IM0 if t == 0 else C_IM
                    dst = SC[:, t % 2, lo:lo + P]
                    dve.tensor_tensor(dst, dst, cst[:, m:m + P], ALU.add).then_inc(s["im"], 1)

                def topk_step(t, k):
                    r, what = divmod(k, 3)
                    a = SC[:, t % 2, 0:keys_of(t)]
                    if k == 0:
                        dve.wait_ge(s["im"], t + 1)
                    if k > 0:
                        dve.wait_ge(s["topk"], 12 * t + k)
                    if k == 11:
                        dve.transpose(idx[:, t, :], idxf[:, :]).then_inc(s["topk"], 1)
                        dve.wait_ge(s["topk"], 12 * t + 12)
                        dve.sem_inc(s["idx_ready"], 1)
                        return
                    if what == 0:
                        ins = dve.max(out=top[:, r, :], in_=a)
                    elif what == 1:
                        ins = dve.max_index(out=idxf[:, 8 * r:8 * r + 8], in_max=top[:, r, :], in_values=a)
                    else:
                        ins = dve.match_replace(out=a, in_to_replace=top[:, r, :], in_values=a, imm_value=LOW)
                    ins.then_inc(s["topk"], 1)

                def q_min(t):
                    dve.wait_ge(s["q_mm"], t + 1)
                    if t >= 1:
                        dve.wait_ge(s["q_chain"], 10 * t)
                    dve.tensor_scalar(qe[:, :, :, :], psM[:, NH * CKV:].rearrange("p (h k f) -> p h k f", h=NH, k=2),
                                      30.0, None, ALU.min).then_inc(s["q_chain"], 1)

                def q_rotate(t, part):
                    base = 10 * t
                    if part == 0:
                        dve.wait_ge(s["q_e"], 2 * t + 2)
                        dve.wait_ge(s["qf_a"], 3 * t + 1)
                        dve.tensor_tensor(qmu[:, :, :, :], qe[:, :, :, :],
                                          psM[:, NH * CKV:].rearrange("p (h k f) -> p h k f", h=NH, k=2),
                                          ALU.max).then_inc(s["q_chain"], 1)
                        dve.wait_ge(s["q_chain"], base + 2)
                    mu2d = qmu[:, :, :, :].rearrange("p h k f -> p (h k) f")
                    for k in (2 * part, 2 * part + 1):
                        dve.tensor_tensor(qt[:, k, :, :], mu2d,
                                          rot[:, k:k + 1, t, :].to_broadcast([P, NH * 2, HALF]),
                                          ALU.mult).then_inc(s["q_chain"], 1)
                    dve.wait_ge(s["q_chain"], base + (4 if part == 0 else 8))
                    tc = qt[:, 2 * part, :, :].rearrange("p (h k) f -> p h k f", k=2)
                    ts = qt[:, 2 * part + 1, :, :].rearrange("p (h k) f -> p h k f", k=2)
                    o = 2 * DR * part
                    if t >= 1:
                        dve.wait_ge(s["q_t"], 2 * t)
                    dve.tensor_tensor(QF[:, :, o:o + HALF], tc[:, :, 0, :], ts[:, :, 1, :],
                                      ALU.subtract).then_inc(s["q_chain"], 1)
                    dve.tensor_tensor(QF[:, :, o + HALF:o + DR], ts[:, :, 0, :], tc[:, :, 1, :],
                                      ALU.add).then_inc(s["q_chain"], 1)

                def g_rotate(n):
                    t, b = divmod(n, NB)
                    dve.wait_ge(s_g[t % 2][b], 64 * (t // 2 + 1))
                    g = G[:, t % 2, GPB * b:GPB * (b + 1), 0:2 * DR]
                    dve.tensor_tensor(g, g, rank_tab[:, :, :, :].rearrange("p a k f -> p (a k f)")[:, None, :]
                                      .to_broadcast([P, GPB, 2 * DR]), ALU.mult).then_inc(s["g_rot"], 1)

                def s_minimum(n):
                    t, b = divmod(n, NB)
                    dve.wait_ge(s["s_mm"], n + 1)
                    if n >= 2:
                        dve.wait_ge(s["p_exp"], n - 1)
                    m = C_MASK0 if t == 0 and b < 4 else C_MASK
                    dve.tensor_tensor_reduce(out=S[:, n % 2, :], in0=psS[n % 2][:, 0:NS], in1=cst[:, m:m + NS],
                                             scale=1.0, scalar=3.0e38, op0=ALU.add, op1=ALU.min,
                                             accum_out=nmin[:, n % 2:n % 2 + 1]).then_inc(s["s_min"], 1)

                def row_inverse(n):
                    dve.wait_ge(s["p_exp"], n + 1)
                    if n >= 2:
                        dve.wait_ge(s["p_nrm"], n - 1)
                    dve.reciprocal(rinv[:, n % 2:n % 2 + 1], psumr[:, n % 4:n % 4 + 1]).then_inc(s["orec"], 1)

                def add_and_stats(t):
                    dve.wait_ge(s["y_mm"], t + 1)
                    dve.tensor_tensor(xa[:, :], PX, xr[:, t, :], ALU.add).then_inc(s["y_add"], 1)
                    dve.wait_ge(s["y_add"], t + 1)
                    dve.bn_stats(out=stats[:, 0, :], in_=xa[:, :]).then_inc(s["bn"], 1)
                    dve.wait_ge(s["bn"], 2 * t + 1)
                    dve.bn_aggr(out=mv[:, 0, :], in_=stats[:, 0, :]).then_inc(s["bn"], 1)

                def normalize(t):
                    dve.wait_ge(s["ln_a"], 2 * t + 2)
                    if t >= 4:
                        dve.wait_ge(s_sct[t % 4], 16 * (t // 4))
                        dve.wait_ge(s["x1d"], t - 3)
                        dve.wait_ge(s["x1_cp"], t - 3)
                    dve.tensor_scalar(x1[:, t % 4, :], xa[:, :], mv[:, 0, 0:1], lnv[:, 1, 0:1], ALU.subtract,
                                      ALU.mult).then_inc(s["x1_n"], 1)

                def route(t):
                    dve.wait_ge(s["lg_mm"], t + 1)
                    if t >= 1:
                        dve.wait_ge(s["lg_e"], t)
                    dve.tensor_copy(rlog[:, :], PX[:, 0:E0]).then_inc(s["lg_cp"], 1)
                    dve.wait_ge(s["lg_cp"], t + 1)
                    dve.max(out=r8[:, :], in_=rlog[:, :]).then_inc(s["rt_a"], 1)
                    dve.wait_ge(s["rt_a"], 4 * t + 1)
                    dve.tensor_scalar(rsm[:, 0:1], r8[:, 0:1], -1.0, None, ALU.mult).then_inc(s["rt"], 1)
                    dve.max_index(out=r8i[:, :], in_max=r8[:, :], in_values=rlog[:, :]).then_inc(s["rt"], 1)
                    dve.wait_ge(s["rt"], 5 * t + 2)
                    dve.tensor_copy(rsm[:, 2:3], r8i[:, 0:1]).then_inc(s["rt"], 1)
                    dve.wait_ge(s["rt"], 5 * t + 3)
                    dve.tensor_scalar(onehot[:, :], cst[:, C_IOTA:C_IOTA + E0], rsm[:, 2:3], None,
                                      ALU.is_equal).then_inc(s["rt"], 1)

                def place(t):
                    dve.wait_ge(s["cum_mm"], t + 1)
                    dve.tensor_tensor(ohsum[:, :], ohsum[:, :], onehot[:, :], ALU.add).then_inc(s["rt"], 1)
                    dve.tensor_tensor_reduce(out=rjunk[:, :], in0=PX[:, E0:2 * E0], in1=onehot[:, :], scale=1.0,
                                             scalar=0.0, op0=ALU.mult, op1=ALU.add,
                                             accum_out=rsm[:, 3:4]).then_inc(s["rte"], 1)
                    dve.wait_ge(s["rte"], t + 1)
                    dve.wait_ge(s["lg_e"], t + 1)
                    dve.tensor_scalar(rsm[:, 4:5], rsm[:, 3:4], float(C0), None, ALU.is_le).then_inc(s["rt_a"], 1)
                    dve.reciprocal(rsm[:, 5:6], rsm[:, 1:2]).then_inc(s["rt_a"], 1)
                    dve.scalar_tensor_tensor(out=rsm[:, 6:7], in0=rsm[:, 2:3], scalar=float(C0), in1=rsm[:, 3:4],
                                             op0=ALU.mult, op1=ALU.add).then_inc(s["rt_a"], 1)
                    dve.wait_ge(s["rt_a"], 4 * t + 4)
                    dve.tensor_tensor(gm[:, t:t + 1], rsm[:, 5:6], rsm[:, 4:5], ALU.mult).then_inc(s["plc"], 1)
                    dve.tensor_scalar(rsm[:, 7:8], rsm[:, 4:5], -2.0 * NSLOT, 2.0 * NSLOT - 1.0, ALU.mult,
                                      ALU.add).then_inc(s["plc"], 1)
                    dve.tensor_scalar(slot_out[:, t:t + 1], rsm[:, 6:7], -1.0, float(NSLOT - 1), ALU.add,
                                      ALU.min).then_inc(s["plc"], 1)
                    dve.wait_ge(s["plc"], 3 * (t + 1))
                    dve.tensor_tensor(slot_in[:, t:t + 1], rsm[:, 6:7], rsm[:, 7:8],
                                      ALU.add).then_inc(s["slots_ready"], 1)

                for n in range(N0, N1):
                    st, b = divmod(n, NB)
                    if 0 <= n + 1 < NT * NB:
                        g_rotate(n + 1)
                    if 0 <= n - 3 < NT * NB:
                        s_minimum(n - 3)
                    if 0 <= n - 5 < NT * NB:
                        row_inverse(n - 5)
                    if 0 <= st + 1 < NT:
                        if b == 1:
                            q_min(st + 1)
                        if b == 2:
                            q_rotate(st + 1, 0)
                        if b == 3:
                            q_rotate(st + 1, 1)
                    if 0 <= st - 2 < NT:
                        if b == 1:
                            add_and_stats(st - 2)
                        if b == 2:
                            normalize(st - 2)
                        if b == 5:
                            route(st - 2)
                        if b == 7:
                            place(st - 2)
                    for kind, t, i in index_steps.get(n, ()):
                        if kind == "sum":
                            combine(t, i)
                            if i == chunks_of(t) - 1:
                                index_mask(t)
                        else:
                            topk_step(t, i)

        flat = G[:, :, :, :].rearrange("p a g n -> p (a g n)")
        strips = {}
        for region, view, parts in (
                ("G", flat, (("x2", NT * D), ("x2T", L), ("vT", L + 2 * ROLL), ("acc", CH), ("tmp", CH), ("mvs", 64))),
                ("R", R[:, :, :, :].rearrange("p a h n -> p (a h n)"), (("yg", NT * D), ("sig", 4 * CH))),
                ("SC", SC[:, :, :].rearrange("p a n -> p (a n)"),
                 (("xb", 2 * EG * D), ("xbT", 2 * EG * C0), ("hid", EG * C0), ("sil", EG * C0), ("yb", 2 * EG * D))),
                ("Q", Q[:, :, :, :].rearrange("p a q h -> p (a q h)"), (("x3", 2 * CH), ("x3T", 2 * CH))),
                ("OT", ot_region[:, :], (("sl", 2 * CH), ("hd", 2 * CH))),
                ("KT", KT[:, :, :, :].rearrange("p a g n -> p (a g n)"), (("n1", CH), ("s2", CH))),
                ("QF", QF[:, :, :].rearrange("p h n -> p (h n)"), (("accf", CH), ("res", CH))),
                ("PT", PT[:, :, :].rearrange("p a n -> p (a n)"), (("tmpP", CH),)),
                ("PR", PR[:, :, :].rearrange("p a n -> p (a n)"), (("accP", CH),))):
            at = 0
            for name, size in parts:
                strips[name] = view[:, at:at + size]
                at += size
            assert at <= view.shape[1], (region, at)
        second_part(nc, dram, out, ctx, sem, strips, dict(
            cst=cst, ident=ident, xr=xr, gm=gm, slot_out=slot_out, w_ex=w_ex, s_we=s_we, load_experts=load_experts,
            w_value=w_value, w_gates=w_gates, w_up=w_up, w_down=w_down, gamma=gamma, beta=beta, w_g8=w_g8,
            xslots=xslots, yslots=yslots, banks=[psK, psX, psI[0], psI[1], psS[0], psP, psS[1], psM]))


def second_part(nc, dram, out, ctx, sem, m, k):
    cst, ident, xr, gm, w_ex, s_we = k["cst"], k["ident"], k["xr"], k["gm"], k["w_ex"], k["s_we"]
    w_value, w_gates, w_up, w_down = k["w_value"], k["w_gates"], k["w_up"], k["w_down"]
    gamma, beta, w_g8 = k["gamma"], k["beta"], k["w_g8"]
    bank = k["banks"]
    GC = EG * C0
    xb = m["xb"].rearrange("p (a e n) -> p a e n", a=2, e=EG)
    yb = m["yb"].rearrange("p (a e n) -> p a e n", a=2, e=EG)
    xbT = m["xbT"].rearrange("p (a n) -> p a n", a=2)
    hid, sil = m["hid"], m["sil"]
    yg = m["yg"].rearrange("p (t n) -> p t n", t=NT)
    x2 = m["x2"].rearrange("p (t n) -> p t n", t=NT)
    x2T, vT = m["x2T"], m["vT"]
    sig = m["sig"].rearrange("p (a n) -> p a n", a=4)
    acc, tmp, accP, tmpP = m["acc"], m["tmp"], m["accP"], m["tmpP"]
    x3 = m["x3"].rearrange("p (a t n) -> p a t n", a=2, t=TPC)
    x3T = m["x3T"].rearrange("p (a n) -> p a n", a=2)
    sl = m["sl"].rearrange("p (a n) -> p a n", a=2)
    hd = m["hd"].rearrange("p (a n) -> p a n", a=2)
    n1 = m["n1"].rearrange("p (t n) -> p t n", t=TPC)
    s2 = m["s2"].rearrange("p (t n) -> p t n", t=TPC)
    accf = m["accf"].rearrange("p (t n) -> p t n", t=TPC)
    res = m["res"].rearrange("p (t n) -> p t n", t=TPC)

    def sb(name, shape, dt=F32):
        return ctx.enter_context(nc.sbuf_tensor(name, shape, dt))

    stt = sb("stt", [P, TPC, 6])
    mv = sb("mv2", [P, TPC, 2])
    rstd = sb("rstd", [P, TPC])
    half = sb("half", [P, TPC])
    lg = sb("lg", [P, TPC, E1])
    lmax = sb("lmax", [P, TPC])
    lsum = sb("lsum", [P, TPC])
    t8 = sb("t8", [P, TPC, 8])
    t8i = sb("t8i", [P, TPC, 8], U32)
    t8f = sb("t8f", [P, TPC, 8])
    oh = sb("oh", [P, 2, TPC, E1])
    wt = sb("wt", [P, 2, TPC, E1])
    den = sb("den", [P, 2, TPC])
    out_rows = out.rearrange("(c t p) d -> c p t d", t=TPC, p=P)

    names = """xbt xbt_cp gate up silu hid y_mm y_cp y_st z ln pool_r x2_n x2_t x2_cp v_mm v_cp wrap
        x2b gt_mm sig prod prodP acc_done o_t lnc x3_t x3_cp lg_mm rt lexp wts h_mm g_mm sl hd d_mm dacc fin st_out
        halfset""".split()
    s = {n: sem("t_" + n) for n in names}
    s_xb = [sem(f"t_xb{i}") for i in range(2)]
    s_yst = [sem(f"t_yst{i}") for i in range(2)]
    s_yg = [sem(f"t_yg{c}") for c in range(NCH)]
    s_out = [sem(f"t_out{i}") for i in range(2)]

    POOL_GATES = (2, 5, 8)
    NPG = len(POOL_GATES)
    DVE_GATES = tuple(i for i in range(NGATE) if i not in POOL_GATES)
    NDG = len(DVE_GATES)
    ORDER = (E1, E1 + 1) + tuple(range(E1))

    with nc.Block() as block:
        @block.sync
        def _(sp):
            for g in range(NEG):
                if g >= 2:
                    sp.wait_ge(s["xbt"], g - 1)
                    sp.wait_ge(s_xb[g % 2], 16 * (g // 2))
                sp.dma_start(xb[0:C0, g % 2, :, :],
                             k["xslots"][GC * g:GC * (g + 1), :].rearrange("(e c) d -> c e d", c=C0)
                             ).then_inc(s_xb[g % 2], 16)
                if g >= 2:
                    sp.wait_ge(s["y_mm"], g - 1)
                    k["load_experts"](sp, g)
            for c in range(NCH):
                sp.wait_ge(s["fin"], c + 1)
                sp.dma_start(out_rows[c], res).then_inc(s_out[c % 2], 16)
                sp.wait_ge(s_out[c % 2], 16 * (c // 2 + 1))

        @block.gpsimd
        def _(pool):
            pool.memset(half[:, :], -0.5).then_inc(s["halfset"], 1)
            pool.wait_ge(s["halfset"], 1)
            for i in range(2):
                pool.wait_ge(s_yst[i], 16 * NEG // 2)
            for t in range(NT):
                pool.indirect_dma_start(yg[:, t, :], None, k["yslots"],
                                        bass.IndirectOffsetOnAxis(ap=k["slot_out"][:, t:t + 1], axis=0)
                                        ).then_inc(s_yg[t // TPC], 16)
            done = [0]

            def root(n_stats):
                pool.wait_ge(s["ln"], n_stats)
                pool.tensor_scalar(rstd[:, :], mv[:, :, 1], LN_EPS, None, ALU.add).then_inc(s["pool_r"], 1)
                done[0] += 1
                pool.wait_ge(s["pool_r"], done[0])
                pool.tensor_tensor(rstd[:, :], rstd[:, :], half[:, :], ALU.pow).then_inc(s["pool_r"], 1)
                done[0] += 1

            for c in range(NCH):
                root(8 * (c + 1))
            pool.wait_ge(s["x2_t"], NCH)
            for c in range(NCH):
                pool.tensor_tensor(x2[:, TPC * c:TPC * (c + 1), :], x2[:, TPC * c:TPC * (c + 1), :],
                                   beta[:, None, :].to_broadcast([P, TPC, D]), ALU.add).then_inc(s["x2b"], 1)
            pool.wait_ge(s["wrap"], 2)
            seen = 8 * NCH
            for j in range(-1, NCH):
                if j + 1 < NCH:
                    c = j + 1
                    for i, g in enumerate(POOL_GATES):
                        n = NGATE * c + g
                        base = (2 * NPG - 1) * c
                        v = vT[:, ROLL + SHIFTS[g] + CH * c:ROLL + SHIFTS[g] + CH * (c + 1)]
                        pool.wait_ge(s["sig"], n + 1)
                        if i == 0:
                            if c >= 1:
                                pool.wait_ge(s["acc_done"], c)
                            pool.tensor_tensor(accP, v, sig[:, n % 4, :], ALU.mult).then_inc(s["prodP"], 1)
                        else:
                            pool.wait_ge(s["prodP"], base + 2 * i - 1)
                            pool.tensor_tensor(tmpP, v, sig[:, n % 4, :], ALU.mult).then_inc(s["prodP"], 1)
                            pool.wait_ge(s["prodP"], base + 2 * i)
                            pool.tensor_tensor(accP, accP, tmpP, ALU.add).then_inc(s["prodP"], 1)
                    for _ in range(2):
                        seen += 8
                        root(seen)
                if j >= 0:
                    seen += 8
                    root(seen)

        @block.tensor
        def _(pe):
            def expert_front(g):
                pe.wait_ge(s_xb[g % 2], 16 * (g // 2 + 1))
                if g >= 2:
                    pe.wait_ge(s["xbt_cp"], g - 1)
                for e in range(EG):
                    mm = pe.transpose(bank[g % 2][:, C0 * e:C0 * (e + 1)], xb[0:C0, g % 2, e, :], ident[0:C0, 0:C0])
                mm.then_inc(s["xbt"], 1)
                pe.wait_ge(s["xbt_cp"], g + 1)
                pe.wait_ge(s_we[g % 2], 48 * (g // 2 + 1))
                if g >= 1:
                    pe.wait_ge(s["silu"], g)
                for e in range(EG):
                    mm = pe.matmul(bank[2][:, C0 * e:C0 * (e + 1)], w_ex[:, g % 2, 0, e, :],
                                   xbT[:, g % 2, C0 * e:C0 * (e + 1)], start=True, stop=True, skip_group_check=True)
                mm.then_inc(s["gate"], 1)
                if g >= 1:
                    pe.wait_ge(s["hid"], g)
                for e in range(EG):
                    mm = pe.matmul(bank[3][:, C0 * e:C0 * (e + 1)], w_ex[:, g % 2, 1, e, :],
                                   xbT[:, g % 2, C0 * e:C0 * (e + 1)], start=True, stop=True, skip_group_check=True)
                mm.then_inc(s["up"], 1)

            def expert_down(g):
                pe.wait_ge(s["hid"], g + 1)
                if g >= 2:
                    pe.wait_ge(s["y_cp"], g - 1)
                for e in range(EG):
                    mm = pe.matmul(bank[4 + g % 2][0:C0, D * e:D * (e + 1)], hid[:, C0 * e:C0 * (e + 1)],
                                   w_ex[:, g % 2, 2, e, :], start=True, stop=True, skip_group_check=True)
                mm.then_inc(s["y_mm"], 1)

            for g in range(NEG):
                expert_front(g)
                expert_down(g)
            for c in range(NCH):
                pe.wait_ge(s["x2_n"], TPC * (c + 1))
                if c >= 2:
                    pe.wait_ge(s["x2_cp"], c - 1)
                for t in range(TPC):
                    mm = pe.transpose(bank[c % 2][:, P * t:P * (t + 1)], x2[:, TPC * c + t, :], ident)
                mm.then_inc(s["x2_t"], 1)
            for c in range(NCH):
                pe.wait_ge(s["x2_cp"], c + 1)
                pe.matmul(bank[2 + c][:, :], w_value, x2T[:, CH * c:CH * (c + 1)], start=True,
                          stop=True).then_inc(s["v_mm"], 1)

            def gates(c):
                for g in range(NGATE):
                    n = NGATE * c + g
                    if n == 0:
                        pe.wait_ge(s["x2_cp"], NCH)
                    if n >= 2:
                        pe.wait_ge(s["sig"], n - 1)
                    if g == 0 and c >= 1:
                        pe.wait_ge(s["x3_cp"], c)
                        pe.wait_ge(s["rt"], 14 * c - 12)
                    pe.matmul(bank[n % 2][:, :], w_gates[:, D * g:D * (g + 1)], x2T[:, CH * c:CH * (c + 1)],
                              start=True, stop=True).then_inc(s["gt_mm"], 1)

            def mixed_transpose(c):
                pe.wait_ge(s["acc_done"], c + 1)
                pe.wait_ge(s["sig"], NGATE * (c + 1))
                for t in range(TPC):
                    mm = pe.transpose(bank[0][:, P * t:P * (t + 1)], acc[:, P * t:P * (t + 1)], ident)
                mm.then_inc(s["o_t"], 1)

            def x3_transpose(c):
                pe.wait_ge(s["lnc"], 10 * (c + 1))
                for t in range(TPC):
                    mm = pe.transpose(bank[0][:, P * t:P * (t + 1)], x3[:, c % 2, t, :], ident)
                mm.then_inc(s["x3_t"], 1)

            def route_logits(c):
                pe.wait_ge(s["x3_cp"], c + 1)
                for t in range(TPC):
                    mm = pe.matmul(bank[1][:, E1 * t:E1 * (t + 1)], x3T[:, c % 2, P * t:P * (t + 1)], w_g8,
                                   start=True, stop=True, skip_group_check=True)
                mm.then_inc(s["lg_mm"], 1)

            def ffn_up(c, i):
                n = NHC * c + i
                if n == 0:
                    pe.wait_ge(s["v_cp"], NCH)
                if n >= 2:
                    pe.wait_ge(s["sl"], n - 1)
                    pe.wait_ge(s["hd"], n - 1)
                e = ORDER[i]
                pe.matmul(bank[2 + 2 * (n % 2)][0:H1, :], w_up[:, 0, e, :], x3T[:, c % 2, :], start=True,
                          stop=True).then_inc(s["h_mm"], 1)
                pe.matmul(bank[3 + 2 * (n % 2)][0:H1, :], w_up[:, 1, e, :], x3T[:, c % 2, :], start=True,
                          stop=True).then_inc(s["g_mm"], 1)

            def ffn_down(c, i):
                n = NHC * c + i
                m_ = 9 * c + i - 1
                if m_ >= 2:
                    pe.wait_ge(s["dacc"], m_ - 1)
                pe.wait_ge(s["hd"], n + 1)
                parts = (0, 1) if i == 1 else (i,)
                for t in range(TPC):
                    for p in parts:
                        mm = pe.matmul(bank[6 + m_ % 2][:, D * t:D * (t + 1)],
                                       hd[0:H1, (NHC * c + p) % 2, P * t:P * (t + 1)], w_down[:, ORDER[p], :],
                                       start=(p == parts[0]), stop=(p == parts[-1]), skip_group_check=True)
                mm.then_inc(s["d_mm"], 1)

            for j in range(-1, NCH):
                if j + 1 < NCH:
                    gates(j + 1)
                for i in range(NHC + 1):
                    if j >= 0 and i < NHC:
                        ffn_up(j, i)
                    if j >= 0 and i >= 2:
                        ffn_down(j, i - 1)
                    if j + 1 < NCH:
                        if i == 1:
                            mixed_transpose(j + 1)
                        if i == 6:
                            x3_transpose(j + 1)
                        if i == 8:
                            route_logits(j + 1)

        @block.scalar
        def _(act):
            for g in range(NEG):
                act.wait_ge(s["gate"], g + 1)
                if g >= 1:
                    act.wait_ge(s["hid"], g)
                act.activation(sil, bank[2][:, 0:GC], ACT.Silu).then_inc(s["silu"], 1)
                act.wait_ge(s["y_mm"], g + 1)
                if g >= 2:
                    act.wait_ge(s_yst[g % 2], 16 * (g // 2))
                act.activation(yb[0:C0, g % 2, :, :].rearrange("p e n -> p (e n)"), bank[4 + g % 2][0:C0, :],
                               ACT.Copy).then_inc(s["y_cp"], 1)
                act.wait_ge(s["y_cp"], g + 1)
                act.dma_start(k["yslots"][GC * g:GC * (g + 1), :].rearrange("(e c) d -> c e d", c=C0),
                              yb[0:C0, g % 2, :, :]).then_inc(s_yst[g % 2], 16)
            for c in range(NCH):
                act.wait_ge(s["x2_t"], c + 1)
                act.activation(x2T[:, CH * c:CH * (c + 1)], bank[c % 2][:, :], ACT.Copy).then_inc(s["x2_cp"], 1)
            for c in range(NCH):
                act.wait_ge(s["v_mm"], c + 1)
                act.activation(vT[:, ROLL + CH * c:ROLL + CH * (c + 1)], bank[2 + c][:, :],
                               ACT.Copy).then_inc(s["v_cp"], 1)
            act.wait_ge(s["v_cp"], NCH)
            act.activation(vT[:, 0:ROLL], vT[:, L:L + ROLL], ACT.Copy).then_inc(s["wrap"], 1)
            act.activation(vT[:, ROLL + L:], vT[:, ROLL:2 * ROLL], ACT.Copy).then_inc(s["wrap"], 1)
            for j in range(-1, NCH):
                if j + 1 < NCH:
                    c = j + 1
                    for g in range(NGATE):
                        n = NGATE * c + g
                        act.wait_ge(s["gt_mm"], n + 1)
                        if n >= 4:
                            wait_product(act, s, n - 4, DVE_GATES, POOL_GATES)
                        act.activation(sig[:, n % 4, :], bank[n % 2][:, :], ACT.Sigmoid).then_inc(s["sig"], 1)
                for i in range(NHC):
                    if j >= 0:
                        n = NHC * j + i
                        act.wait_ge(s["h_mm"], n + 1)
                        if n >= 2:
                            act.wait_ge(s["hd"], n - 1)
                        act.activation(sl[0:H1, n % 2, :], bank[2 + 2 * (n % 2)][0:H1, :],
                                       ACT.Silu).then_inc(s["sl"], 1)
                if j + 1 < NCH:
                    c = j + 1
                    act.wait_ge(s["rt"], 14 * c + 2)
                    act.activation(lg[:, :, :], lg[:, :, :], ACT.Exp).then_inc(s["lexp"], 1)

        @block.vector
        def _(dve):
            for g in range(NEG):
                dve.wait_ge(s["xbt"], g + 1)
                if g >= 2:
                    dve.wait_ge(s["up"], g - 1)
                dve.tensor_copy(xbT[:, g % 2, :], bank[g % 2][:, 0:GC]).then_inc(s["xbt_cp"], 1)
                dve.wait_ge(s["silu"], g + 1)
                dve.wait_ge(s["up"], g + 1)
                if g >= 1:
                    dve.wait_ge(s["y_mm"], g)
                dve.tensor_tensor(hid, sil, bank[3][:, 0:GC], ALU.mult).then_inc(s["hid"], 1)
            for c in range(NCH):
                dve.wait_ge(s_yg[c], 16 * TPC)
                for i in range(TPC):
                    t = TPC * c + i
                    dve.scalar_tensor_tensor(out=yg[:, t, :], in0=yg[:, t, :], scalar=gm[:, t:t + 1],
                                             in1=xr[:, t, :], op0=ALU.mult, op1=ALU.add).then_inc(s["z"], 1)
                for i in range(TPC):
                    t = TPC * c + i
                    dve.wait_ge(s["z"], t + 1)
                    if c >= 1 and i == 0:
                        dve.wait_ge(s["x2_n"], TPC * c)
                    dve.bn_stats(out=stt[:, i, :], in_=yg[:, t, :]).then_inc(s["ln"], 1)
                for i in range(TPC):
                    dve.wait_ge(s["ln"], 8 * c + i + 1)
                    dve.bn_aggr(out=mv[:, i, :], in_=stt[:, i, :]).then_inc(s["ln"], 1)
                dve.wait_ge(s["pool_r"], 2 * (c + 1))
                for i in range(TPC):
                    t = TPC * c + i
                    dve.tensor_scalar(x2[:, t, :], yg[:, t, :], mv[:, i, 0:1], rstd[:, i:i + 1], ALU.subtract,
                                      ALU.mult).then_inc(s["x2_n"], 1)
            lnn = [8 * NCH]
            pooln = [2 * NCH]

            def statistics(src, after):
                after()
                for i in range(TPC):
                    dve.bn_stats(out=stt[:, i, :], in_=src(i)).then_inc(s["ln"], 1)
                    lnn[0] += 1
                for i in range(TPC):
                    dve.wait_ge(s["ln"], lnn[0] - TPC + i + 1)
                    dve.bn_aggr(out=mv[:, i, :], in_=stt[:, i, :]).then_inc(s["ln"], 1)
                lnn[0] += TPC

            def wait_root():
                pooln[0] += 2
                dve.wait_ge(s["pool_r"], pooln[0])

            def product(c, g):
                i = DVE_GATES.index(g)
                n = NGATE * c + g
                base = (2 * NDG - 1) * c
                v = vT[:, ROLL + SHIFTS[g] + CH * c:ROLL + SHIFTS[g] + CH * (c + 1)]
                dve.wait_ge(s["sig"], n + 1)
                if i == 0:
                    if c == 0:
                        dve.wait_ge(s["wrap"], 2)
                    else:
                        dve.wait_ge(s["o_t"], c)
                    dve.tensor_tensor(acc, v, sig[:, n % 4, :], ALU.mult).then_inc(s["prod"], 1)
                else:
                    dve.tensor_tensor(tmp, v, sig[:, n % 4, :], ALU.mult).then_inc(s["prod"], 1)
                    dve.wait_ge(s["prod"], base + 2 * i)
                    dve.tensor_tensor(acc, acc, tmp, ALU.add).then_inc(s["prod"], 1)
                    dve.wait_ge(s["prod"], base + 2 * i + 1)

            def mix_sum(c):
                dve.wait_ge(s["prodP"], (2 * NPG - 1) * (c + 1))
                dve.tensor_tensor(acc, acc, accP, ALU.add).then_inc(s["acc_done"], 1)

            def norm1(c):
                statistics(lambda i: bank[0][:, P * i:P * (i + 1)], lambda: dve.wait_ge(s["o_t"], c + 1))

            def norm2(c):
                b = 10 * c
                wait_root()
                for i in range(TPC):
                    dve.tensor_scalar(n1[:, i, :], bank[0][:, P * i:P * (i + 1)], mv[:, i, 0:1], rstd[:, i:i + 1],
                                      ALU.subtract, ALU.mult).then_inc(s["lnc"], 1)
                dve.wait_ge(s["lnc"], b + 4)
                dve.tensor_tensor(n1, n1, gamma[:, None, :].to_broadcast([P, TPC, D]), ALU.mult).then_inc(s["lnc"], 1)
                dve.wait_ge(s["lnc"], b + 5)
                dve.wait_ge(s["x2b"], c + 1)
                dve.tensor_tensor(s2, n1, x2[:, TPC * c:TPC * (c + 1), :], ALU.add).then_inc(s["lnc"], 1)
                dve.wait_ge(s["lnc"], b + 6)
                statistics(lambda i: s2[:, i, :], lambda: None)

            def norm3(c):
                wait_root()
                for i in range(TPC):
                    dve.tensor_scalar(x3[:, c % 2, i, :], s2[:, i, :], mv[:, i, 0:1], rstd[:, i:i + 1],
                                      ALU.subtract, ALU.mult).then_inc(s["lnc"], 1)

            def x3_copy(c):
                dve.wait_ge(s["x3_t"], c + 1)
                dve.tensor_copy(x3T[:, c % 2, :], bank[0][:, :]).then_inc(s["x3_cp"], 1)

            def route_max(c):
                b = 14 * c
                dve.wait_ge(s["lg_mm"], c + 1)
                l4 = bank[1][:, 0:TPC * E1].rearrange("p (t e) -> p t e", t=TPC)
                dve.tensor_reduce(lmax[:, :], l4, mybir.AxisListType.X, ALU.max).then_inc(s["rt"], 1)
                dve.wait_ge(s["rt"], b + 1)
                dve.tensor_tensor(lg[:, :, :], l4, lmax[:, :, None].to_broadcast([P, TPC, E1]),
                                  ALU.subtract).then_inc(s["rt"], 1)

            def route_weights(c):
                b = 14 * c
                dve.wait_ge(s["lexp"], c + 1)
                dve.tensor_reduce(lsum[:, :], lg[:, :, :], mybir.AxisListType.X, ALU.add).then_inc(s["rt"], 1)
                dve.wait_ge(s["rt"], b + 3)
                dve.reciprocal(lsum[:, :], lsum[:, :]).then_inc(s["rt"], 1)
                dve.wait_ge(s["rt"], b + 4)
                dve.tensor_tensor(lg[:, :, :], lg[:, :, :], lsum[:, :, None].to_broadcast([P, TPC, E1]),
                                  ALU.mult).then_inc(s["rt"], 1)
                dve.wait_ge(s["rt"], b + 5)
                for i in range(TPC):
                    ins = dve.max(out=t8[:, i, :], in_=lg[:, i, :])
                ins.then_inc(s["rt"], 1)
                dve.wait_ge(s["rt"], b + 6)
                for i in range(TPC):
                    ins = dve.max_index(out=t8i[:, i, :], in_max=t8[:, i, :], in_values=lg[:, i, :])
                ins.then_inc(s["rt"], 1)
                dve.wait_ge(s["rt"], b + 7)
                dve.tensor_copy(t8f[:, :, :], t8i[:, :, :]).then_inc(s["rt"], 1)
                dve.tensor_tensor(den[:, 0, :], t8[:, :, 0], t8[:, :, 1], ALU.add).then_inc(s["rt"], 1)
                dve.wait_ge(s["rt"], b + 9)
                dve.tensor_scalar(den[:, 0, :], den[:, 0, :], SUM_EPS, None, ALU.add).then_inc(s["rt"], 1)
                iota = cst[:, None, C_IOTA:C_IOTA + E1].to_broadcast([P, TPC, E1])
                for i in range(2):
                    dve.tensor_tensor(oh[:, i, :, :], iota, t8f[:, :, i:i + 1].to_broadcast([P, TPC, E1]),
                                      ALU.is_equal).then_inc(s["rt"], 1)
                dve.wait_ge(s["rt"], b + 12)
                dve.reciprocal(den[:, 1, :], den[:, 0, :]).then_inc(s["rt"], 1)
                for i in range(2):
                    ins = dve.tensor_tensor(oh[:, i, :, :], oh[:, i, :, :],
                                            t8[:, :, i:i + 1].to_broadcast([P, TPC, E1]), ALU.mult)
                ins.then_inc(s["rt"], 1)
                dve.wait_ge(s["rt"], b + 14)
                dve.tensor_tensor(oh[:, 0, :, :], oh[:, 0, :, :], oh[:, 1, :, :], ALU.add).then_inc(s["wts"], 1)
                dve.wait_ge(s["wts"], 2 * c + 1)
                dve.tensor_tensor(wt[:, c % 2, :, :], oh[:, 0, :, :], den[:, 1, :, None].to_broadcast([P, TPC, E1]),
                                  ALU.mult).then_inc(s["wts"], 1)

            def hidden(c, i):
                n = NHC * c + i
                dve.wait_ge(s["sl"], n + 1)
                dve.wait_ge(s["g_mm"], n + 1)
                if n >= 2:
                    if i == 2:
                        dve.wait_ge(s["d_mm"], 9 * c + 1)
                    elif i < 2:
                        dve.wait_ge(s["d_mm"], 9 * (c - 1) + 8 + i)
                    else:
                        dve.wait_ge(s["d_mm"], 9 * c + i - 2)
                dve.tensor_tensor(hd[0:H1, n % 2, :], sl[0:H1, n % 2, :], bank[3 + 2 * (n % 2)][0:H1, :],
                                  ALU.mult).then_inc(s["hd"], 1)

            def accumulate(c, i):
                m_ = 9 * c + i - 1
                dve.wait_ge(s["d_mm"], m_ + 1)
                src = bank[6 + m_ % 2][:, :].rearrange("p (t n) -> p t n", t=TPC)
                if m_ >= 1:
                    dve.wait_ge(s["dacc"], m_)
                if i == 1:
                    dve.tensor_tensor(accf, src, x3[:, c % 2, :, :], ALU.add).then_inc(s["dacc"], 1)
                else:
                    e = ORDER[i]
                    if i == 2:
                        dve.wait_ge(s["wts"], 2 * c + 2)
                    for t in range(TPC):
                        ins = dve.scalar_tensor_tensor(out=accf[:, t, :], in0=src[:, t, :],
                                                       scalar=wt[:, c % 2, t, e:e + 1], in1=accf[:, t, :],
                                                       op0=ALU.mult, op1=ALU.add)
                    ins.then_inc(s["dacc"], 1)

            def finish(c):
                dve.wait_ge(s["dacc"], 9 * (c + 1))
                statistics(lambda i: accf[:, i, :], lambda: None)
                wait_root()
                if c >= 1:
                    dve.wait_ge(s_out[(c - 1) % 2], 16 * ((c - 1) // 2 + 1))
                for i in range(TPC):
                    ins = dve.tensor_scalar(res[:, i, :], accf[:, i, :], mv[:, i, 0:1], rstd[:, i:i + 1],
                                            ALU.subtract, ALU.mult)
                ins.then_inc(s["fin"], 1)

            for j in range(-1, NCH):
                nx = j + 1 < NCH
                if nx:
                    for g in DVE_GATES:
                        product(j + 1, g)
                    mix_sum(j + 1)
                for i in range(NHC + 1):
                    if j >= 0 and i < NHC:
                        hidden(j, i)
                    if j >= 0 and i >= 2:
                        accumulate(j, i - 1)
                    if nx:
                        if i == 1:
                            norm1(j + 1)
                        if i == 3:
                            norm2(j + 1)
                        if i == 5:
                            norm3(j + 1)
                        if i == 6:
                            x3_copy(j + 1)
                        if i == 8:
                            route_max(j + 1)
                if j >= 0:
                    finish(j)
                if nx:
                    route_weights(j + 1)


def wait_product(act, s, n, dve_gates, pool_gates):
    c, g = divmod(n, NGATE)
    if g in pool_gates:
        i = pool_gates.index(g)
        act.wait_ge(s["prodP"], (2 * len(pool_gates) - 1) * c + max(2 * i, 1))
    else:
        i = dve_gates.index(g)
        act.wait_ge(s["prod"], (2 * len(dve_gates) - 1) * c + max(2 * i, 1))


def kernel(**inputs):
    import concourse.bacc as _bacc
    from concourse.bass_utils import run_bass_kernel_spmd as _run

    def a(name):
        return np.asarray(inputs[name])

    consts, tables = shape_constants()
    raw = a("L0_attn_raw_delta")
    x = a("L0_attn_x").reshape(L, D)

    def heads(w, rows):
        return np.ascontiguousarray(w.reshape(rows, NH, DH).transpose(2, 1, 0))

    arrays = {
        "cst": consts,
        "tab": tables,
        "raw": np.concatenate([np.tile(raw, (P, 1)), np.tile(raw, P // HALF)[:, None]], 1),
        "xT": np.ascontiguousarray(x.T),
        "x": np.ascontiguousarray(x.reshape(NT, P, D).transpose(1, 0, 2)),
        "idx_wk": a("L0_attn_idx_wk"),
        "idx_wq": a("L0_attn_idx_wq"),
        "idx_w": np.tile(a("L0_attn_idx_w"), (P, 1)),
        "W_kr": a("L0_attn_W_kr"),
        "W_dkv": a("L0_attn_W_dkv"),
        "W_dq": a("L0_attn_W_dq"),
        "W_qr": a("L0_attn_W_qr"),
        "W_uqT": heads(a("L0_attn_W_uq"), CQ),
        "W_ukT": heads(a("L0_attn_W_uk"), CKV),
        "W_uvT": heads(a("L0_attn_W_uv"), CKV),
        "W_out": np.ascontiguousarray(a("L0_attn_W_out").reshape(NH, DH, D).transpose(1, 0, 2)),
        "w_router": a("L0_ffn_w_router"),
        "w_gate": a("L0_ffn_w_gate"),
        "w_up": a("L0_ffn_w_up"),
        "w_down": a("L0_ffn_w_down"),
        "gate_W": np.ascontiguousarray(a("L1_attn_gate_W").T),
        "value_W": np.ascontiguousarray(a("L1_attn_value_W").T),
        "gamma": np.tile(a("L1_attn_gamma"), (P, 1)),
        "beta": np.tile(a("L1_attn_beta"), (P, 1)),
        "Wg": np.ascontiguousarray(a("L1_ffn_Wg").T),
        "W1": np.ascontiguousarray(a("L1_ffn_W1").transpose(1, 0, 2)),
        "W3": np.ascontiguousarray(a("L1_ffn_W3").transpose(1, 0, 2)),
        "W2": np.ascontiguousarray(a("L1_ffn_W2").transpose(1, 0, 2)),
        "Ws1": np.ascontiguousarray(a("L1_ffn_Ws1").reshape(D, 2, H1)),
        "Ws3": np.ascontiguousarray(a("L1_ffn_Ws3").reshape(D, 2, H1)),
        "Ws2": np.ascontiguousarray(a("L1_ffn_Ws2").reshape(2, H1, D).transpose(1, 0, 2)),
    }
    nc = _bacc.Bacc("TRN2", target_bir_lowering=False, num_devices=1)
    sent = {f"in_{n}": np.ascontiguousarray(v) for n, v in arrays.items()}
    dram = {n: nc.dram_tensor(f"in_{n}", v.shape, F32, kind="ExternalInput").ap() for n, v in arrays.items()}
    out = nc.dram_tensor("out_0", (L, D), F32, kind="ExternalOutput").ap()
    program(nc, dram, out)
    r = _run(nc, [sent], core_ids=[0])
    return r.results[0]["out_0"].reshape(1, L, D)
```

```python
from contextlib import ExitStack

import numpy as np

import concourse.bass as bass
from concourse import mybir

F32 = mybir.dt.float32
U32 = mybir.dt.uint32
ALU = mybir.AluOpType
ACT = mybir.ActivationFunctionType

P = 128
L = 2048
D = 128
NT = L // P
CKV, CQ = 32, 64
NH, DH, DR = 8, 64, 32
HALF = DR // 2
NIH = 4
KTS, LW = 96, 64
NSEL = KTS - LW
SCALE = (DH + DR) ** -0.5
ROPE_BASE = 10000.0
QB = 16
NB = P // QB
GPB = 4
NG = NB * GPB
WIN = QB + LW
NS = P + WIN
PAD = LW
BIG = 1.0e30
LOW = -3.0e38
E0, C0 = 32, 80
NSLOT = E0 * C0
EG = 4
NEG = E0 // EG
NXB = 4
NEW = 5
SHIFTS = (0, -32, -16, -4, -1, 1, 4, 16, 32)
NGATE = len(SHIFTS)
ROLL = 32
E1, H1 = 8, 88
NHC = E1 + 2
CH = 512
NCH = L // CH
TPC = CH // P
LN_EPS = 1e-5
SUM_EPS = 1e-20


def keys_of(t):
    return P if t == 0 else P * t + LW


def chunks_of(t):
    return -(-keys_of(t) // CH)


def chunk_base(t):
    return sum(chunks_of(u) for u in range(t))


N0, N1 = -2 * NB, NT * NB + 2 * NB
INDEX_END = NB * (NT - 2) - -1
START_ROOM = 0.25
TOP_STEPS = 12


def index_plan():
    items = [("sum", 1, c) for c in range(chunks_of(1))]
    for t in range(1, NT):
        nxt = chunks_of(t + 1) if t + 1 < NT else 0
        at = [TOP_STEPS if t == 1 else (c + 1) * TOP_STEPS // (nxt + 1) for c in range(nxt)]
        for k in range(TOP_STEPS):
            items.append(("top", t, k))
            items += [("sum", t + 1, c) for c in range(nxt) if at[c] == k + 1]

    def cost(item):
        kind, t, i = item
        if kind == "sum":
            return 3 * 1.16 * min(CH, keys_of(t) - CH * i) / 1000 + 0.2
        return (1.04 * keys_of(t) / 1000 + 0.07) if i < TOP_STEPS - 1 else 0.1

    other = (0.0, 0.9, 1.9, 1.3, 0.0, 0.6, 0.0, 0.8)

    def lay(level):
        plan, done_at, top_end, n, left = {}, {0: N0}, {0: N0}, N0 + 2, 0.0
        for item in items:
            m = chunk_base(item[1]) + item[2]
            first = N0
            if item[0] == "sum":
                first = done_at[m - 1] + 2 if n >= -6 else done_at[m - 2] + 2 if m >= 2 else N0
            if item[0] == "sum" and item[2] == 0 and item[1] >= 2:
                first = max(first, top_end[item[1] - 2] + 3)
            while left <= 0 or n < first:
                n += 1
                if n < 0:
                    left = min(left, 0.0) + START_ROOM
                else:
                    left = min(left, 0.0) + max(0.0, level - (0.7 if n >= 3 else 0.0) - other[n % NB])
            plan.setdefault(n, []).append(item)
            if item[0] == "sum":
                done_at[m] = n
            else:
                top_end[item[1]] = n
            left -= cost(item)
        return plan, done_at, n

    level = 2.0
    while lay(level)[2] > INDEX_END:
        level += 0.02
    plan, done_at, _ = lay(level)
    pairs = {}
    for t in range(1, NT):
        for c in range(chunks_of(t)):
            m = chunk_base(t) + c
            last = done_at[m] - 2
            first = max(last - 1, done_at[m - 2] if m >= 2 else N0, done_at[m - 1] - 2 if m >= 1 else N0)
            for u, n in ((0, first), (1, last)):
                pairs.setdefault(n, []).append((t, 2 * c + u))
    for t in range(1, NT):
        ready = max(n for n, its in plan.items() if ("top", t, TOP_STEPS - 1) in its)
        assert ready < NB * (t - 1) + 6 or t <= 2
    return pairs, plan


C_ID = 0
C_MASK = C_ID + P
C_MASK0 = C_MASK + NS
C_IM = C_MASK0 + NS
C_IM0 = C_IM + P
C_TRI = C_IM0 + P
C_IOTA = C_TRI + P
C_RC = C_IOTA + E0
C_RS = C_RC + HALF
C_ONES = C_RS + HALF
C_EPS = C_ONES + P
C_N = C_EPS + 1


def shape_constants():
    c = np.zeros((P, C_N), np.float32)
    c[:, C_ID:C_ID + P] = np.eye(P)
    row = np.arange(P)
    ql = row // NH
    col = np.arange(P)
    sel = (ql[:, None] % GPB) == (col[None, :] // NSEL)
    w = np.arange(WIN)
    local = (w[None, :] >= ql[:, None] + 1) & (w[None, :] <= ql[:, None] + LW)
    first = np.broadcast_to(w[None, :] < LW, (P, WIN))
    for base, loc in ((C_MASK, local), (C_MASK0, first)):
        c[:, base:base + P] = np.where(sel, 0, BIG)
        c[:, base + P:base + NS] = np.where(loc, 0, BIG)
    qi = 4 * (row % 32) + row // 32
    c[:, C_IM:C_IM + P] = np.where(col[None, :] <= qi[:, None], 0, -BIG)
    b = np.maximum(qi - (LW - 1), 0)[:, None]
    c[:, C_IM0:C_IM0 + P] = np.where(col[None, :] < b, 0, np.where(col[None, :] < b + LW, LOW, -BIG))
    c[:, C_TRI:C_TRI + P] = row[:, None] <= row[None, :]
    c[:, C_IOTA:C_IOTA + E0] = np.arange(E0)
    theta = (np.float32(1.0) / np.float32(ROPE_BASE) ** (np.float32(2.0) * np.arange(HALF, dtype=np.float32)
                                                        / np.float32(DR))).astype(np.float32)
    rank = ((LW + row % NSEL).astype(np.float32)[:, None] * theta[None, :]).astype(np.float64)
    c[:, C_RC:C_RC + HALF] = np.cos(rank)
    c[:, C_RS:C_RS + HALF] = np.sin(rank)
    c[:, C_ONES:C_ONES + P] = 1.0
    c[:, C_EPS] = LN_EPS
    q = np.arange(L)
    tq = (q.astype(np.float32)[:, None] * theta[None, :]).astype(np.float64)
    tk = q[:, None] * theta[None, :].astype(np.float64)
    tl = tq + np.maximum(q - (LW - 1), 0)[:, None] * theta[None, :].astype(np.float64)
    tab = np.stack([np.cos(tq), np.sin(tq), np.cos(tl), np.sin(tl), np.cos(tk), np.sin(tk)], 1)
    tab = tab.reshape(NT, P, 6, HALF).transpose(1, 2, 0, 3)
    return c, np.ascontiguousarray(tab.reshape(P, 6 * NT * HALF)).astype(np.float32)


def program(nc, dram, out):
    with ExitStack() as ctx:
        def sb(name, shape, dt=F32):
            return ctx.enter_context(nc.sbuf_tensor(name, shape, dt))

        def sem(name):
            return ctx.enter_context(nc.semaphore(name))

        key_rows = nc.dram_tensor("key_rows", (L, P), F32, kind="Internal").ap()
        val_rows_h = nc.dram_tensor("val_rows", (PAD + L, CKV), F32, kind="Internal")
        val_rows = val_rows_h.ap()
        xslots = nc.dram_tensor("xslots", (NSLOT, D), F32, kind="Internal").ap()
        yslots = nc.dram_tensor("yslots", (NSLOT, D), F32, kind="Internal").ap()

        cst = sb("cst", [P, C_N])
        ident = cst[:, C_ID:C_ID + P]
        ones = cst[:, C_ONES:C_ONES + P]
        tab = sb("tab", [P, 6, NT, HALF])
        rot = sb("rot", [P, 6, NT, HALF])
        rtmp = sb("rtmp", [P, 2, NT, HALF])
        rank_tab = sb("rank_tab", [P, 2, 2, HALF])
        raw = sb("raw", [P, HALF + 1])
        dlt = sb("dlt", [P, 8, HALF + 1])
        xT = sb("xT", [P, L])
        xr = sb("xr", [P, NT, D])
        w_idxq = sb("w_idxq", [P, 2 * P])
        w_idxk = sb("w_idxk", [P, P])
        w_kv = sb("w_kv", [P, DR + CKV])
        w_dq = sb("w_dq", [P, CQ])
        w_uqT = sb("w_uqT", [DH, NH, CQ])
        w_ukT = sb("w_ukT", [DH, NH, CKV])
        w_uvT = sb("w_uvT", [DH, NH, CKV])
        w_out = sb("w_out", [DH, NH, D])
        w_q = sb("w_q", [CQ, 2 * NH * DR])
        w_vo = sb("w_vo", [CKV, NH, D])
        w_i = sb("w_i", [P, NIH])
        w_router = sb("w_router", [P, E0])
        kiT = sb("kiT", [P, L])
        qiT = sb("qiT", [P, 2, L])
        cq_region = sb("cq_region", [P, L])
        cqT = cq_region[0:CQ, :]
        klocT = sb("klocT", [P, PAD + L])
        kmu = sb("kmu", [P, NT, DR])
        G = sb("G", [P, 2, NG, P])
        grow = G[:, 1, 0:NT, :]
        lrow = G[:, 1, NT:2 * NT, :]
        idxf = sb("idxf", [P, NSEL], U32)
        idx = sb("idx", [P, NT, NG], U32)
        R = sb("R", [P, 2, NIH, CH])
        SC = sb("SC", [P, 2, L])
        top = sb("top", [P, 4, 8])
        QF = sb("QF", [P, NH, P])
        qe = sb("qe", [P, NH, 2, HALF])
        qmu = sb("qmu", [P, NH, 2, HALF])
        qt = sb("qt", [P, 4, NH * 2, HALF])
        Q = sb("Q", [P, 2, P, NH])
        KT = sb("KT", [P, 2, GPB, P])
        S = sb("S", [P, 2, NS])
        PR = sb("PR", [P, 4, 2 * P])
        PT = sb("PT", [P, 2, 2 * P])
        V = sb("V", [WIN, 2, NB, CKV])
        ot_region = sb("ot_region", [P, 2 * NB * QB * NH])
        OT = ot_region[0:CKV, :].rearrange("p (a b q h) -> p a b q h", a=2, b=NB, q=QB)
        nmin = sb("nmin", [P, 2])
        psumr = sb("psumr", [P, 4])
        rinv = sb("rinv", [P, 2])
        xa = sb("xa", [P, D])
        stats = sb("stats", [P, TPC, 6])
        mv = sb("mv", [P, TPC, 2])
        lnv = sb("lnv", [P, 2, TPC])
        x1 = sb("x1", [P, 4, D])
        x1T = sb("x1T", [P, P])
        r8 = sb("r8", [P, 8])
        r8i = sb("r8i", [P, 8], U32)
        rex = sb("rex", [P, E0])
        rlog = sb("rlog", [P, E0])
        rsm = sb("rsm", [P, 8])
        onehot = sb("onehot", [P, E0])
        ohsum = sb("ohsum", [P, E0])
        rjunk = sb("rjunk", [P, E0])
        gm = sb("gm", [P, NT])
        slot_in = sb("slot_in", [P, NT], U32)
        slot_out = sb("slot_out", [P, NT], U32)
        zrow = sb("zrow", [P, 5 * P])

        w_value = kiT[:, 0:D]
        w_gates = kiT[:, D:D * (1 + NGATE)]
        EW = 3 * EG * D
        w_ex = [region[:, EW * i:EW * (i + 1)].rearrange("p (w e n) -> p w e n", w=3, e=EG)
                for region, i in ((qiT[:, :, :].rearrange("p a n -> p (a n)"), 0),
                                  (qiT[:, :, :].rearrange("p a n -> p (a n)"), 1),
                                  (R[:, :, :, :].rearrange("p a h n -> p (a h n)"), 0),
                                  (R[:, :, :, :].rearrange("p a h n -> p (a h n)"), 1),
                                  (tab[:, :, :, :].rearrange("p a t f -> p (a t f)"), 0))]
        w_up = xT[:, 0:2 * NHC * H1].rearrange("p (a e n) -> p a e n", a=2, e=NHC)
        w_down = cq_region[0:H1, 0:NHC * D].rearrange("p (e n) -> p e n", e=NHC)
        gamma = cq_region[:, NHC * D:(NHC + 1) * D]
        beta = cq_region[:, (NHC + 1) * D:(NHC + 2) * D]
        w_g8 = cq_region[:, (NHC + 2) * D:(NHC + 2) * D + E1]

        psK = ctx.enter_context(nc.psum_tensor("psK", [P, CH], F32))
        psX = ctx.enter_context(nc.psum_tensor("psX", [P, CH], F32))
        psS = [ctx.enter_context(nc.psum_tensor(f"psS{i}", [P, CH], F32)) for i in range(2)]
        psP = ctx.enter_context(nc.psum_tensor("psP", [P, CH], F32))
        psI = [ctx.enter_context(nc.psum_tensor(f"psI{i}", [P, CH], F32)) for i in range(2)]
        psM = ctx.enter_context(nc.psum_tensor("psM", [P, CH], F32))
        PX = psX[:, 0:P]

        names = """ld_cst ld_tab ld_x ld_x2 ld_w ld_raw ld_late zeroed z_ready zslots kv_mm
            w_mm w_cp kproj kproj_cp rope_p lat_row mu_row key_l mu lrot kr_out val_out g_rot lT lT_cp rope rope_a
            i_mm i_relu i_first comb im topk idx_ready q_mm q_e q_chain qf_a q_t q_cp
            k_t k_ev s_mm s_min p_exp p_t p_cp pv orec p_nrm o_cp v_ld
            y_mm y_add bn ln_a x1_n x1d x1_t x1_cp lg_mm lg_e rt_a rt cum_mm lg_cp rte plc slots_ready ld_l1""".split()
        s = {n: sem("s_" + n) for n in names}
        s_we = [sem(f"s_we{i}") for i in range(NEW)]
        s_sct = [sem(f"s_sct{i}") for i in range(4)]
        s_g = [[sem(f"s_g{i}_{b}") for b in range(NB)] for i in range(2)]

        CHUNKS = L // CH

        index_pairs, index_steps = index_plan()

        def load_experts(sp, k):
            for i, w in enumerate(("w_gate", "w_up", "w_down")):
                sp.dma_start(w_ex[k % NEW][:, i, :, :],
                             dram[w][EG * k:EG * (k + 1)].rearrange("e h f -> h e f")).then_inc(s_we[k % NEW], 16)

        def rotary_angles(eng, link, tmp, tables):
            cd = dlt[:, 6:7, 0:HALF].to_broadcast([P, NT, HALF])
            sd = dlt[:, 7:8, 0:HALF].to_broadcast([P, NT, HALF])
            for k in tables:
                c, sn = tab[:, 2 * k, :, :], tab[:, 2 * k + 1, :, :]
                for dst, a, b, op in ((2 * k, c, sn, ALU.subtract), (2 * k + 1, sn, c, ALU.add)):
                    link(eng.tensor_tensor(tmp[:, 0, :, :], a, cd, ALU.mult))
                    link(eng.tensor_tensor(tmp[:, 1, :, :], b, sd, ALU.mult))
                    link(eng.tensor_tensor(rot[:, dst, :, :], tmp[:, 0, :, :], tmp[:, 1, :, :], op))

        def proj_banks(c):
            return [psI[0], psI[1], psK, psX] if c == 0 else [psS[1], psP, psK, psX]

        def scatter(pool, t):
            pool.wait_ge(s["slots_ready"], t + 1)
            pool.indirect_dma_start(
                xslots, bass.IndirectOffsetOnAxis(ap=slot_in[:, t:t + 1], axis=0), x1[:, t % 4, :], None,
                bounds_check=NSLOT - 1, oob_is_err=False).then_inc(s_sct[t % 4], 16)

        with nc.Block() as block:
            @block.sync
            def _(sp):
                sp.dma_start(w_idxk[:, 0:DH], dram["idx_wk"]).then_inc(s["ld_w"], 16)
                sp.dma_start(w_idxk[:, DH:P], dram["idx_wk"]).then_inc(s["ld_w"], 16)
                sp.dma_start(xT[:, 0:CH], dram["xT"][:, 0:CH]).then_inc(s["ld_x"], 16)
                sp.dma_start(w_idxq[:, :], dram["idx_wq"]).then_inc(s["ld_w"], 16)
                sp.dma_start(w_dq[:, :], dram["W_dq"]).then_inc(s["ld_w"], 16)
                sp.dma_start(w_kv[:, 0:DR], dram["W_kr"]).then_inc(s["ld_w"], 16)
                sp.dma_start(w_kv[:, DR:DR + CKV], dram["W_dkv"]).then_inc(s["ld_w"], 16)
                sp.dma_start(w_i[:, :], dram["idx_w"]).then_inc(s["ld_w"], 16)
                sp.dma_start(raw[:, :], dram["raw"]).then_inc(s["ld_raw"], 16)
                sp.dma_start(xT[:, CH:], dram["xT"][:, CH:]).then_inc(s["ld_x2"], 16)
                sp.dma_start(cst[:, :], dram["cst"]).then_inc(s["ld_cst"], 16)
                sp.dma_start(tab[:, :, :, :], dram["tab"]).then_inc(s["ld_tab"], 16)
                sp.dma_start(w_uqT[:, :, :], dram["W_uqT"]).then_inc(s["ld_late"], 16)
                sp.dma_start(w_ukT[:, :, :], dram["W_ukT"]).then_inc(s["ld_late"], 16)
                sp.dma_start(w_uvT[:, :, :], dram["W_uvT"]).then_inc(s["ld_late"], 16)
                sp.dma_start(w_out[:, :, :], dram["W_out"]).then_inc(s["ld_late"], 16)
                sp.dma_start(w_q[:, NH * CKV:], dram["W_qr"]).then_inc(s["ld_late"], 16)
                sp.dma_start(w_router[:, :], dram["w_router"]).then_inc(s["ld_late"], 16)
                sp.dma_start(xr[:, :, :], dram["x"]).then_inc(s["ld_late"], 16)
                sp.wait_ge(s["z_ready"], 1)
                sp.dma_start(val_rows[0:PAD, :], zrow[0:PAD, 0:CKV]).then_inc(s["val_out"], 16)
                for i in range(4):
                    n = NSLOT // 4
                    sp.dma_start(xslots[n * i:n * (i + 1), :].rearrange("(p r) d -> p (r d)", p=P),
                                 zrow[:, :]).then_inc(s["zslots"], 16)
                sp.wait_ge(s["mu_row"], 2)
                sp.wait_ge(s["zeroed"], 5)
                sp.wait_ge(s["lat_row"], 4)
                sp.dma_start(key_rows.rearrange("(t p) d -> p t d", p=P), grow).then_inc(s["kr_out"], 16)
                sp.dma_start(val_rows[PAD:, :].rearrange("(t p) d -> p t d", p=P),
                             grow[:, :, 3 * DR:]).then_inc(s["val_out"], 16)
                sp.wait_ge(s["val_out"], 32)
                for t in range(NT):
                    if t >= 2:
                        sp.wait_ge(s["pv"], NB * (t - 1))
                    if t == 0:
                        for b in range(4):
                            sp.dma_start(V[:, 0, b, :], val_rows[PAD:PAD + WIN, :]).then_inc(s["v_ld"], 16)
                        src = bass.AP(val_rows_h, 4 * QB * CKV, [[CKV, WIN], [QB * CKV, NB - 4], [1, CKV]])
                        sp.dma_start(V[:, 0, 4:, :], src).then_inc(s["v_ld"], 16)
                    else:
                        src = bass.AP(val_rows_h, P * t * CKV, [[CKV, WIN], [QB * CKV, NB], [1, CKV]])
                        sp.wait_ge(s["v_ld"], 16 * (4 + t))
                        sp.dma_start(V[:, t % 2, :, :], src).then_inc(s["v_ld"], 16)
                sp.wait_ge(s["i_relu"], 4 * chunk_base(NT))
                sp.wait_ge(s["comb"], 3 * chunk_base(NT))
                sp.dma_start(w_value, dram["value_W"]).then_inc(s["ld_l1"], 16)
                sp.dma_start(w_gates, dram["gate_W"]).then_inc(s["ld_l1"], 16)
                sp.dma_start(w_up[:, 0, 0:E1, :], dram["W1"]).then_inc(s["ld_l1"], 16)
                sp.dma_start(w_up[:, 1, 0:E1, :], dram["W3"]).then_inc(s["ld_l1"], 16)
                sp.dma_start(w_up[:, 0, E1:, :], dram["Ws1"]).then_inc(s["ld_l1"], 16)
                sp.dma_start(w_up[:, 1, E1:, :], dram["Ws3"]).then_inc(s["ld_l1"], 16)
                for k in range(NEW):
                    load_experts(sp, k)
                sp.wait_ge(s["q_mm"], NT)
                sp.dma_start(w_down[:, 0:E1, :], dram["W2"]).then_inc(s["ld_l1"], 16)
                sp.dma_start(w_down[:, E1:, :], dram["Ws2"]).then_inc(s["ld_l1"], 16)
                sp.dma_start(gamma, dram["gamma"]).then_inc(s["ld_l1"], 16)
                sp.dma_start(beta, dram["beta"]).then_inc(s["ld_l1"], 16)
                sp.dma_start(w_g8, dram["Wg"]).then_inc(s["ld_l1"], 16)
                sp.wait_ge(s["ld_l1"], 16 * 11)
                for k in range(NEW):
                    sp.wait_ge(s_we[k], 16 * 3)

            @block.gpsimd
            def _(pool):
                pool.memset(zrow[:, :], 0.0).then_inc(s["z_ready"], 1)
                pool.memset(ohsum[:, :], 0.0).then_inc(s["zeroed"], 1)
                pool.memset(klocT[:, 0:PAD], 0.0).then_inc(s["zeroed"], 1)
                pool.memset(PR[:, :, NS:], 0.0).then_inc(s["zeroed"], 1)
                pool.memset(lrow[:, :, 0:2 * DR], 0.0).then_inc(s["zeroed"], 1)
                pool.memset(grow[:, :, 2 * DR:3 * DR], 0.0).then_inc(s["zeroed"], 1)
                done = [0]

                def link(ins):
                    done[0] += 1
                    ins.then_inc(s["rope_p"], 1)
                    pool.wait_ge(s["rope_p"], done[0])

                pool.wait_ge(s["rope"], 6)
                pool.wait_ge(s["ld_tab"], 16)
                rotary_angles(pool, link, QF[:, 0:4, :].rearrange("p a (b f) -> p (a b) f", f=HALF).rearrange(
                    "p (a t) f -> p a t f", a=2), (2, 0))
                pool.wait_ge(s["kr_out"], 16)
                for t in range(NT):
                    pool.wait_ge(s["idx_ready"], t + 1)
                    if t == 1:
                        pool.wait_ge(s["lT"], NT)
                        pool.wait_ge(s["val_out"], 32)
                    for g in range(NG):
                        b = g // GPB
                        if t >= 2 and g % GPB == 0:
                            pool.wait_ge(s["pv"], NB * (t - 2) + b + 1)
                        pool.indirect_dma_start(
                            G[:, t % 2, g, :], None, key_rows,
                            bass.IndirectOffsetOnAxis(ap=idx[:, t, g:g + 1], axis=0),
                        ).then_inc(s_g[t % 2][b], 16)
                    if t == 4:
                        pool.wait_ge(s["zslots"], 64)
                    if t >= 4:
                        scatter(pool, t - 4)
                for t in range(NT - 4, NT):
                    scatter(pool, t)
                for i in range(4):
                    pool.wait_ge(s_sct[i], 16 * NT // 4)

            @block.tensor
            def _(pe):
                def index_pair(t, u):
                    c, pair = u // 2, u % 2
                    w = min(CH, keys_of(t) - CH * c)
                    m = 2 * chunk_base(t) + u
                    if m == 0:
                        pe.wait_ge(s["kproj_cp"], 4)
                    else:
                        pe.wait_ge(s["i_relu"], 2 * m)
                    for i in range(2):
                        lhs = qiT[64 * i:64 * i + 64, pair, P * t:P * (t + 1)]
                        pe.matmul(psI[i][:, 0:w], lhs, kiT[64 * i:64 * i + 64, CH * c:CH * c + w],
                                  start=True, stop=True).then_inc(s["i_mm"], 1)

                pe.wait_ge(s["ld_w"], 16 * 7)
                pe.wait_ge(s["ld_x"], 16)
                def project(c):
                    for i, (lhs, rows) in enumerate(((w_idxk[:, :], P), (w_idxq[:, 0:P], P), (w_idxq[:, P:2 * P], P),
                                                     (w_dq[:, :], CQ))):
                        n = 4 * c + i
                        if n >= 4:
                            pe.wait_ge(s["kproj_cp"], n - 3)
                        pe.matmul(proj_banks(c)[i][0:rows, :], lhs, xT[:, CH * c:CH * (c + 1)],
                                  start=True, stop=True).then_inc(s["kproj"], 1)

                project(0)
                pe.wait_ge(s["ld_x2"], 16)
                for h in range(2):
                    for i in range(8):
                        t = 8 * h + i
                        mm = pe.matmul([psS[0], psM][h][:, 64 * i:64 * i + 64], xT[:, P * t:P * (t + 1)], w_kv[:, :],
                                       start=True, stop=True, skip_group_check=True)
                    mm.then_inc(s["kv_mm"], 1)
                for u in range(2):
                    index_pair(0, u)
                for c in range(1, CHUNKS):
                    project(c)
                pe.wait_ge(s["kproj_cp"], 4 * CHUNKS)
                pe.wait_ge(s["ld_late"], 16 * 7)
                for h in range(NH):
                    mm = pe.matmul(psP[0:CQ, CKV * h:CKV * (h + 1)], w_uqT[:, h, :], w_ukT[:, h, :],
                                   start=True, stop=True, skip_group_check=True)
                mm.then_inc(s["w_mm"], 1)
                for j in range(2):
                    pe.wait_ge(s["w_cp"], 1 + j)
                    for h in range(4):
                        mm = pe.matmul(psP[0:CKV, D * h:D * (h + 1)], w_uvT[:, 4 * j + h, :], w_out[:, 4 * j + h, :],
                                       start=True, stop=True, skip_group_check=True)
                    mm.then_inc(s["w_mm"], 1)

                def q_project(t):
                    if t == 0:
                        pe.wait_ge(s["w_cp"], 3)
                        pe.wait_ge(s["kproj_cp"], 4 * CHUNKS)
                        pe.wait_ge(s["lat_row"], 4)
                        pe.wait_ge(s["mu"], 4)
                    if t >= 1:
                        pe.wait_ge(s["q_cp"], 2 * t)
                    pe.matmul(psM[:, :], cqT[:, P * t:P * (t + 1)], w_q[:, :], start=True,
                              stop=True).then_inc(s["q_mm"], 1)

                def q_transpose(t, j):
                    if j == 0:
                        pe.wait_ge(s["q_chain"], 10 * (t + 1))
                        pe.wait_ge(s["qf_a"], 3 * (t + 1))
                    else:
                        pe.wait_ge(s["q_cp"], 2 * t + 1)
                    for h in range(4):
                        mm = pe.transpose(psM[:, P * h:P * (h + 1)], QF[:, 4 * j + h, :], ident)
                    mm.then_inc(s["q_t"], 1)

                def front(n):
                    t, b = divmod(n, NB)
                    pe.wait_ge(s["g_rot"], n + 1)
                    if n >= 1:
                        pe.wait_ge(s["k_ev"], n)
                    else:
                        pe.wait_ge(s["lT_cp"], NT // 4)
                    for j in range(GPB):
                        mm = pe.transpose(psK[:, P * j:P * (j + 1)], G[:, t % 2, GPB * b + j, :], ident)
                    mm.then_inc(s["k_t"], 1)

                def scores(n):
                    t, b = divmod(n, NB)
                    pe.wait_ge(s["k_ev"], n + 1)
                    pe.wait_ge(s["q_cp"], 2 * t + 2)
                    if n >= 2:
                        pe.wait_ge(s["s_min"], n - 1)
                    ps = psS[n % 2]
                    qb = Q[:, t % 2, QB * b:QB * (b + 1), :].rearrange("p q h -> p (q h)")
                    for j in range(GPB):
                        pe.matmul(ps[32 * j:32 * j + 32, 0:P], qb[:, 32 * j:32 * j + 32], KT[:, n % 2, j, :],
                                  start=True, stop=True, skip_group_check=True)
                    w0 = PAD if t == 0 and b < 4 else P * t + QB * b
                    pe.matmul(ps[:, P:NS], qb, klocT[:, w0:w0 + WIN],
                              start=True, stop=True, skip_group_check=True).then_inc(s["s_mm"], 1)

                def p_transpose(n):
                    pe.wait_ge(s["p_nrm"], n + 1)
                    if n >= 1:
                        pe.wait_ge(s["p_cp"], n)
                    if n >= 2:
                        pe.wait_ge(s["o_cp"], n - 1)
                    for i in range(2):
                        mm = pe.transpose(psP[:, P * i:P * (i + 1)], PR[:, n % 4, P * i:P * (i + 1)], ident)
                    mm.then_inc(s["p_t"], 1)

                def weighted(n):
                    t, b = divmod(n, NB)
                    pe.wait_ge(s["p_cp"], n + 1)
                    pe.wait_ge(s["v_ld"], 16 * (5 + t))
                    if n >= 1:
                        pe.wait_ge(s["o_cp"], n)
                    o = psP[0:CKV, 2 * P:3 * P]
                    pe.matmul(o, V[:, t % 2, b, :], PT[0:WIN, n % 2, P:2 * P], start=True, stop=False,
                              skip_group_check=True)
                    for j in range(GPB):
                        mm = pe.matmul(o[:, 32 * j:32 * j + 32], G[:, t % 2, GPB * b + j, 3 * DR:],
                                       PT[:, n % 2, 32 * j:32 * j + 32], start=False, stop=(j == GPB - 1),
                                       skip_group_check=True)
                    mm.then_inc(s["pv"], 1)

                def out_project(t):
                    pe.wait_ge(s["o_cp"], NB * (t + 1))
                    if t >= 1:
                        pe.wait_ge(s["rte"], t)
                    for h in range(NH):
                        mm = pe.matmul(PX, OT[:, t % 2, :, :, h].rearrange("p b q -> p (b q)"), w_vo[:, h, :],
                                       start=(h == 0), stop=(h == NH - 1), skip_group_check=True)
                    mm.then_inc(s["y_mm"], 1)

                def x1_transpose(t):
                    pe.wait_ge(s["x1_n"], t + 1)
                    pe.transpose(PX, x1[:, t % 4, :], ident).then_inc(s["x1_t"], 1)

                def router(t):
                    pe.wait_ge(s["x1_cp"], t + 1)
                    pe.matmul(PX[:, 0:E0], x1T[:, :], w_router[:, :], start=True, stop=True,
                              skip_group_check=True).then_inc(s["lg_mm"], 1)

                def cumulate(t):
                    pe.wait_ge(s["rt"], 5 * t + 4)
                    pe.matmul(PX[:, E0:2 * E0], cst[:, C_TRI:C_TRI + P], onehot[:, :], start=True, stop=False,
                              skip_group_check=True)
                    pe.matmul(PX[:, E0:2 * E0], ones, ohsum[:, :], start=False, stop=True,
                              skip_group_check=True).then_inc(s["cum_mm"], 1)

                for n in range(N0, N1):
                    st, b = divmod(n, NB)
                    if 0 <= n - 7 < NT * NB:
                        p_transpose(n - 7)
                    if 0 <= n - 8 < NT * NB:
                        weighted(n - 8)
                    if 0 <= n < NT * NB:
                        front(n)
                    if 0 <= n - 2 < NT * NB:
                        scores(n - 2)
                    if n == -NB:
                        for i in range(NT // 4):
                            if i == 0:
                                pe.wait_ge(s["lrot"], 2)
                                pe.wait_ge(s["lat_row"], 4)
                                pe.wait_ge(s["zeroed"], 5)
                            if i >= 2:
                                pe.wait_ge(s["lT_cp"], i - 1)
                            for j in range(4):
                                pe.transpose([psK, psP][i % 2][:, P * j:P * (j + 1)], lrow[:, 4 * i + j, :],
                                             ident).then_inc(s["lT"], 1)
                    for t, u in index_pairs.get(n, ()):
                        index_pair(t, u)
                    if 0 <= st + 1 < NT:
                        if b == 4:
                            q_transpose(st + 1, 0)
                        if b == 5:
                            q_transpose(st + 1, 1)
                    if 0 <= st + 2 < NT and b == 7:
                        q_project(st + 2)
                    if 0 <= st - 2 < NT:
                        if b == 0:
                            out_project(st - 2)
                        if b == 3:
                            x1_transpose(st - 2)
                        if b == 4:
                            router(st - 2)
                        if b == 6:
                            cumulate(st - 2)

            @block.scalar
            def _(act):
                def relu_pair(t, u):
                    c, pair = u // 2, u % 2
                    w = min(CH, keys_of(t) - CH * c)
                    m = 2 * chunk_base(t) + u
                    if m // 2 >= 2:
                        act.wait_ge(s["comb"], 3 * (m // 2 - 1))
                    for i in range(2):
                        act.wait_ge(s["i_mm"], 2 * m + i + 1)
                        act.activation(R[:, (m // 2) % 2, 2 * pair + i, 0:w], psI[i][:, 0:w],
                                       ACT.Relu).then_inc(s["i_relu"], 1)
                    if pair == 0:
                        if c == 0 and t >= 2:
                            act.wait_ge(s["topk"], TOP_STEPS * (t - 1))
                        act.wait_ge(s["i_relu"], 2 * m + 1)
                        act.activation(SC[:, t % 2, CH * c:CH * c + w], R[:, (m // 2) % 2, 0, 0:w], ACT.Copy,
                                       scale=w_i[:, 0:1]).then_inc(s["i_first"], 1)

                act.wait_ge(s["ld_raw"], 16)
                act.activation(dlt[:, 0, :], raw[:, :], ACT.Exp, scale=-1.0).then_inc(s["rope_a"], 1)
                act.wait_ge(s["rope"], 3)
                act.activation(dlt[:, 3, :], dlt[:, 2, :], ACT.Sin).then_inc(s["rope_a"], 1)
                act.activation(dlt[:, 4, :], dlt[:, 2, :], ACT.Sin, scale=0.5).then_inc(s["rope_a"], 1)
                act.preload_act_table_set("natural_log_exp_and_others")
                def projected(c):
                    for i, (dst, rows) in enumerate(((kiT[:, :], P), (qiT[:, 0, :], P), (qiT[:, 1, :], P),
                                                     (cqT[:, :], CQ))):
                        act.wait_ge(s["kproj"], 4 * c + i + 1)
                        to, src = dst[:, CH * c:CH * (c + 1)], proj_banks(c)[i][0:rows, :]
                        if i in (1, 2):
                            to = to.rearrange("p (t a g) -> p t a g", t=TPC, a=GPB)
                            src = src.rearrange("p (t g a) -> p t a g", t=TPC, a=GPB)
                        act.activation(to, src, ACT.Copy).then_inc(s["kproj_cp"], 1)

                projected(0)
                for h in range(2):
                    act.wait_ge(s["mu"], h + 1)
                    m = kmu[:, 8 * h:8 * h + 8, :]
                    act.activation(m, m, ACT.Exp).then_inc(s["key_l"], 1)
                    act.wait_ge(s["key_l"], 2 * h + 1)
                    act.activation(m, m, ACT.Ln, bias=1.0).then_inc(s["key_l"], 1)
                act.wait_ge(s["mu"], 2)
                for dst in (grow, lrow):
                    for h in range(2):
                        src = [psS[0], psM][h][:, :].rearrange("p (t d) -> p t d", d=64)[:, :, DR:]
                        act.activation(dst[:, 8 * h:8 * h + 8, 3 * DR:], src, ACT.Copy).then_inc(s["lat_row"], 1)
                    if dst is grow:
                        for u in range(2):
                            relu_pair(0, u)
                for c in range(1, CHUNKS):
                    projected(c)
                act.wait_ge(s["w_mm"], 1)
                act.activation(w_q[:, 0:NH * CKV], psP[0:CQ, 0:NH * CKV], ACT.Copy).then_inc(s["w_cp"], 1)
                for j in range(2):
                    act.wait_ge(s["w_mm"], 2 + j)
                    act.activation(w_vo[:, 4 * j:4 * j + 4, :].rearrange("p h d -> p (h d)"), psP[0:CKV, :],
                                   ACT.Copy).then_inc(s["w_cp"], 1)

                def q_softplus(t):
                    act.wait_ge(s["q_chain"], 10 * t + 1)
                    if t == 0:
                        act.wait_ge(s["rope_p"], 12)
                    if t >= 1:
                        act.wait_ge(s["q_t"], 2 * t)
                    act.activation(QF[:, :, 3 * DR:], psM[:, 0:NH * CKV].rearrange("p (h d) -> p h d", h=NH),
                                   ACT.Copy, scale=-SCALE).then_inc(s["qf_a"], 1)
                    act.activation(qe[:, :, :, :], qe[:, :, :, :], ACT.Exp).then_inc(s["q_e"], 1)
                    act.wait_ge(s["q_e"], 2 * t + 1)
                    act.activation(qe[:, :, :, :], qe[:, :, :, :], ACT.Ln, bias=1.0).then_inc(s["q_e"], 1)

                def q_copies(t):
                    act.wait_ge(s["q_chain"], 10 * t + 6)
                    act.activation(QF[:, :, DR:DR + HALF], QF[:, :, HALF:DR], ACT.Copy).then_inc(s["qf_a"], 1)
                    act.activation(QF[:, :, DR + HALF:2 * DR], QF[:, :, 0:HALF], ACT.Copy,
                                   scale=-1.0).then_inc(s["qf_a"], 1)

                def q_evac(t, j):
                    act.wait_ge(s["q_t"], 2 * t + j + 1)
                    if t >= 2 and j == 0:
                        act.wait_ge(s["s_mm"], NB * (t - 1))
                    act.activation(Q[:, t % 2, :, 4 * j:4 * j + 4].rearrange("p q h -> p h q"),
                                   psM[:, :].rearrange("p (h q) -> p h q", h=4), ACT.Copy).then_inc(s["q_cp"], 1)

                def exps(n):
                    act.wait_ge(s["s_min"], n + 1)
                    if n == 0:
                        act.wait_ge(s["zeroed"], 5)
                    if n >= 4:
                        act.wait_ge(s["p_t"], n - 3)
                    act.activation(PR[:, n % 4, 0:NS], S[:, n % 2, :], ACT.Exp, bias=nmin[:, n % 2:n % 2 + 1],
                                   scale=-1.0, accum_out=psumr[:, n % 4:n % 4 + 1]).then_inc(s["p_exp"], 1)

                def p_norm(n):
                    act.wait_ge(s["orec"], n + 1)
                    pr = PR[:, n % 4, 0:NS]
                    act.activation(pr, pr, ACT.Copy, scale=rinv[:, n % 2:n % 2 + 1]).then_inc(s["p_nrm"], 1)

                def k_copy(n):
                    act.wait_ge(s["k_t"], n + 1)
                    if n >= 2:
                        act.wait_ge(s["s_mm"], n - 1)
                    act.activation(KT[:, n % 2, :, :].rearrange("p g i -> p (g i)"), psK[:, :],
                                   ACT.Copy).then_inc(s["k_ev"], 1)

                def p_copy(n):
                    act.wait_ge(s["p_t"], n + 1)
                    if n >= 1:
                        act.wait_ge(s["pv"], n)
                    act.activation(PT[:, n % 2, :], psP[:, 0:2 * P], ACT.Copy).then_inc(s["p_cp"], 1)

                def o_copy(n):
                    t, b = divmod(n, NB)
                    act.wait_ge(s["pv"], n + 1)
                    if b == 0 and t >= 2:
                        act.wait_ge(s["y_mm"], t - 1)
                    act.activation(OT[:, t % 2, b, :, :].rearrange("p q h -> p (q h)"), psP[0:CKV, 2 * P:3 * P],
                                   ACT.Copy).then_inc(s["o_cp"], 1)

                def norm_scale(t):
                    act.wait_ge(s["bn"], 2 * t + 2)
                    act.activation(lnv[:, 0, 0:1], mv[:, 0, 1:2], ACT.Ln,
                                   bias=cst[:, C_EPS:C_EPS + 1]).then_inc(s["ln_a"], 1)
                    act.wait_ge(s["ln_a"], 2 * t + 1)
                    act.activation(lnv[:, 1, 0:1], lnv[:, 0, 0:1], ACT.Exp, scale=-0.5).then_inc(s["ln_a"], 1)

                def x1_copy(t):
                    act.wait_ge(s["x1_n"], t + 1)
                    act.activation(xr[:, t, :], x1[:, t % 4, :], ACT.Copy, scale=2.0).then_inc(s["x1d"], 1)
                    act.wait_ge(s["x1_t"], t + 1)
                    act.activation(x1T[:, :], PX, ACT.Copy).then_inc(s["x1_cp"], 1)

                def gate_exp(t):
                    act.wait_ge(s["rt"], 5 * t + 1)
                    act.activation(rex[:, :], rlog[:, :], ACT.Exp, bias=rsm[:, 0:1],
                                   accum_out=rsm[:, 1:2]).then_inc(s["lg_e"], 1)

                for n in range(N0, N1):
                    st, b = divmod(n, NB)
                    if 0 <= n - 7 < NT * NB:
                        p_copy(n - 7)
                    if 0 <= n - 8 < NT * NB:
                        o_copy(n - 8)
                    for t, u in index_pairs.get(n - 1, ()):
                        relu_pair(t, u)
                    if 0 <= n - 4 < NT * NB:
                        exps(n - 4)
                    if 0 <= n - 6 < NT * NB:
                        p_norm(n - 6)
                    if 0 <= n < NT * NB:
                        k_copy(n)
                    if n == -NB:
                        for i in range(NT // 4):
                            act.wait_ge(s["lT"], 4 * i + 4)
                            act.activation(klocT[:, PAD + CH * i:PAD + CH * (i + 1)], [psK, psP][i % 2][:, :],
                                           ACT.Copy).then_inc(s["lT_cp"], 1)
                    if 0 <= st + 1 < NT:
                        if b == 1:
                            q_softplus(st + 1)
                        if b == 3:
                            q_copies(st + 1)
                        if b == 5:
                            q_evac(st + 1, 0)
                        if b == 6:
                            q_evac(st + 1, 1)
                    if 0 <= st - 2 < NT:
                        if b == 1:
                            norm_scale(st - 2)
                        if b == 4:
                            x1_copy(st - 2)
                        if b == 6:
                            gate_exp(st - 2)

            @block.vector
            def _(dve):
                def combine(t, c):
                    w = min(CH, keys_of(t) - CH * c)
                    m = chunk_base(t) + c
                    dst = SC[:, t % 2, CH * c:CH * c + w]
                    dve.wait_ge(s["i_first"], m + 1)
                    dve.wait_ge(s["i_relu"], 4 * (m + 1))
                    for h in range(1, NIH):
                        if h > 1:
                            dve.wait_ge(s["comb"], 3 * m + h - 1)
                        dve.scalar_tensor_tensor(out=dst, in0=R[:, m % 2, h, 0:w], scalar=w_i[:, h:h + 1], in1=dst,
                                                 op0=ALU.mult, op1=ALU.add).then_inc(s["comb"], 1)

                def index_mask(t):
                    dve.wait_ge(s["comb"], 3 * chunk_base(t + 1))
                    lo = keys_of(t) - P
                    m = C_IM0 if t == 0 else C_IM
                    dst = SC[:, t % 2, lo:lo + P]
                    dve.tensor_tensor(dst, dst, cst[:, m:m + P], ALU.add).then_inc(s["im"], 1)

                def topk_step(t, k):
                    r, what = divmod(k, 3)
                    a = SC[:, t % 2, 0:keys_of(t)]
                    if k == 0:
                        dve.wait_ge(s["im"], t + 1)
                    if k > 0:
                        dve.wait_ge(s["topk"], TOP_STEPS * t + k)
                    if k == 11:
                        dve.transpose(idx[:, t, :], idxf[:, :]).then_inc(s["topk"], 1)
                        dve.wait_ge(s["topk"], TOP_STEPS * (t + 1))
                        dve.sem_inc(s["idx_ready"], 1)
                        return
                    if what == 0:
                        ins = dve.max(out=top[:, r, :], in_=a)
                    elif what == 1:
                        ins = dve.max_index(out=idxf[:, 8 * r:8 * r + 8], in_max=top[:, r, :], in_values=a)
                    else:
                        ins = dve.match_replace(out=a, in_to_replace=top[:, r, :], in_values=a, imm_value=LOW)
                    ins.then_inc(s["topk"], 1)

                rope = [0]

                def link(ins):
                    rope[0] += 1
                    ins.then_inc(s["rope"], 1)
                    dve.wait_ge(s["rope"], rope[0])

                dve.wait_ge(s["rope_a"], 1)
                link(dve.tensor_scalar(dlt[:, 0, :], dlt[:, 0, :], 1.0, None, ALU.add))
                link(dve.reciprocal(dlt[:, 1, :], dlt[:, 0, :]))
                link(dve.tensor_scalar(dlt[:, 2, :], dlt[:, 1, :], float(-2 * np.pi), float(np.pi),
                                       ALU.mult, ALU.add))
                dve.wait_ge(s["rope_a"], 3)
                link(dve.tensor_tensor(dlt[:, 5, :], dlt[:, 4, :], dlt[:, 4, :], ALU.mult))
                link(dve.tensor_scalar(dlt[:, 6, :], dlt[:, 5, :], 2.0, -1.0, ALU.mult, ALU.add))
                link(dve.tensor_scalar(dlt[:, 7, :], dlt[:, 3, :], -1.0, None, ALU.mult))
                for h in range(2):
                    dve.wait_ge(s["kv_mm"], h + 1)
                    kr = [psS[0], psM][h][:, :].rearrange("p (t d) -> p t d", d=64)[:, :, 0:DR]
                    dve.tensor_scalar(kmu[:, 8 * h:8 * h + 8, :], kr, 30.0, None, ALU.min).then_inc(s["mu"], 1)
                for h in range(2):
                    dve.wait_ge(s["key_l"], 2 * h + 2)
                    dve.wait_ge(s["lat_row"], 4)
                    m = kmu[:, 8 * h:8 * h + 8, :]
                    kr = [psS[0], psM][h][:, :].rearrange("p (t d) -> p t d", d=64)[:, :, 0:DR]
                    dve.tensor_tensor(m, m, kr, ALU.max).then_inc(s["mu"], 1)
                dve.wait_ge(s["mu"], 4)
                for i in range(2):
                    dve.tensor_copy(grow[:, :, DR * i:DR * (i + 1)], kmu[:, :, :]).then_inc(s["mu_row"], 1)
                combine(0, 0)
                dve.wait_ge(s["ld_cst"], 16)
                index_mask(0)
                for i in range(TOP_STEPS):
                    topk_step(0, i)
                dve.wait_ge(s["ld_late"], 16 * 7)
                dve.wait_ge(s["ld_tab"], 16)
                dve.wait_ge(s["ld_cst"], 16)
                cr, sr = (cst[:, None, a:a + HALF].to_broadcast([P, 2, HALF]) for a in (C_RC, C_RS))
                cd, sd = (dlt[:, i:i + 1, 0:HALF].to_broadcast([P, 2, HALF]) for i in (6, 7))
                for k, (a, b, op) in enumerate(((cr, sr, ALU.subtract), (sr, cr, ALU.add))):
                    link(dve.tensor_tensor(rtmp[:, 0, 0:2, :], a, cd, ALU.mult))
                    link(dve.tensor_tensor(rtmp[:, 1, 0:2, :], b, sd, ALU.mult))
                    link(dve.tensor_tensor(rank_tab[:, k, :, :], rtmp[:, 0, 0:2, :], rtmp[:, 1, 0:2, :], op))
                rotary_angles(dve, link, rtmp[:, :, :, :], (1,))
                dve.wait_ge(s["rope_p"], 12)
                link(dve.tensor_scalar(rot[:, 0:4, :, :].rearrange("p a t f -> p (a t f)"),
                                       rot[:, 0:4, :, :].rearrange("p a t f -> p (a t f)"), -SCALE, None, ALU.mult))
                m1, m2 = kmu[:, :, 0:HALF], kmu[:, :, HALF:DR]
                ck, sk = rot[:, 4, :, :], rot[:, 5, :, :]
                for i, (a, b, op) in enumerate(((m1, m2, ALU.subtract), (m2, m1, ALU.add))):
                    link(dve.tensor_tensor(rtmp[:, 0, :, :], a, ck, ALU.mult))
                    link(dve.tensor_tensor(rtmp[:, 1, :, :], b, sk, ALU.mult))
                    dve.tensor_tensor(lrow[:, :, 2 * DR + HALF * i:2 * DR + HALF * (i + 1)], rtmp[:, 0, :, :],
                                      rtmp[:, 1, :, :], op).then_inc(s["lrot"], 1)
                    dve.wait_ge(s["lrot"], i + 1)

                def q_min(t):
                    dve.wait_ge(s["q_mm"], t + 1)
                    if t >= 1:
                        dve.wait_ge(s["q_chain"], 10 * t)
                    dve.tensor_scalar(qe[:, :, :, :], psM[:, NH * CKV:].rearrange("p (h k f) -> p h k f", h=NH, k=2),
                                      30.0, None, ALU.min).then_inc(s["q_chain"], 1)

                def q_rotate(t, part):
                    base = 10 * t
                    if part == 0:
                        dve.wait_ge(s["q_e"], 2 * t + 2)
                        dve.wait_ge(s["qf_a"], 3 * t + 1)
                        dve.tensor_tensor(qmu[:, :, :, :], qe[:, :, :, :],
                                          psM[:, NH * CKV:].rearrange("p (h k f) -> p h k f", h=NH, k=2),
                                          ALU.max).then_inc(s["q_chain"], 1)
                        dve.wait_ge(s["q_chain"], base + 2)
                    mu2d = qmu[:, :, :, :].rearrange("p h k f -> p (h k) f")
                    for k in (2 * part, 2 * part + 1):
                        dve.tensor_tensor(qt[:, k, :, :], mu2d,
                                          rot[:, k:k + 1, t, :].to_broadcast([P, NH * 2, HALF]),
                                          ALU.mult).then_inc(s["q_chain"], 1)
                    dve.wait_ge(s["q_chain"], base + (4 if part == 0 else 8))
                    tc = qt[:, 2 * part, :, :].rearrange("p (h k) f -> p h k f", k=2)
                    ts = qt[:, 2 * part + 1, :, :].rearrange("p (h k) f -> p h k f", k=2)
                    o = 2 * DR * part
                    if t >= 1:
                        dve.wait_ge(s["q_t"], 2 * t)
                    dve.tensor_tensor(QF[:, :, o:o + HALF], tc[:, :, 0, :], ts[:, :, 1, :],
                                      ALU.subtract).then_inc(s["q_chain"], 1)
                    dve.tensor_tensor(QF[:, :, o + HALF:o + DR], ts[:, :, 0, :], tc[:, :, 1, :],
                                      ALU.add).then_inc(s["q_chain"], 1)

                def g_rotate(n):
                    t, b = divmod(n, NB)
                    dve.wait_ge(s_g[t % 2][b], 64 * (t // 2 + 1))
                    g = G[:, t % 2, GPB * b:GPB * (b + 1), 0:2 * DR]
                    dve.tensor_tensor(g, g, rank_tab[:, :, :, :].rearrange("p a k f -> p (a k f)")[:, None, :]
                                      .to_broadcast([P, GPB, 2 * DR]), ALU.mult).then_inc(s["g_rot"], 1)

                def s_minimum(n):
                    t, b = divmod(n, NB)
                    dve.wait_ge(s["s_mm"], n + 1)
                    if n >= 2:
                        dve.wait_ge(s["p_exp"], n - 1)
                    m = C_MASK0 if t == 0 and b < 4 else C_MASK
                    dve.tensor_tensor_reduce(out=S[:, n % 2, :], in0=psS[n % 2][:, 0:NS], in1=cst[:, m:m + NS],
                                             scale=1.0, scalar=3.0e38, op0=ALU.add, op1=ALU.min,
                                             accum_out=nmin[:, n % 2:n % 2 + 1]).then_inc(s["s_min"], 1)

                def row_inverse(n):
                    dve.wait_ge(s["p_exp"], n + 1)
                    if n >= 2:
                        dve.wait_ge(s["p_nrm"], n - 1)
                    dve.reciprocal(rinv[:, n % 2:n % 2 + 1], psumr[:, n % 4:n % 4 + 1]).then_inc(s["orec"], 1)

                def add_and_stats(t):
                    dve.wait_ge(s["y_mm"], t + 1)
                    dve.tensor_tensor(xa[:, :], PX, xr[:, t, :], ALU.add).then_inc(s["y_add"], 1)
                    dve.wait_ge(s["y_add"], t + 1)
                    dve.bn_stats(out=stats[:, 0, :], in_=xa[:, :]).then_inc(s["bn"], 1)
                    dve.wait_ge(s["bn"], 2 * t + 1)
                    dve.bn_aggr(out=mv[:, 0, :], in_=stats[:, 0, :]).then_inc(s["bn"], 1)

                def normalize(t):
                    dve.wait_ge(s["ln_a"], 2 * t + 2)
                    if t >= 4:
                        dve.wait_ge(s_sct[t % 4], 16 * (t // 4))
                        dve.wait_ge(s["x1d"], t - 3)
                        dve.wait_ge(s["x1_cp"], t - 3)
                    dve.tensor_scalar(x1[:, t % 4, :], xa[:, :], mv[:, 0, 0:1], lnv[:, 1, 0:1], ALU.subtract,
                                      ALU.mult).then_inc(s["x1_n"], 1)

                def route(t):
                    dve.wait_ge(s["lg_mm"], t + 1)
                    if t >= 1:
                        dve.wait_ge(s["lg_e"], t)
                    dve.tensor_copy(rlog[:, :], PX[:, 0:E0]).then_inc(s["lg_cp"], 1)
                    dve.wait_ge(s["lg_cp"], t + 1)
                    dve.max(out=r8[:, :], in_=rlog[:, :]).then_inc(s["rt_a"], 1)
                    dve.wait_ge(s["rt_a"], 4 * t + 1)
                    dve.tensor_scalar(rsm[:, 0:1], r8[:, 0:1], -1.0, None, ALU.mult).then_inc(s["rt"], 1)
                    dve.max_index(out=r8i[:, :], in_max=r8[:, :], in_values=rlog[:, :]).then_inc(s["rt"], 1)
                    dve.wait_ge(s["rt"], 5 * t + 2)
                    dve.tensor_copy(rsm[:, 2:3], r8i[:, 0:1]).then_inc(s["rt"], 1)
                    dve.wait_ge(s["rt"], 5 * t + 3)
                    dve.tensor_scalar(onehot[:, :], cst[:, C_IOTA:C_IOTA + E0], rsm[:, 2:3], None,
                                      ALU.is_equal).then_inc(s["rt"], 1)

                def place(t):
                    dve.wait_ge(s["cum_mm"], t + 1)
                    dve.tensor_tensor(ohsum[:, :], ohsum[:, :], onehot[:, :], ALU.add).then_inc(s["rt"], 1)
                    dve.tensor_tensor_reduce(out=rjunk[:, :], in0=PX[:, E0:2 * E0], in1=onehot[:, :], scale=1.0,
                                             scalar=0.0, op0=ALU.mult, op1=ALU.add,
                                             accum_out=rsm[:, 3:4]).then_inc(s["rte"], 1)
                    dve.wait_ge(s["rte"], t + 1)
                    dve.wait_ge(s["lg_e"], t + 1)
                    dve.tensor_scalar(rsm[:, 4:5], rsm[:, 3:4], float(C0), None, ALU.is_le).then_inc(s["rt_a"], 1)
                    dve.reciprocal(rsm[:, 5:6], rsm[:, 1:2]).then_inc(s["rt_a"], 1)
                    dve.scalar_tensor_tensor(out=rsm[:, 6:7], in0=rsm[:, 2:3], scalar=float(C0), in1=rsm[:, 3:4],
                                             op0=ALU.mult, op1=ALU.add).then_inc(s["rt_a"], 1)
                    dve.wait_ge(s["rt_a"], 4 * t + 4)
                    dve.tensor_tensor(gm[:, t:t + 1], rsm[:, 5:6], rsm[:, 4:5], ALU.mult).then_inc(s["plc"], 1)
                    dve.tensor_scalar(rsm[:, 7:8], rsm[:, 4:5], -2.0 * NSLOT, 2.0 * NSLOT - 1.0, ALU.mult,
                                      ALU.add).then_inc(s["plc"], 1)
                    dve.tensor_scalar(slot_out[:, t:t + 1], rsm[:, 6:7], -1.0, float(NSLOT - 1), ALU.add,
                                      ALU.min).then_inc(s["plc"], 1)
                    dve.wait_ge(s["plc"], 3 * (t + 1))
                    dve.tensor_tensor(slot_in[:, t:t + 1], rsm[:, 6:7], rsm[:, 7:8],
                                      ALU.add).then_inc(s["slots_ready"], 1)

                for n in range(N0, N1):
                    st, b = divmod(n, NB)
                    if 0 <= n + 1 < NT * NB:
                        g_rotate(n + 1)
                    if 0 <= n - 3 < NT * NB:
                        s_minimum(n - 3)
                    if 0 <= n - 5 < NT * NB:
                        row_inverse(n - 5)
                    if 0 <= st + 1 < NT:
                        if b == 1:
                            q_min(st + 1)
                        if b == 2:
                            q_rotate(st + 1, 0)
                        if b == 3:
                            q_rotate(st + 1, 1)
                    if 0 <= st - 2 < NT:
                        if b == 1:
                            add_and_stats(st - 2)
                        if b == 2:
                            normalize(st - 2)
                        if b == 5:
                            route(st - 2)
                        if b == 7:
                            place(st - 2)
                    for kind, t, i in index_steps.get(n, ()):
                        if kind == "sum":
                            combine(t, i)
                            if i == chunks_of(t) - 1:
                                index_mask(t)
                        else:
                            topk_step(t, i)

        flat = G[:, :, :, :].rearrange("p a g n -> p (a g n)")
        strips = {}
        for region, view, parts in (
                ("G", flat, (("x2", NT * D), ("x2T", L), ("vT", L + 2 * ROLL), ("acc", CH), ("tmp", CH), ("mvs", 64))),
                ("R", R[:, :, :, :].rearrange("p a h n -> p (a h n)"), (("yg", NT * D), ("sig", 4 * CH))),
                ("SC", SC[:, :, :].rearrange("p a n -> p (a n)"),
                 (("xb", NXB * EG * D), ("xbT", 2 * EG * C0), ("yb", 2 * EG * D))),
                ("Q", Q[:, :, :, :].rearrange("p a q h -> p (a q h)"), (("x3", 2 * CH), ("x3T", 2 * CH))),
                ("OT", ot_region[:, :], (("sl", 2 * CH), ("hd", 2 * CH))),
                ("OT, before", ot_region[:, :], (("hid", 2 * EG * C0), ("sil", 2 * EG * C0))),
                ("KT", KT[:, :, :, :].rearrange("p a g n -> p (a g n)"), (("n1", CH), ("s2", CH))),
                ("QF", QF[:, :, :].rearrange("p h n -> p (h n)"), (("accf", CH), ("res", CH))),
                ("PT", PT[:, :, :].rearrange("p a n -> p (a n)"), (("tmpP", CH),)),
                ("PR", PR[:, :, :].rearrange("p a n -> p (a n)"), (("accP", CH),))):
            at = 0
            for name, size in parts:
                strips[name] = view[:, at:at + size]
                at += size
            assert at <= view.shape[1], (region, at)
        second_part(nc, dram, out, ctx, sem, strips, dict(
            cst=cst, ident=ident, xr=xr, gm=gm, slot_out=slot_out, w_ex=w_ex, s_we=s_we, load_experts=load_experts,
            w_value=w_value, w_gates=w_gates, w_up=w_up, w_down=w_down, gamma=gamma, beta=beta, w_g8=w_g8,
            xslots=xslots, yslots=yslots, banks=[psK, psX, psI[0], psI[1], psS[0], psP, psS[1], psM]))


def second_part(nc, dram, out, ctx, sem, m, k):
    cst, ident, xr, gm, w_ex, s_we = k["cst"], k["ident"], k["xr"], k["gm"], k["w_ex"], k["s_we"]
    w_value, w_gates, w_up, w_down = k["w_value"], k["w_gates"], k["w_up"], k["w_down"]
    gamma, beta, w_g8 = k["gamma"], k["beta"], k["w_g8"]
    bank = k["banks"]
    GC = EG * C0
    xb = m["xb"].rearrange("p (a e n) -> p a e n", a=NXB, e=EG)
    yb = m["yb"].rearrange("p (a e n) -> p a e n", a=2, e=EG)
    xbT = m["xbT"].rearrange("p (a n) -> p a n", a=2)
    hid = m["hid"].rearrange("p (a n) -> p a n", a=2)
    sil = m["sil"].rearrange("p (a n) -> p a n", a=2)
    yg = m["yg"].rearrange("p (t n) -> p t n", t=NT)
    x2 = m["x2"].rearrange("p (t n) -> p t n", t=NT)
    x2T, vT = m["x2T"], m["vT"]
    sig = m["sig"].rearrange("p (a n) -> p a n", a=4)
    acc, tmp, accP, tmpP = m["acc"], m["tmp"], m["accP"], m["tmpP"]
    x3 = m["x3"].rearrange("p (a t n) -> p a t n", a=2, t=TPC)
    x3T = m["x3T"].rearrange("p (a n) -> p a n", a=2)
    sl = m["sl"].rearrange("p (a n) -> p a n", a=2)
    hd = m["hd"].rearrange("p (a n) -> p a n", a=2)
    n1 = m["n1"].rearrange("p (t n) -> p t n", t=TPC)
    s2 = m["s2"].rearrange("p (t n) -> p t n", t=TPC)
    accf = m["accf"].rearrange("p (t n) -> p t n", t=TPC)
    res = m["res"].rearrange("p (t n) -> p t n", t=TPC)

    def sb(name, shape, dt=F32):
        return ctx.enter_context(nc.sbuf_tensor(name, shape, dt))

    stt = sb("stt", [P, TPC, 6])
    mv = sb("mv2", [P, TPC, 2])
    rstd = sb("rstd", [P, TPC])
    half = sb("half", [P, TPC])
    lg = sb("lg", [P, TPC, E1])
    lmax = sb("lmax", [P, TPC])
    lsum = sb("lsum", [P, TPC])
    t8 = sb("t8", [P, TPC, 8])
    t8i = sb("t8i", [P, TPC, 8], U32)
    t8f = sb("t8f", [P, TPC, 8])
    oh = sb("oh", [P, 2, TPC, E1])
    wt = sb("wt", [P, 2, TPC, E1])
    den = sb("den", [P, 2, TPC])
    out_rows = out.rearrange("(c t p) d -> c p t d", t=TPC, p=P)

    names = """xbt xbt_cp gate up silu hid y_mm y_cp z ln pool_r x2_n x2_t x2_cp v_mm v_cp wrap
        x2b gt_mm sig prod prodP acc_done o_t lnc lnp x3_t x3_cp lg_mm rt lexp wts h_mm g_mm sl hd root d_mm dacc fin
        halfset""".split()
    s = {n: sem("t_" + n) for n in names}
    s_xb = [sem(f"t_xb{i}") for i in range(NXB)]
    s_yst = [sem(f"t_yst{i}") for i in range(2)]
    s_yg = [sem(f"t_yg{c}") for c in range(NCH)]
    s_out = [sem(f"t_out{i}") for i in range(2)]

    POOL_GATES = (1, 4, 7)
    NPG = len(POOL_GATES)
    DVE_GATES = tuple(i for i in range(NGATE) if i not in POOL_GATES)
    NDG = len(DVE_GATES)
    ORDER = (E1, E1 + 1) + tuple(range(E1))

    def gate_bank(n):
        return bank[n % 2 + (2 if n // NGATE == 1 else 0)]

    with nc.Block() as block:
        @block.sync
        def _(sp):
            def load_slots(g):
                if g >= NXB:
                    sp.wait_ge(s["xbt"], g - NXB + 1)
                sp.dma_start(xb[0:C0, g % NXB, :, :],
                             k["xslots"][GC * g:GC * (g + 1), :].rearrange("(e c) d -> c e d", c=C0)
                             ).then_inc(s_xb[g % NXB], 16)

            for g in range(NXB):
                load_slots(g)
            for g in range(NXB, NEG):
                load_slots(g)
                if g < NEG - 1:
                    sp.wait_ge(s["y_mm"], g - NXB + 1)
                    k["load_experts"](sp, g + 1)
            for c in range(NCH):
                sp.wait_ge(s["fin"], c + 1)
                sp.dma_start(out_rows[c], res).then_inc(s_out[c % 2], 16)
                sp.wait_ge(s_out[c % 2], 16 * (c // 2 + 1))

        @block.gpsimd
        def _(pool):
            pool.memset(half[:, :], -0.5).then_inc(s["halfset"], 1)
            pool.wait_ge(s["halfset"], 1)
            for i in range(2):
                pool.wait_ge(s_yst[i], 16 * NEG // 2)
            for t in range(NT):
                pool.indirect_dma_start(yg[:, t, :], None, k["yslots"],
                                        bass.IndirectOffsetOnAxis(ap=k["slot_out"][:, t:t + 1], axis=0)
                                        ).then_inc(s_yg[t // TPC], 16)
            done = [0]

            def root(n_stats):
                pool.wait_ge(s["ln"], n_stats)
                pool.tensor_scalar(rstd[:, :], mv[:, :, 1], LN_EPS, None, ALU.add).then_inc(s["pool_r"], 1)
                done[0] += 1
                pool.wait_ge(s["pool_r"], done[0])
                pool.tensor_tensor(rstd[:, :], rstd[:, :], half[:, :], ALU.pow).then_inc(s["pool_r"], 1)
                done[0] += 1

            pool.wait_ge(s["x2_t"], NCH)
            for c in range(NCH):
                pool.tensor_tensor(x2[:, TPC * c:TPC * (c + 1), :], x2[:, TPC * c:TPC * (c + 1), :],
                                   beta[:, None, :].to_broadcast([P, TPC, D]), ALU.add).then_inc(s["x2b"], 1)
            pool.wait_ge(s["wrap"], 2)
            seen = 8 * NCH

            def product(c, i):
                g = POOL_GATES[i]
                n = NGATE * c + g
                base = (2 * NPG - 1) * c
                v = vT[:, ROLL + SHIFTS[g] + CH * c:ROLL + SHIFTS[g] + CH * (c + 1)]
                pool.wait_ge(s["sig"], n + 1)
                if i == 0:
                    if c >= 1:
                        pool.wait_ge(s["acc_done"], c)
                    pool.tensor_tensor(accP, v, sig[:, n % 4, :], ALU.mult).then_inc(s["prodP"], 1)
                else:
                    pool.wait_ge(s["prodP"], base + 2 * i - 1)
                    pool.tensor_tensor(tmpP, v, sig[:, n % 4, :], ALU.mult).then_inc(s["prodP"], 1)
                    pool.wait_ge(s["prodP"], base + 2 * i)
                    pool.tensor_tensor(accP, accP, tmpP, ALU.add).then_inc(s["prodP"], 1)

            for j in range(-1, NCH + 1):
                if j != 0 and j + 1 < NCH:
                    for i in range(NPG):
                        product(j + 1, i)
                if j >= 1:
                    seen += 8
                    root(seen)
                if j + 1 < NCH:
                    c = j + 1
                    seen += 8
                    root(seen)
                    if j < 0:
                        product(1, 0)
                    pool.wait_ge(s["lnc"], 8 * c + 4)
                    pool.tensor_tensor(n1, n1, gamma[:, None, :].to_broadcast([P, TPC, D]),
                                       ALU.mult).then_inc(s["lnp"], 1)
                    pool.wait_ge(s["lnp"], 2 * c + 1)
                    pool.wait_ge(s["x2b"], c + 1)
                    pool.tensor_tensor(s2, n1, x2[:, TPC * c:TPC * (c + 1), :], ALU.add).then_inc(s["lnp"], 1)
                    if j < 0:
                        product(1, 1)
                    seen += 8
                    root(seen)
                    if j < 0:
                        product(1, 2)

        @block.tensor
        def _(pe):
            expert_gate, expert_linear = (bank[2], bank[6]), (bank[3], bank[7])

            def expert_transpose(g):
                pe.wait_ge(s_xb[g % NXB], 16 * (g // NXB + 1))
                if g >= 2:
                    pe.wait_ge(s["xbt_cp"], g - 1)
                for e in range(EG):
                    mm = pe.transpose(bank[g % 2][:, C0 * e:C0 * (e + 1)], xb[0:C0, g % NXB, e, :],
                                      ident[0:C0, 0:C0])
                mm.then_inc(s["xbt"], 1)

            def expert_up(g):
                pe.wait_ge(s["xbt_cp"], g + 1)
                pe.wait_ge(s_we[g % NEW], 48 * (g // NEW + 1))
                if g >= 2:
                    pe.wait_ge(s["silu"], g - 1)
                for e in range(EG):
                    mm = pe.matmul(expert_gate[g % 2][:, C0 * e:C0 * (e + 1)], w_ex[g % NEW][:, 0, e, :],
                                   xbT[:, g % 2, C0 * e:C0 * (e + 1)], start=True, stop=True, skip_group_check=True)
                mm.then_inc(s["gate"], 1)
                if g >= 2:
                    pe.wait_ge(s["hid"], g - 1)
                for e in range(EG):
                    mm = pe.matmul(expert_linear[g % 2][:, C0 * e:C0 * (e + 1)], w_ex[g % NEW][:, 1, e, :],
                                   xbT[:, g % 2, C0 * e:C0 * (e + 1)], start=True, stop=True, skip_group_check=True)
                mm.then_inc(s["up"], 1)

            def expert_down(g):
                pe.wait_ge(s["hid"], g + 1)
                if g >= 2:
                    pe.wait_ge(s["y_cp"], g - 1)
                for e in range(EG):
                    mm = pe.matmul(bank[4 + g % 2][0:C0, D * e:D * (e + 1)], hid[:, g % 2, C0 * e:C0 * (e + 1)],
                                   w_ex[g % NEW][:, 2, e, :], start=True, stop=True, skip_group_check=True)
                mm.then_inc(s["y_mm"], 1)

            expert_transpose(0)
            for g in range(NEG):
                if g + 1 < NEG:
                    expert_transpose(g + 1)
                expert_up(g)
                if g >= 1:
                    expert_down(g - 1)
            expert_down(NEG - 1)
            for c in range(NCH):
                pe.wait_ge(s["x2_n"], TPC * (c + 1))
                if c >= 2:
                    pe.wait_ge(s["x2_cp"], c - 1)
                for t in range(TPC):
                    mm = pe.transpose(bank[c % 2][:, P * t:P * (t + 1)], x2[:, TPC * c + t, :], ident)
                mm.then_inc(s["x2_t"], 1)
            for c in range(NCH):
                pe.wait_ge(s["x2_cp"], c + 1)
                pe.matmul(bank[2 + c][:, :], w_value, x2T[:, CH * c:CH * (c + 1)], start=True,
                          stop=True).then_inc(s["v_mm"], 1)

            def gates(c):
                for g in range(NGATE):
                    n = NGATE * c + g
                    if n == 0:
                        pe.wait_ge(s["x2_cp"], NCH)
                    if n >= 2:
                        pe.wait_ge(s["sig"], n - 1)
                    if g == 0 and c == 1:
                        pe.wait_ge(s["v_cp"], NCH)
                    if g == 0 and c >= 2:
                        pe.wait_ge(s["x3_cp"], c)
                        pe.wait_ge(s["rt"], 14 * c - 12)
                    pe.matmul(gate_bank(n)[:, :], w_gates[:, D * g:D * (g + 1)], x2T[:, CH * c:CH * (c + 1)],
                              start=True, stop=True).then_inc(s["gt_mm"], 1)

            def mixed_transpose(c):
                pe.wait_ge(s["acc_done"], c + 1)
                pe.wait_ge(s["sig"], NGATE * (c + 1))
                for t in range(TPC):
                    mm = pe.transpose(bank[0][:, P * t:P * (t + 1)], acc[:, P * t:P * (t + 1)], ident)
                mm.then_inc(s["o_t"], 1)

            def x3_transpose(c):
                pe.wait_ge(s["lnc"], 8 * (c + 1))
                for t in range(TPC):
                    mm = pe.transpose(bank[0][:, P * t:P * (t + 1)], x3[:, c % 2, t, :], ident)
                mm.then_inc(s["x3_t"], 1)

            def route_logits(c):
                pe.wait_ge(s["x3_cp"], c + 1)
                for t in range(TPC):
                    mm = pe.matmul(bank[1][:, E1 * t:E1 * (t + 1)], x3T[:, c % 2, P * t:P * (t + 1)], w_g8,
                                   start=True, stop=True, skip_group_check=True)
                mm.then_inc(s["lg_mm"], 1)

            def ffn_up(c, i):
                n = NHC * c + i
                if n == 0:
                    pe.wait_ge(s["sig"], 2 * NGATE)
                if n >= 2:
                    pe.wait_ge(s["sl"], n - 1)
                    pe.wait_ge(s["hd"], n - 1)
                e = ORDER[i]
                pe.matmul(bank[2 + 2 * (n % 2)][0:H1, :], w_up[:, 0, e, :], x3T[:, c % 2, :], start=True,
                          stop=True).then_inc(s["h_mm"], 1)
                pe.matmul(bank[3 + 2 * (n % 2)][0:H1, :], w_up[:, 1, e, :], x3T[:, c % 2, :], start=True,
                          stop=True).then_inc(s["g_mm"], 1)

            def ffn_down(c, i):
                n = NHC * c + i
                m_ = 9 * c + i - 1
                if m_ >= 2:
                    pe.wait_ge(s["dacc"], m_ - 1)
                pe.wait_ge(s["hd"], n + 1)
                parts = (0, 1) if i == 1 else (i,)
                for t in range(TPC):
                    for p in parts:
                        mm = pe.matmul(bank[6 + m_ % 2][:, D * t:D * (t + 1)],
                                       hd[0:H1, (NHC * c + p) % 2, P * t:P * (t + 1)], w_down[:, ORDER[p], :],
                                       start=(p == parts[0]), stop=(p == parts[-1]), skip_group_check=True)
                mm.then_inc(s["d_mm"], 1)

            for j in range(-1, NCH):
                if j != 0 and j + 1 < NCH:
                    gates(j + 1)
                for i in range(NHC + 1):
                    if j >= 0 and i < NHC:
                        ffn_up(j, i)
                    if j >= 0 and i >= 2:
                        ffn_down(j, i - 1)
                    if j + 1 < NCH:
                        if i == 2:
                            mixed_transpose(j + 1)
                            if j < 0:
                                gates(1)
                        if i == 7:
                            x3_transpose(j + 1)
                        if i == 8:
                            route_logits(j + 1)

        @block.scalar
        def _(act):
            def expert_silu(g):
                act.wait_ge(s["gate"], g + 1)
                if g >= 2:
                    act.wait_ge(s["hid"], g - 1)
                act.activation(sil[:, g % 2, :], (bank[2], bank[6])[g % 2][:, 0:GC], ACT.Silu).then_inc(s["silu"], 1)

            def expert_store(g):
                act.wait_ge(s["y_mm"], g + 1)
                if g >= 2:
                    act.wait_ge(s_yst[g % 2], 16 * (g // 2))
                act.activation(yb[0:C0, g % 2, :, :].rearrange("p e n -> p (e n)"), bank[4 + g % 2][0:C0, :],
                               ACT.Copy).then_inc(s["y_cp"], 1)
                act.wait_ge(s["y_cp"], g + 1)
                act.dma_start(k["yslots"][GC * g:GC * (g + 1), :].rearrange("(e c) d -> c e d", c=C0),
                              yb[0:C0, g % 2, :, :]).then_inc(s_yst[g % 2], 16)

            for g in range(NEG):
                expert_silu(g)
                if g >= 1:
                    expert_store(g - 1)
            expert_store(NEG - 1)
            act.preload_act_table_set("natural_log_exp_and_others")
            for c in range(NCH):
                act.wait_ge(s["ln"], 8 * (c + 1))
                if c >= 1:
                    act.wait_ge(s["x2_n"], TPC * c)
                act.activation(rstd[:, :], mv[:, :, 1], ACT.Ln, bias=cst[:, C_EPS:C_EPS + 1]).then_inc(s["root"], 1)
                act.wait_ge(s["root"], 2 * c + 1)
                act.activation(rstd[:, :], rstd[:, :], ACT.Exp, scale=-0.5).then_inc(s["root"], 1)
                act.wait_ge(s["x2_t"], c + 1)
                act.activation(x2T[:, CH * c:CH * (c + 1)], bank[c % 2][:, :], ACT.Copy).then_inc(s["x2_cp"], 1)
            act.preload_act_table_set("sigmoid_and_others")
            for c in range(NCH):
                act.wait_ge(s["v_mm"], c + 1)
                act.activation(vT[:, ROLL + CH * c:ROLL + CH * (c + 1)], bank[2 + c][:, :],
                               ACT.Copy).then_inc(s["v_cp"], 1)
            act.wait_ge(s["v_cp"], NCH)
            act.activation(vT[:, 0:ROLL], vT[:, L:L + ROLL], ACT.Copy).then_inc(s["wrap"], 1)
            act.activation(vT[:, ROLL + L:], vT[:, ROLL:2 * ROLL], ACT.Copy).then_inc(s["wrap"], 1)
            for j in range(-1, NCH):
                for c in ((0, 1) if j < 0 else (j + 1,) if 0 < j < NCH - 1 else ()):
                    for g in range(NGATE):
                        n = NGATE * c + g
                        act.wait_ge(s["gt_mm"], n + 1)
                        if n >= 4:
                            wait_product(act, s, n - 4, DVE_GATES, POOL_GATES)
                        act.activation(sig[:, n % 4, :], gate_bank(n)[:, :], ACT.Sigmoid).then_inc(s["sig"], 1)
                for i in range(NHC):
                    if j + 1 < NCH and i == 8:
                        act.wait_ge(s["x3_t"], j + 2)
                        act.activation(x3T[:, (j + 1) % 2, :], bank[0][:, :], ACT.Copy).then_inc(s["x3_cp"], 1)
                    if j >= 0:
                        n = NHC * j + i
                        act.wait_ge(s["h_mm"], n + 1)
                        if n >= 2:
                            act.wait_ge(s["hd"], n - 1)
                        act.activation(sl[0:H1, n % 2, :], bank[2 + 2 * (n % 2)][0:H1, :],
                                       ACT.Silu).then_inc(s["sl"], 1)
                if j + 1 < NCH:
                    act.wait_ge(s["rt"], 14 * (j + 1) + 2)
                    act.activation(lg[:, :, :], lg[:, :, :], ACT.Exp).then_inc(s["lexp"], 1)

        @block.vector
        def _(dve):
            def expert_copy(g):
                dve.wait_ge(s["xbt"], g + 1)
                if g >= 2:
                    dve.wait_ge(s["up"], g - 1)
                dve.tensor_copy(xbT[:, g % 2, :], bank[g % 2][:, 0:GC]).then_inc(s["xbt_cp"], 1)

            expert_copy(0)
            for g in range(NEG):
                if g + 1 < NEG:
                    expert_copy(g + 1)
                dve.wait_ge(s["silu"], g + 1)
                dve.wait_ge(s["up"], g + 1)
                if g >= 2:
                    dve.wait_ge(s["y_mm"], g - 1)
                dve.tensor_tensor(hid[:, g % 2, :], sil[:, g % 2, :], (bank[3], bank[7])[g % 2][:, 0:GC],
                                  ALU.mult).then_inc(s["hid"], 1)
            for c in range(NCH):
                dve.wait_ge(s_yg[c], 16 * TPC)
                for i in range(TPC):
                    t = TPC * c + i
                    dve.scalar_tensor_tensor(out=yg[:, t, :], in0=yg[:, t, :], scalar=gm[:, t:t + 1],
                                             in1=xr[:, t, :], op0=ALU.mult, op1=ALU.add).then_inc(s["z"], 1)
                for i in range(TPC):
                    t = TPC * c + i
                    dve.wait_ge(s["z"], t + 1)
                    if c >= 1 and i == 0:
                        dve.wait_ge(s["x2_n"], TPC * c)
                    dve.bn_stats(out=stt[:, i, :], in_=yg[:, t, :]).then_inc(s["ln"], 1)
                for i in range(TPC):
                    dve.wait_ge(s["ln"], 8 * c + i + 1)
                    dve.bn_aggr(out=mv[:, i, :], in_=stt[:, i, :]).then_inc(s["ln"], 1)
                dve.wait_ge(s["root"], 2 * (c + 1))
                for i in range(TPC):
                    t = TPC * c + i
                    dve.tensor_scalar(x2[:, t, :], yg[:, t, :], mv[:, i, 0:1], rstd[:, i:i + 1], ALU.subtract,
                                      ALU.mult).then_inc(s["x2_n"], 1)
            lnn = [8 * NCH]
            pooln = [0]

            def statistics(src, after):
                after()
                for i in range(TPC):
                    dve.bn_stats(out=stt[:, i, :], in_=src(i)).then_inc(s["ln"], 1)
                    lnn[0] += 1
                for i in range(TPC):
                    dve.wait_ge(s["ln"], lnn[0] - TPC + i + 1)
                    dve.bn_aggr(out=mv[:, i, :], in_=stt[:, i, :]).then_inc(s["ln"], 1)
                lnn[0] += TPC

            def wait_root():
                pooln[0] += 2
                dve.wait_ge(s["pool_r"], pooln[0])

            def product(c, g):
                i = DVE_GATES.index(g)
                n = NGATE * c + g
                base = (2 * NDG - 1) * c
                v = vT[:, ROLL + SHIFTS[g] + CH * c:ROLL + SHIFTS[g] + CH * (c + 1)]
                dve.wait_ge(s["sig"], n + 1)
                if i == 0:
                    if c == 0:
                        dve.wait_ge(s["wrap"], 2)
                    else:
                        dve.wait_ge(s["o_t"], c)
                    dve.tensor_tensor(acc, v, sig[:, n % 4, :], ALU.mult).then_inc(s["prod"], 1)
                else:
                    dve.tensor_tensor(tmp, v, sig[:, n % 4, :], ALU.mult).then_inc(s["prod"], 1)
                    dve.wait_ge(s["prod"], base + 2 * i)
                    dve.tensor_tensor(acc, acc, tmp, ALU.add).then_inc(s["prod"], 1)
                    dve.wait_ge(s["prod"], base + 2 * i + 1)

            def mix_sum(c):
                dve.wait_ge(s["prodP"], (2 * NPG - 1) * (c + 1))
                dve.tensor_tensor(acc, acc, accP, ALU.add).then_inc(s["acc_done"], 1)

            def norm1(c):
                statistics(lambda i: bank[0][:, P * i:P * (i + 1)], lambda: dve.wait_ge(s["o_t"], c + 1))

            def norm2(c):
                wait_root()
                for i in range(TPC):
                    dve.tensor_scalar(n1[:, i, :], bank[0][:, P * i:P * (i + 1)], mv[:, i, 0:1], rstd[:, i:i + 1],
                                      ALU.subtract, ALU.mult).then_inc(s["lnc"], 1)

            def norm2_statistics(c):
                statistics(lambda i: s2[:, i, :], lambda: dve.wait_ge(s["lnp"], 2 * (c + 1)))

            def norm3(c):
                wait_root()
                for i in range(TPC):
                    dve.tensor_scalar(x3[:, c % 2, i, :], s2[:, i, :], mv[:, i, 0:1], rstd[:, i:i + 1],
                                      ALU.subtract, ALU.mult).then_inc(s["lnc"], 1)

            def route_max(c):
                b = 14 * c
                dve.wait_ge(s["lg_mm"], c + 1)
                l4 = bank[1][:, 0:TPC * E1].rearrange("p (t e) -> p t e", t=TPC)
                dve.tensor_reduce(lmax[:, :], l4, mybir.AxisListType.X, ALU.max).then_inc(s["rt"], 1)
                dve.wait_ge(s["rt"], b + 1)
                dve.tensor_tensor(lg[:, :, :], l4, lmax[:, :, None].to_broadcast([P, TPC, E1]),
                                  ALU.subtract).then_inc(s["rt"], 1)

            def route_top(c):
                b = 14 * c
                dve.wait_ge(s["lexp"], c + 1)
                dve.tensor_reduce(lsum[:, :], lg[:, :, :], mybir.AxisListType.X, ALU.add).then_inc(s["rt"], 1)
                dve.wait_ge(s["rt"], b + 3)
                dve.reciprocal(lsum[:, :], lsum[:, :]).then_inc(s["rt"], 1)
                dve.wait_ge(s["rt"], b + 4)
                dve.tensor_tensor(lg[:, :, :], lg[:, :, :], lsum[:, :, None].to_broadcast([P, TPC, E1]),
                                  ALU.mult).then_inc(s["rt"], 1)
                dve.wait_ge(s["rt"], b + 5)
                for i in range(TPC):
                    ins = dve.max(out=t8[:, i, :], in_=lg[:, i, :])
                ins.then_inc(s["rt"], 1)
                dve.wait_ge(s["rt"], b + 6)
                for i in range(TPC):
                    ins = dve.max_index(out=t8i[:, i, :], in_max=t8[:, i, :], in_values=lg[:, i, :])
                ins.then_inc(s["rt"], 1)
                dve.wait_ge(s["rt"], b + 7)
                dve.tensor_copy(t8f[:, :, :], t8i[:, :, :]).then_inc(s["rt"], 1)

            def route_weights(c):
                b = 14 * c
                dve.tensor_tensor(den[:, 0, :], t8[:, :, 0], t8[:, :, 1], ALU.add).then_inc(s["rt"], 1)
                dve.wait_ge(s["rt"], b + 9)
                dve.tensor_scalar(den[:, 0, :], den[:, 0, :], SUM_EPS, None, ALU.add).then_inc(s["rt"], 1)
                iota = cst[:, None, C_IOTA:C_IOTA + E1].to_broadcast([P, TPC, E1])
                for i in range(2):
                    dve.tensor_tensor(oh[:, i, :, :], iota, t8f[:, :, i:i + 1].to_broadcast([P, TPC, E1]),
                                      ALU.is_equal).then_inc(s["rt"], 1)
                dve.wait_ge(s["rt"], b + 12)
                dve.reciprocal(den[:, 1, :], den[:, 0, :]).then_inc(s["rt"], 1)
                for i in range(2):
                    ins = dve.tensor_tensor(oh[:, i, :, :], oh[:, i, :, :],
                                            t8[:, :, i:i + 1].to_broadcast([P, TPC, E1]), ALU.mult)
                ins.then_inc(s["rt"], 1)
                dve.wait_ge(s["rt"], b + 14)
                dve.tensor_tensor(oh[:, 0, :, :], oh[:, 0, :, :], oh[:, 1, :, :], ALU.add).then_inc(s["wts"], 1)
                dve.wait_ge(s["wts"], 2 * c + 1)
                dve.tensor_tensor(wt[:, c % 2, :, :], oh[:, 0, :, :], den[:, 1, :, None].to_broadcast([P, TPC, E1]),
                                  ALU.mult).then_inc(s["wts"], 1)

            def hidden(c, i):
                n = NHC * c + i
                dve.wait_ge(s["sl"], n + 1)
                dve.wait_ge(s["g_mm"], n + 1)
                if n >= 2:
                    if i == 2:
                        dve.wait_ge(s["d_mm"], 9 * c + 1)
                    elif i < 2:
                        dve.wait_ge(s["d_mm"], 9 * (c - 1) + 8 + i)
                    else:
                        dve.wait_ge(s["d_mm"], 9 * c + i - 2)
                dve.tensor_tensor(hd[0:H1, n % 2, :], sl[0:H1, n % 2, :], bank[3 + 2 * (n % 2)][0:H1, :],
                                  ALU.mult).then_inc(s["hd"], 1)

            def accumulate(c, i):
                m_ = 9 * c + i - 1
                dve.wait_ge(s["d_mm"], m_ + 1)
                src = bank[6 + m_ % 2][:, :].rearrange("p (t n) -> p t n", t=TPC)
                if m_ >= 1:
                    dve.wait_ge(s["dacc"], m_)
                if i == 1:
                    if c >= 1:
                        dve.wait_ge(s["fin"], c)
                    dve.tensor_tensor(accf, src, x3[:, c % 2, :, :], ALU.add).then_inc(s["dacc"], 1)
                else:
                    e = ORDER[i]
                    if i == 2:
                        dve.wait_ge(s["wts"], 2 * c + 2)
                    for t in range(TPC):
                        ins = dve.scalar_tensor_tensor(out=accf[:, t, :], in0=src[:, t, :],
                                                       scalar=wt[:, c % 2, t, e:e + 1], in1=accf[:, t, :],
                                                       op0=ALU.mult, op1=ALU.add)
                    ins.then_inc(s["dacc"], 1)

            def finish_statistics(c):
                statistics(lambda i: accf[:, i, :], lambda: dve.wait_ge(s["dacc"], 9 * (c + 1)))

            def finish(c):
                wait_root()
                if c >= 1:
                    dve.wait_ge(s_out[(c - 1) % 2], 16 * ((c - 1) // 2 + 1))
                for i in range(TPC):
                    ins = dve.tensor_scalar(res[:, i, :], accf[:, i, :], mv[:, i, 0:1], rstd[:, i:i + 1],
                                            ALU.subtract, ALU.mult)
                ins.then_inc(s["fin"], 1)

            for j in range(-1, NCH):
                nx = j + 1 < NCH
                if nx and j != 0:
                    for g in DVE_GATES:
                        product(j + 1, g)
                for i in range(NHC + 1):
                    if j >= 0 and i < NHC:
                        hidden(j, i)
                    if i == 1 and nx and j != 0:
                        mix_sum(j + 1)
                    if i == 1 and j >= 1:
                        finish_statistics(j - 1)
                    if i == 1 and j >= 0:
                        route_top(j)
                    if i == 2 and j >= 1:
                        finish(j - 1)
                    if j >= 0 and i == NHC and nx:
                        route_max(j + 1)
                    if j >= 0 and i >= 2:
                        accumulate(j, i - 1)
                    if i == 2 and j >= 0:
                        route_weights(j)
                    if nx:
                        if i == 2:
                            norm1(j + 1)
                        if j < 0 and i in (2, 3, 5):
                            pair = {2: 0, 3: 1, 5: 2}[i]
                            if i > 2:
                                (norm2 if i == 3 else norm2_statistics)(0)
                            for g in DVE_GATES[2 * pair:2 * pair + 2]:
                                product(1, g)
                            continue
                        if i == 3:
                            norm2(j + 1)
                        if i == 5:
                            norm2_statistics(j + 1)
                        if i == 6:
                            norm3(j + 1)
                        if i == NHC and j < 0:
                            mix_sum(1)
                            route_max(j + 1)
            finish_statistics(NCH - 1)
            finish(NCH - 1)


def wait_product(act, s, n, dve_gates, pool_gates):
    c, g = divmod(n, NGATE)
    if g in pool_gates:
        i = pool_gates.index(g)
        act.wait_ge(s["prodP"], (2 * len(pool_gates) - 1) * c + max(2 * i, 1))
    else:
        i = dve_gates.index(g)
        act.wait_ge(s["prod"], (2 * len(dve_gates) - 1) * c + max(2 * i, 1))


def kernel(**inputs):
    import concourse.bacc as _bacc
    from concourse.bass_utils import run_bass_kernel_spmd as _run

    def a(name):
        return np.asarray(inputs[name])

    consts, tables = shape_constants()
    raw = a("L0_attn_raw_delta")
    x = a("L0_attn_x").reshape(L, D)

    def heads(w, rows):
        return np.ascontiguousarray(w.reshape(rows, NH, DH).transpose(2, 1, 0))

    arrays = {
        "cst": consts,
        "tab": tables,
        "raw": np.concatenate([np.tile(raw, (P, 1)), np.tile(raw, P // HALF)[:, None]], 1),
        "xT": np.ascontiguousarray(x.T),
        "x": np.ascontiguousarray(x.reshape(NT, P, D).transpose(1, 0, 2)),
        "idx_wk": a("L0_attn_idx_wk"),
        "idx_wq": a("L0_attn_idx_wq"),
        "idx_w": np.tile(a("L0_attn_idx_w"), (P, 1)),
        "W_kr": a("L0_attn_W_kr"),
        "W_dkv": a("L0_attn_W_dkv"),
        "W_dq": a("L0_attn_W_dq"),
        "W_qr": a("L0_attn_W_qr"),
        "W_uqT": heads(a("L0_attn_W_uq"), CQ),
        "W_ukT": heads(a("L0_attn_W_uk"), CKV),
        "W_uvT": heads(a("L0_attn_W_uv"), CKV),
        "W_out": np.ascontiguousarray(a("L0_attn_W_out").reshape(NH, DH, D).transpose(1, 0, 2)),
        "w_router": a("L0_ffn_w_router"),
        "w_gate": a("L0_ffn_w_gate"),
        "w_up": a("L0_ffn_w_up"),
        "w_down": a("L0_ffn_w_down"),
        "gate_W": np.ascontiguousarray(a("L1_attn_gate_W").T),
        "value_W": np.ascontiguousarray(a("L1_attn_value_W").T),
        "gamma": np.tile(a("L1_attn_gamma"), (P, 1)),
        "beta": np.tile(a("L1_attn_beta"), (P, 1)),
        "Wg": np.ascontiguousarray(a("L1_ffn_Wg").T),
        "W1": np.ascontiguousarray(a("L1_ffn_W1").transpose(1, 0, 2)),
        "W3": np.ascontiguousarray(a("L1_ffn_W3").transpose(1, 0, 2)),
        "W2": np.ascontiguousarray(a("L1_ffn_W2").transpose(1, 0, 2)),
        "Ws1": np.ascontiguousarray(a("L1_ffn_Ws1").reshape(D, 2, H1)),
        "Ws3": np.ascontiguousarray(a("L1_ffn_Ws3").reshape(D, 2, H1)),
        "Ws2": np.ascontiguousarray(a("L1_ffn_Ws2").reshape(2, H1, D).transpose(1, 0, 2)),
    }
    nc = _bacc.Bacc("TRN2", target_bir_lowering=False, num_devices=1)
    sent = {f"in_{n}": np.ascontiguousarray(v) for n, v in arrays.items()}
    dram = {n: nc.dram_tensor(f"in_{n}", v.shape, F32, kind="ExternalInput").ap() for n, v in arrays.items()}
    out = nc.dram_tensor("out_0", (L, D), F32, kind="ExternalOutput").ap()
    program(nc, dram, out)
    r = _run(nc, [sent], core_ids=[0])
    return r.results[0]["out_0"].reshape(1, L, D)
```
